# Optimizing a Trainium2 kernel written in Bass

```python
import numpy as np
import jax
import jax.numpy as jnp

def _softmax(x, axis=-1):
    return jax.nn.softmax(x, axis=axis)

def _gelu(x):
    return jax.nn.gelu(x, approximate=True)

def _silu(x):
    return jax.nn.silu(x)

def _sigmoid(x):
    return jax.nn.sigmoid(x)

def _layernorm(x, axis=-1, eps=1e-05):
    m = jnp.mean(x, axis=axis, keepdims=True)
    v = jnp.var(x, axis=axis, keepdims=True)
    return (x - m) / jnp.sqrt(v + eps)

def _scatter_add(tgt, idx, src, axis=0):
    return tgt.at[idx].add(src)

def _segment_sum(src, seg, n):
    return jax.ops.segment_sum(src, seg, n)
kernel_name = 'mk_gnn_ffn_d2_gnn_r32_c33bc7'

def setup_inputs(seed: int=0):
    np.random.seed(seed)
    _w = jnp.asarray

    def _rec_inputs():
        import jax
        import jax.numpy as jnp
        _gk = jax.random.key(seed)
        x = -0.0002117 + 1 * jax.random.normal(jax.random.fold_in(_gk, 1), (3125, 256), jnp.float32)
        src = jax.random.randint(jax.random.fold_in(_gk, 2), (50000,), 0, 3125, jnp.int32)
        dst = jax.random.randint(jax.random.fold_in(_gk, 3), (50000,), 0, 3125, jnp.int32)
        _o = jnp.argsort(dst, stable=True)
        src = src[_o]
        dst = dst[_o]
        edge_attr_2 = jax.random.uniform(jax.random.fold_in(_gk, 11), (50000, 2), jnp.float32, 0.0, 1)
        edge_type_16 = jax.random.randint(jax.random.fold_in(_gk, 13), (50000,), 0, 16, jnp.int32)
        edge_weight = jax.random.uniform(jax.random.fold_in(_gk, 14), (50000,), jnp.float32, 0.0, 0.999999)
        return (x, src, dst, edge_attr_2, edge_type_16, edge_weight)
    x, src, dst, edge_attr_2, edge_type_16, edge_weight = _rec_inputs()

    def _L0_gnn_setup():
        import jax, jax.numpy as jnp
        import numpy as np
        N_NODES = 3125
        N_EDGES = 50000
        IN_FEATS = 256
        OUT_FEATS = 64
        NUM_HEADS = 4
        key = jax.random.key(seed)
        k_h, k_adj, k_dir, k_wf, k_wr, k_af = jax.random.split(key, 6)
        h = jax.random.normal(k_h, (N_NODES, IN_FEATS), dtype=jnp.float32)
        adj = jax.random.randint(k_adj, (2, N_EDGES), 0, N_NODES, dtype=jnp.int64)
        bit = jax.random.randint(k_dir, (N_EDGES,), 0, 2).astype(jnp.float32)
        direction = jnp.stack([bit, 1.0 - bit], axis=1)
        s_w = float(np.sqrt(6.0 / (IN_FEATS + OUT_FEATS)))
        s_a = float(np.sqrt(6.0 / (NUM_HEADS + OUT_FEATS)))
        W_forward = jax.random.uniform(k_wf, (OUT_FEATS, IN_FEATS), jnp.float32, -s_w, s_w)
        W_reverse = jax.random.uniform(k_wr, (OUT_FEATS, IN_FEATS), jnp.float32, -s_w, s_w)
        attn_forward = jax.random.uniform(k_af, (1, NUM_HEADS, OUT_FEATS), jnp.float32, -s_a, s_a)
        return {'h': h, 'adj': adj, 'direction': direction, 'W_forward': W_forward, 'W_reverse': W_reverse, 'attn_forward': attn_forward}
    _L0_gnn_all = _L0_gnn_setup()
    _L0_gnn_in = {k: v for k, v in _L0_gnn_all.items() if k in ('W_forward', 'W_reverse', 'attn_forward')}
    del _L0_gnn_all

    def _L0_ffn_setup():
        import jax, jax.numpy as jnp
        import numpy as np
        E, D, H, TOP_K = (6, 256, 256, 2)
        ROUTER_H = D // 2
        key = jax.random.key(seed)
        ks = jax.random.split(key, 12)
        s = 1.0 / np.sqrt(D)
        sh = 1.0 / np.sqrt(H)
        sr = 1.0 / np.sqrt(ROUTER_H)
        return {'features': jax.random.normal(ks[0], (8, 128, D), dtype=jnp.float32), 'router_w1': jax.random.uniform(ks[1], (D, ROUTER_H), jnp.float32, -s, s), 'router_b1': jnp.zeros((ROUTER_H,), jnp.float32), 'router_w2': jax.random.uniform(ks[2], (ROUTER_H, E), jnp.float32, -sr, sr), 'router_b2': jnp.zeros((E,), jnp.float32), 'expert_w1': jax.random.uniform(ks[3], (E, D, H), jnp.float32, -s, s), 'expert_b1': jnp.zeros((E, H), jnp.float32), 'expert_w2': jax.random.uniform(ks[4], (E, H, H), jnp.float32, -sh, sh), 'expert_b2': jnp.zeros((E, H), jnp.float32), 'expert_w3': jax.random.uniform(ks[5], (E, H, D), jnp.float32, -sh, sh), 'expert_b3': jnp.zeros((E, D), jnp.float32)}
    _L0_ffn_all = _L0_ffn_setup()
    _L0_ffn_in = {k: v for k, v in _L0_ffn_all.items() if k in ('router_w1', 'router_b1', 'router_w2', 'router_b2', 'expert_w1', 'expert_b1', 'expert_w2', 'expert_b2', 'expert_w3', 'expert_b3')}
    del _L0_ffn_all

    def _L1_gnn_setup():
        import jax, jax.numpy as jnp
        import numpy as np
        N = 50000
        E = 25000
        D = 256
        R = 16
        B = 8
        LN_EPS = 1e-05

        def _layer_norm(x, g, b):
            mu = jnp.mean(x, axis=-1, keepdims=True)
            var = jnp.mean(jnp.square(x - mu), axis=-1, keepdims=True)
            return (x - mu) * jax.lax.rsqrt(var + LN_EPS) * g + b

        def _rgcn_layer(x, edge_index, edge_type, edge_attr, basis, att, root, bias):
            n = x.shape[0]
            r = att.shape[0]
            weight = jnp.einsum('rb,bio->rio', att, basis)
            H = jnp.einsum('ni,rio->nro', x, weight)
            loop = jnp.arange(n, dtype=edge_index.dtype)
            src = jnp.concatenate([edge_index[0], loop])
            dst = jnp.concatenate([edge_index[1], loop])
            et = jnp.concatenate([edge_type, jnp.full((n,), r - 1, dtype=edge_type.dtype)])
            ea = jnp.concatenate([edge_attr, jnp.ones((n,), dtype=x.dtype)])
            msg = H[src, et] * ea[:, None]
            summ = jax.ops.segment_sum(msg, dst, num_segments=n)
            cnt = jax.ops.segment_sum(jnp.ones_like(ea), dst, num_segments=n)
            agg = summ / cnt[:, None]
            return agg + x @ root + bias
        key = jax.random.key(seed)
        ks = jax.random.split(key, 20)
        s_basis = np.sqrt(2.0 / (D + D)).astype(np.float32)
        s_att = np.sqrt(2.0 / (R + B)).astype(np.float32)
        inp = {'x': jax.random.normal(ks[0], (N, D), dtype=jnp.float32), 'edge_index': jax.random.randint(ks[1], (2, E), 0, N), 'edge_type': jax.random.randint(ks[2], (E,), 0, R), 'edge_attr': jax.random.uniform(ks[3], (E,), dtype=jnp.float32), 'basis1': jax.random.normal(ks[4], (B, D, D), dtype=jnp.float32) * s_basis, 'att1': jax.random.normal(ks[5], (R, B), dtype=jnp.float32) * s_att, 'root1': jax.random.normal(ks[6], (D, D), dtype=jnp.float32) * s_basis, 'bias1': jnp.zeros((D,), dtype=jnp.float32), 'ln1_g': jnp.ones((D,), dtype=jnp.float32), 'ln1_b': jnp.zeros((D,), dtype=jnp.float32), 'basis2': jax.random.normal(ks[7], (B, D, D), dtype=jnp.float32) * s_basis, 'att2': jax.random.normal(ks[8], (R, B), dtype=jnp.float32) * s_att, 'root2': jax.random.normal(ks[9], (D, D), dtype=jnp.float32) * s_basis, 'bias2': jnp.zeros((D,), dtype=jnp.float32), 'ln2_g': jnp.ones((D,), dtype=jnp.float32), 'ln2_b': jnp.zeros((D,), dtype=jnp.float32)}
        return inp
    _L1_gnn_all = _L1_gnn_setup()
    _L1_gnn_in = {k: v for k, v in _L1_gnn_all.items() if k in ('basis1', 'att1', 'root1', 'bias1', 'ln1_g', 'ln1_b', 'basis2', 'att2', 'root2', 'bias2', 'ln2_g', 'ln2_b')}
    del _L1_gnn_all

    def _L1_ffn_setup():
        import jax, jax.numpy as jnp
        import numpy as np
        B, K, D = (512, 16, 256)
        E = 32
        H = int(D * 0.25)
        key = jax.random.key(seed)
        ks = jax.random.split(key, 7)
        d_rs = D ** (-0.5)
        h_rs = H ** (-0.5)
        x = jax.random.normal(ks[0], (B, K, D), dtype=jnp.float32)
        router_w = jax.random.uniform(ks[1], (E, D), jnp.float32, -d_rs, d_rs)
        router_b = jax.random.uniform(ks[2], (E,), jnp.float32, -d_rs, d_rs)
        W1 = jax.random.uniform(ks[3], (E, D, H), jnp.float32, -h_rs, h_rs)
        b1 = jax.random.uniform(ks[4], (E, H), jnp.float32, -h_rs, h_rs)
        W2 = jax.random.uniform(ks[5], (E, H, D), jnp.float32, -d_rs, d_rs)
        b2 = jax.random.uniform(ks[6], (E, D), jnp.float32, -d_rs, d_rs)
        return {'x': x, 'router_w': router_w, 'router_b': router_b, 'W1': W1, 'b1': b1, 'W2': W2, 'b2': b2}
    _L1_ffn_all = _L1_ffn_setup()
    _L1_ffn_in = {k: v for k, v in _L1_ffn_all.items() if k in ('router_w', 'router_b', 'W1', 'b1', 'W2', 'b2')}
    del _L1_ffn_all
    return {'x': x, 'src': src, 'dst': dst, 'edge_attr_2': edge_attr_2, 'edge_type_16': edge_type_16, 'edge_weight': edge_weight, 'L0_gnn_W_forward': _L0_gnn_in['W_forward'], 'L0_gnn_W_reverse': _L0_gnn_in['W_reverse'], 'L0_gnn_attn_forward': _L0_gnn_in['attn_forward'], 'L0_ffn_router_w1': _L0_ffn_in['router_w1'], 'L0_ffn_router_b1': _L0_ffn_in['router_b1'], 'L0_ffn_router_w2': _L0_ffn_in['router_w2'], 'L0_ffn_router_b2': _L0_ffn_in['router_b2'], 'L0_ffn_expert_w1': _L0_ffn_in['expert_w1'], 'L0_ffn_expert_b1': _L0_ffn_in['expert_b1'], 'L0_ffn_expert_w2': _L0_ffn_in['expert_w2'], 'L0_ffn_expert_b2': _L0_ffn_in['expert_b2'], 'L0_ffn_expert_w3': _L0_ffn_in['expert_w3'], 'L0_ffn_expert_b3': _L0_ffn_in['expert_b3'], 'L1_gnn_basis1': _L1_gnn_in['basis1'], 'L1_gnn_att1': _L1_gnn_in['att1'], 'L1_gnn_root1': _L1_gnn_in['root1'], 'L1_gnn_bias1': _L1_gnn_in['bias1'], 'L1_gnn_ln1_g': _L1_gnn_in['ln1_g'], 'L1_gnn_ln1_b': _L1_gnn_in['ln1_b'], 'L1_gnn_basis2': _L1_gnn_in['basis2'], 'L1_gnn_att2': _L1_gnn_in['att2'], 'L1_gnn_root2': _L1_gnn_in['root2'], 'L1_gnn_bias2': _L1_gnn_in['bias2'], 'L1_gnn_ln2_g': _L1_gnn_in['ln2_g'], 'L1_gnn_ln2_b': _L1_gnn_in['ln2_b'], 'L1_ffn_router_w': _L1_ffn_in['router_w'], 'L1_ffn_router_b': _L1_ffn_in['router_b'], 'L1_ffn_W1': _L1_ffn_in['W1'], 'L1_ffn_b1': _L1_ffn_in['b1'], 'L1_ffn_W2': _L1_ffn_in['W2'], 'L1_ffn_b2': _L1_ffn_in['b2']}

def reference(x, src, dst, edge_attr_2, edge_type_16, edge_weight, L0_gnn_W_forward, L0_gnn_W_reverse, L0_gnn_attn_forward, L0_ffn_router_w1, L0_ffn_router_b1, L0_ffn_router_w2, L0_ffn_router_b2, L0_ffn_expert_w1, L0_ffn_expert_b1, L0_ffn_expert_w2, L0_ffn_expert_b2, L0_ffn_expert_w3, L0_ffn_expert_b3, L1_gnn_basis1, L1_gnn_att1, L1_gnn_root1, L1_gnn_bias1, L1_gnn_ln1_g, L1_gnn_ln1_b, L1_gnn_basis2, L1_gnn_att2, L1_gnn_root2, L1_gnn_bias2, L1_gnn_ln2_g, L1_gnn_ln2_b, L1_ffn_router_w, L1_ffn_router_b, L1_ffn_W1, L1_ffn_b1, L1_ffn_W2, L1_ffn_b2):
    import jax
    import jax.numpy as jnp

    def _L0_gnn_ref(h, adj, direction, W_forward, W_reverse, attn_forward):
        import jax, jax.numpy as jnp
        import numpy as np
        N_NODES = 3125
        N_EDGES = 50000
        IN_FEATS = 256
        OUT_FEATS = 64
        NUM_HEADS = 4
        N = h.shape[0]
        H = attn_forward.shape[1]
        h_fwd = h @ W_forward.T
        h_rev = h @ W_reverse.T
        src, dst = (adj[0], adj[1])
        messages = h_fwd[src] * direction[:, 0:1] + h_rev[src] * direction[:, 1:2]
        scores = jnp.einsum('ef,hf->eh', messages, attn_forward[0])
        scores = jax.nn.leaky_relu(scores, negative_slope=0.2)
        exp_scores = jnp.exp(scores - scores.max(axis=0, keepdims=True))
        sum_exp = jax.ops.segment_sum(exp_scores, dst, num_segments=N)
        norm = exp_scores / (sum_exp[dst] + 1e-10)
        outs = [jax.ops.segment_sum(messages * norm[:, hd:hd + 1], dst, num_segments=N) for hd in range(H)]
        out = jnp.stack(outs, axis=1)
        return out.reshape(N, -1)

    def _L0_ffn_ref(features, router_w1, router_b1, router_w2, router_b2, expert_w1, expert_b1, expert_w2, expert_b2, expert_w3, expert_b3):
        import jax, jax.numpy as jnp
        import numpy as np
        E, D, H, TOP_K = (6, 256, 256, 2)
        ROUTER_H = D // 2
        rh = jax.nn.relu(features @ router_w1 + router_b1)
        expert_logits = jax.nn.softmax(rh @ router_w2 + router_b2, axis=-1)
        top_w, top_i = jax.lax.top_k(expert_logits, TOP_K)
        routing_weights = jax.nn.softmax(top_w, axis=-1)
        h1 = jax.nn.relu(jnp.einsum('bsd,edh->bseh', features, expert_w1) + expert_b1)
        h2 = jax.nn.relu(jnp.einsum('bseh,ehf->bsef', h1, expert_w2) + expert_b2)
        expert_out = jnp.einsum('bsef,efo->bseo', h2, expert_w3) + expert_b3
        sel = jnp.take_along_axis(expert_out, top_i[:, :, :, None], axis=2)
        combined = jnp.sum(sel * routing_weights[..., None], axis=2)
        return combined

    def _L1_gnn_ref(x, edge_index, edge_type, edge_attr, basis1, att1, root1, bias1, ln1_g, ln1_b, basis2, att2, root2, bias2, ln2_g, ln2_b):
        import jax, jax.numpy as jnp
        import numpy as np
        N = 50000
        E = 25000
        D = 256
        R = 16
        B = 8
        LN_EPS = 1e-05

        def _layer_norm(x, g, b):
            mu = jnp.mean(x, axis=-1, keepdims=True)
            var = jnp.mean(jnp.square(x - mu), axis=-1, keepdims=True)
            return (x - mu) * jax.lax.rsqrt(var + LN_EPS) * g + b

        def _rgcn_layer(x, edge_index, edge_type, edge_attr, basis, att, root, bias):
            n = x.shape[0]
            r = att.shape[0]
            weight = jnp.einsum('rb,bio->rio', att, basis)
            H = jnp.einsum('ni,rio->nro', x, weight)
            loop = jnp.arange(n, dtype=edge_index.dtype)
            src = jnp.concatenate([edge_index[0], loop])
            dst = jnp.concatenate([edge_index[1], loop])
            et = jnp.concatenate([edge_type, jnp.full((n,), r - 1, dtype=edge_type.dtype)])
            ea = jnp.concatenate([edge_attr, jnp.ones((n,), dtype=x.dtype)])
            msg = H[src, et] * ea[:, None]
            summ = jax.ops.segment_sum(msg, dst, num_segments=n)
            cnt = jax.ops.segment_sum(jnp.ones_like(ea), dst, num_segments=n)
            agg = summ / cnt[:, None]
            return agg + x @ root + bias
        h = x
        h_out = _rgcn_layer(h, edge_index, edge_type, edge_attr, basis1, att1, root1, bias1)
        h = jax.nn.relu(_layer_norm(h + h_out, ln1_g, ln1_b))
        h_out = _rgcn_layer(h, edge_index, edge_type, edge_attr, basis2, att2, root2, bias2)
        h = jax.nn.relu(_layer_norm(h + h_out, ln2_g, ln2_b))
        return h

    def _L1_ffn_ref(x, router_w, router_b, W1, b1, W2, b2):
        import jax, jax.numpy as jnp
        import numpy as np
        B, K, D = (512, 16, 256)
        E = 32
        H = int(D * 0.25)
        xf = x.reshape(-1, D)
        logits = xf @ router_w.T + router_b
        idx = jnp.argmax(logits, axis=-1)
        w1t = jnp.take(W1, idx, axis=0)
        h = jnp.einsum('nd,ndh->nh', xf, w1t) + jnp.take(b1, idx, axis=0)
        h = jax.nn.relu(h)
        w2t = jnp.take(W2, idx, axis=0)
        out = jnp.einsum('nh,nhd->nd', h, w2t) + jnp.take(b2, idx, axis=0)
        out = jax.nn.relu(out)
        return out.reshape(x.shape)
    edge_index = jnp.stack([src, dst])
    x = x + _L0_gnn_ref(_layernorm(x, axis=-1), edge_index, edge_attr_2, L0_gnn_W_forward, L0_gnn_W_reverse, L0_gnn_attn_forward)
    x = x + _L0_ffn_ref(_layernorm(x, axis=-1)[None], L0_ffn_router_w1, L0_ffn_router_b1, L0_ffn_router_w2, L0_ffn_router_b2, L0_ffn_expert_w1, L0_ffn_expert_b1, L0_ffn_expert_w2, L0_ffn_expert_b2, L0_ffn_expert_w3, L0_ffn_expert_b3)[0]
    x = x + _L1_gnn_ref(_layernorm(x, axis=-1), edge_index, edge_type_16, edge_weight, L1_gnn_basis1, L1_gnn_att1, L1_gnn_root1, L1_gnn_bias1, L1_gnn_ln1_g, L1_gnn_ln1_b, L1_gnn_basis2, L1_gnn_att2, L1_gnn_root2, L1_gnn_bias2, L1_gnn_ln2_g, L1_gnn_ln2_b)
    x = x + _L1_ffn_ref(_layernorm(x, axis=-1)[None], L1_ffn_router_w, L1_ffn_router_b, L1_ffn_W1, L1_ffn_b1, L1_ffn_W2, L1_ffn_b2)[0]
    return x

_drawn_inputs = setup_inputs


def setup_inputs(seed=0):
    import zlib

    import numpy as np

    out = dict(_drawn_inputs(seed))
    spreads = {'L0_ffn_router_b1': (0.0, 0.1),
     'L0_ffn_router_b2': (0.0, 0.1),
     'L0_ffn_expert_b1': (0.0, 0.516),
     'L0_ffn_expert_b2': (0.0, 0.1),
     'L0_ffn_expert_b3': (0.0, 0.1),
     'L1_gnn_bias1': (0.0, 0.1),
     'L1_gnn_ln1_g': (1.0, 0.2),
     'L1_gnn_ln1_b': (0.0, 0.1),
     'L1_gnn_bias2': (0.0, 0.1),
     'L1_gnn_ln2_g': (1.0, 0.2),
     'L1_gnn_ln2_b': (0.0, 0.1)}
    factors = {'L1_ffn_b1': 8.0, 'L1_ffn_b2': 3.756}
    for name, (base, spread) in spreads.items():
        noise = np.random.default_rng([zlib.crc32(name.encode()), seed]).standard_normal(out[name].shape)
        drawn = base * np.exp(spread * noise) if base else spread * noise
        out[name] = jnp.asarray(drawn.astype(out[name].dtype))
    for name, factor in factors.items():
        out[name] = (out[name] * factor).astype(out[name].dtype)
    return out
```

```python
from contextlib import ExitStack

import concourse.bass as bass
from concourse import mybir

ALU = mybir.AluOpType
ACT = mybir.ActivationFunctionType
AX = mybir.AxisListType
F32 = mybir.dt.float32
BF16 = mybir.dt.bfloat16
I32 = mybir.dt.int32
U32 = mybir.dt.uint32
I16 = mybir.dt.int16

P = 128
N = 3125
NT = 25
G = 5
NG = NT // G
GN = G * P
HB = GN // 2
D = 256
E = 50000
ET = (E + P - 1) // P
U = 4
GT = (ET + U - 1) // U
ETP = GT * U
NOWHERE = 4096
HEADS = 4
F = 64
C0 = F + HEADS
T0W = 2 * C0
MW = F + 1 + HEADS
S0W = HEADS * (F + 1) + 1
R = 16
B = 8
X0 = 6
X1 = 32
H1 = 64
M1 = X1 * H1 // P
EPS = 1e-5
FAR = -1.7e38


class Steps:

    def __init__(self, eng, sem):
        self.eng, self.sem = eng, sem
        self.before, self.n, self.turn, self.per_turn = 0, 0, None, 0

    def enter(self, turn, per_turn):
        self.before += self.n
        self.turn, self.per_turn, self.n = turn, per_turn, 0

    def leave(self, turns):
        assert self.n == self.per_turn, f"steps a turn: {self.n}"
        self.before += turns * self.per_turn
        self.turn, self.n = None, 0

    def step(self, ins):
        ins.then_inc(self.sem, 1)
        self.n += 1
        if self.turn is None:
            self.eng.wait_ge(self.sem, self.before + self.n)
        else:
            self.eng.wait_ge(self.sem, self.turn * self.per_turn + (self.before + self.n))
            self.eng.nop(nofuse=True)


def hold(eng, sem, value):
    eng.wait_ge(sem, value)
    eng.nop(nofuse=True)


def build(nc, a, out):
    ctx = ExitStack()
    with ctx:
        def sb(name, shape, dt=F32):
            return ctx.enter_context(nc.sbuf_tensor(name, shape, dt))

        def sem(name):
            return ctx.enter_context(nc.semaphore(name))

        gat_table = nc.dram_tensor("gat_table", (NT * P, T0W), F32, kind="Internal").ap()
        rel_table = [nc.dram_tensor(f"rel_table{l}", (NT * P * R, D), F32, kind="Internal").ap()
                     for l in range(2)]

        x_res = sb("x_res", [P, NT, D])
        region_a = sb("region_a", [P, 9216])
        region_b = sb("region_b", [P, 4096])
        region_m = sb("region_m", [P, GT * U * MW])
        iota_n = sb("iota_n", [P, NT * P], I16)
        src_idx = sb("src_idx", [P, ETP + U], I32)
        rel_idx = sb("rel_idx", [P, ETP], I32)
        dst_f = sb("dst_f", [P, ETP])
        ea = sb("ea", [P, ETP])
        idx4 = sb("idx4", [P, U], I32)
        ring = sb("ring", [P, U, D])
        onehot = sb("onehot", [P, U, P])
        ident = sb("ident", [P, P])
        rb1 = sb("rb1", [P, 1])
        rw2 = sb("rw2", [P, X0])
        rb2 = sb("rb2", [P, X0])
        eb1 = sb("eb1", [P, X0, 2])
        eb2 = sb("eb2", [P, X0, 2])
        eb3 = sb("eb3", [X0, D])
        stats = sb("stats", [P, G, 6])
        mv = sb("mv", [P, G, 2])
        veps = sb("veps", [P, G])
        std = sb("std", [P, G])
        rstd = sb("rstd", [P, G])
        rcnt = sb("rcnt", [P, NT])
        mx = sb("mx", [P, HEADS])
        gmx = sb("gmx", [P, HEADS])
        glr = sb("glr", [P, HEADS])
        den = sb("den", [P, HEADS + 1])
        rden = sb("rden", [P, HEADS + 1])
        ranges = sb("ranges", [P, 3, NT], I32)
        zeros = sb("zeros", [P, S0W], BF16)
        att_bc = sb("att_bc", [P, 2, R * B])
        att_cur = sb("att_cur", [P, B])
        lg = sb("lg", [P, G, X1])
        pr = sb("pr", [P, G, 8])
        top = sb("top", [P, G, 8])
        topi = sb("topi", [P, G, 8], U32)
        idxf = sb("idxf", [P, G, 2])
        gate = sb("gate", [P, G, 4])
        wsel = sb("wsel", [P, 2, G, X0])
        oh = sb("oh", [P, G, X1])
        iota_x = sb("iota_x", [P, X1])
        tile_no = sb("tile_no", [P, U])

        ew = [[region_a[:, (e * 3 + w) * 512:(e * 3 + w + 1) * 512].rearrange("p (k n) -> p k n", k=2)
               for w in range(3)] for e in range(X0)]
        h_res = region_a[:, 0:NT * D].rearrange("p (t d) -> p t d", d=D)
        rows_bc = region_a[:, 6656:6656 + 6 * D].rearrange("p (l c d) -> p l c d", l=2, c=3)
        root = region_a[:, 8192:8192 + 4 * D].rearrange("p (l k d) -> p l k d", l=2, k=2)
        negmask = region_a[0:X1, 0:1024].bitcast(BF16)
        ohT = region_a[0:X1, 1024:1024 + GN]
        ohTb = region_a[0:X1, 1664:1664 + GN // 2].bitcast(BF16)
        xb2 = region_a[0:X1, 2048:2048 + D]
        rwT = region_a[:, 2304:2304 + 2 * X1].rearrange("p (k n) -> p k n", k=2)
        rb = region_a[:, 2368:2368 + X1]
        xb1 = region_a[:, 2400:2400 + M1]
        outs = region_a[:, 2432:2432 + G * D].rearrange("p (t d) -> p t d", d=D)
        dir_e = region_b[:, 0:2 * ETP].rearrange("p (t c) -> p t c", c=2)
        rev = region_b[:, 800:800 + U * C0].rearrange("p (j c) -> p j c", c=C0)
        rhs0 = region_b[:, 1072:1072 + U * (S0W + 1)].rearrange("p (j c) -> p j c", c=S0W + 1)
        t0s = region_b[:, 1072:1072 + G * T0W].rearrange("p (j c) -> p j c", c=T0W)
        dstT = region_b[:, 2120:2120 + 512].bitcast(I32).rearrange("p (j c) -> p j c", c=P)
        et_i = region_b[:, 2632:2632 + ETP].bitcast(I32)
        dst_i = region_b[:, 3028:3028 + ETP].bitcast(I32)
        wcat = region_b[:, 3424:3424 + 2 * T0W].rearrange("p (k c) -> p k c", k=2)
        basis = region_b[:, :].rearrange("p (b k n) -> p b k n", b=B, k=2)
        stage = region_b
        msg = region_m[:, :].rearrange("p (t c) -> p t c", c=MW)
        wrel = [region_m[:, l * 8192:(l + 1) * 8192].rearrange("p (k n) -> p k n", k=2) for l in range(2)]
        at = 16384
        base = region_m[:, at:at + NT * D].rearrange("p (t d) -> p t d", d=D)
        h1T = region_m[:, at:at + 2560].rearrange("p (s m n) -> p s m n", s=2, m=2)
        h2T = region_m[:, at + 2560:at + 5120].rearrange("p (s m n) -> p s m n", s=2, m=2)
        wacc = region_m[:, at + 5120:at + 6144].rearrange("p (s k n) -> p s k n", s=2, k=2)
        at += NT * D
        rhT = region_m[:, at:at + GN]
        wT = region_m[0:X0, at + GN:at + 2 * GN]
        at += 2 * GN
        xn5 = region_m[:, at:at + G * D].rearrange("p (t d) -> p t d", d=D)
        at += G * D
        xT5 = region_m[:, at:at + 2 * GN].rearrange("p (k n) -> p k n", k=2)
        at += 2 * GN
        rw1 = region_m[:, at:at + 2 * P].rearrange("p (k n) -> p k n", k=2)
        assert at + 2 * P <= GT * U * MW
        xw1 = region_m[:, 0:4096].rearrange("p (k n) -> p k n", k=2)
        xw2 = region_m[:, 4096:8192].rearrange("p (m n) -> p m n", m=M1)
        hmT = region_m[:, 8192:8192 + M1 * GN].rearrange("p (m n) -> p m n", m=M1)

        bank = [ctx.enter_context(nc.psum_tensor(f"bank{i}", [P, 512], F32)) for i in range(8)]

        meta_loaded, x_loaded, gatw_loaded, ident_loaded = map(sem, (
            "meta_loaded", "x_loaded", "gatw_loaded", "ident_loaded"))
        ffn0_loaded, small0_loaded, basis_loaded, rows_loaded, ffn1_loaded = map(sem, (
            "ffn0_loaded", "small0_loaded", "basis_loaded", "rows_loaded", "ffn1_loaded"))
        consts_done, bounds_ready, bounds_max, ranges_done, relidx_done = map(sem, (
            "consts_done", "bounds_ready", "bounds_max", "ranges_done", "relidx_done"))
        attw_done, wcat_done = map(sem, ("attw_done", "wcat_done"))
        var_ready, std_ready, xn_ready, turned, xT_ready = map(sem, (
            "var_ready", "std_ready", "xn_ready", "turned", "xT_ready"))
        t_product, t_staged, t_stored = map(sem, ("t_product", "t_staged", "t_stored"))
        g0_rev, lmax_ready, gmax_ready, exp_in, exp_out = map(sem, (
            "g0_rev", "lmax_ready", "gmax_ready", "exp_in", "exp_out"))
        s0_ready, s0_summed, s0_read = map(sem, ("s0_ready", "s0_summed", "s0_read"))
        s0_used = [sem(f"s0_used{j}") for j in range(U)]
        f_rh, f_rhT, f_logits, f_softin, f_softout, f_gap, f_gapexp, f_w, f_wturned, f_wT = map(sem, (
            "f_rh", "f_rhT", "f_logits", "f_softin", "f_softout", "f_gap", "f_gapexp", "f_w", "f_wturned", "f_wT"))
        f_h1, f_h1T, f_h2, f_h2T, f_o, f_oread = map(sem, ("f_h1", "f_h1T", "f_h2", "f_h2T", "f_o", "f_oread"))
        wrel_done = sem("wrel_done")
        rw1_loaded = sem("rw1_loaded")
        r_rootx, r_based, r_even, r_odd, r_evenout, r_oddout = [
            [sem(f"{n}{l}") for l in range(2)] for n in (
                "r_rootx", "r_based", "r_even", "r_odd", "r_evenout", "r_oddout")]
        r_stored = [[sem(f"r_stored{l}_{c}") for c in range(4)] for l in range(2)]
        e_ready, e_summed, e_read, e_var, e_std, e_posted = [
            [sem(f"{n}{l}") for l in range(2)] for n in (
                "e_ready", "e_summed", "e_read", "e_var", "e_std", "e_posted")]
        got = [[sem(f"got{l}_{j}") for j in range(U)] for l in range(3)]
        used = [[sem(f"used{l}_{j}") for j in range(U)] for l in range(3)]
        x_logits, x_oh, x_ohturned, x_ohT, x_h, x_hT, x_o, x_oread, x_stored = map(sem, (
            "x_logits", "x_oh", "x_ohturned", "x_ohT", "x_h", "x_hT", "x_o", "x_oread", "x_stored"))
        dve_step, pool_step = map(sem, ("dve_step", "pool_step"))

        x_d = a["x"].rearrange("(t p) d -> p t d", p=P)
        gat_rows = gat_table.rearrange("(t p) c -> p t c", p=P)
        rel_rows = [rel_table[l].rearrange("(t p r) d -> p t (r d)", p=P, r=R) for l in range(2)]
        out_rows = out.rearrange("(t p) d -> p t d", p=P)
        small_loads = 6 + 2 * X0

        def walk(eng, t):
            return (eng.value_load(ranges[0:1, 0, bass.ds(t, 1)], min_val=0, max_val=ET),
                    eng.value_load(ranges[0:1, 1, bass.ds(t, 1)], min_val=U, max_val=GT * U),
                    eng.value_load(ranges[0:1, 2, bass.ds(t, 1)], min_val=0, max_val=NT * GT * U))

        def tile_of(lo, r):
            return nc.s_assert_within(lo + r, 0, ETP - U)

        block = ctx.enter_context(nc.Block())

        @block.sync
        def _(sp):
            def load(dst, src, done):
                sp.dma_start(dst, src).then_inc(done, 16)

            sp.nop().then_inc(t_stored, 16)
            for l in range(2):
                for c in range(4):
                    sp.nop().then_inc(r_stored[l][c], 16)
            sp.nop().then_inc(x_stored, 16)

            load(x_res[:, :, :], x_d, x_loaded)
            load(dstT, a["dst_rows"], meta_loaded)
            load(dst_i, a["dst_t"], meta_loaded)
            load(src_idx[:, 0:ETP], a["src_t"], meta_loaded)
            load(et_i, a["et_t"], meta_loaded)
            load(ea[:, :], a["ea_t"], meta_loaded)
            load(dir_e, a["dir_t"], meta_loaded)
            load(wcat[:, :, 0:F], a["wf_T"].rearrange("(k p) f -> p k f", p=P), gatw_loaded)
            load(wcat[:, :, C0:C0 + F], a["wr_T"].rearrange("(k p) f -> p k f", p=P), gatw_loaded)
            load(onehot[0:F, 0:2, :], a["wf"].rearrange("f (k n) -> f k n", k=2), gatw_loaded)
            load(onehot[0:F, 2:4, :], a["wr"].rearrange("f (k n) -> f k n", k=2), gatw_loaded)
            load(ring[0:F, 0, 0:HEADS], a["attn_T"], gatw_loaded)
            load(ident[:, :], a["ident"], ident_loaded)
            for e in range(X0):
                for w, name in enumerate(("ew1", "ew2", "ew3")):
                    load(ew[e][w], a[name][e].rearrange("(k p) n -> p k n", p=P), ffn0_loaded)
            load(rb1[:, :], a["rb1"].rearrange("(p o) -> p o", o=1), small0_loaded)
            load(rw2[:, :], a["rw2"], small0_loaded)
            load(rb2[:, :], a["rb2"].partition_broadcast(P), small0_loaded)
            for e in range(X0):
                load(eb1[:, e, :], a["eb1T"][:, e, :], small0_loaded)
                load(eb2[:, e, :], a["eb2T"][:, e, :], small0_loaded)
            load(eb3[:, :], a["eb3"], small0_loaded)
            for l in range(2):
                load(att_bc[:, l, :], a[f"att{l}"].partition_broadcast(P), small0_loaded)

            with sp.Fori(0, NG) as g:
                sp.wait_ge(t_staged, (g + 1) * 2)
                sp.dma_start(gat_rows[:, bass.ds(g * G, G), :], t0s).then_inc(t_stored, 16)
            sp.wait_ge(s0_read, NT + 1)
            load(basis, a["basis0"].rearrange("b (k p) n -> p b k n", p=P), basis_loaded)
            load(rw1, a["rw1"].rearrange("(k p) n -> p k n", p=P), rw1_loaded)
            sp.wait_ge(wrel_done, R)
            load(basis, a["basis1"].rearrange("b (k p) n -> p b k n", p=P), basis_loaded)
            sp.wait_ge(f_oread, NG * 21 + 1)
            for l in range(2):
                for c, name in enumerate(("bias", "ln_g", "ln_b")):
                    load(rows_bc[:, l, c, :], a[f"{name}{l}"].partition_broadcast(P), rows_loaded)
                load(root[:, l, :, :], a[f"root{l}"].rearrange("(k p) n -> p k n", p=P), rows_loaded)

            def store_rel(l):
                with sp.Fori(0, NT) as t:
                    for c in range(4):
                        sp.wait_ge(r_evenout[l], t * 4 + (c + 3))
                        sp.wait_ge(r_oddout[l], t * 4 + (c + 3))
                        sp.dma_start(rel_rows[l][:, bass.ds(t, 1), c * 1024:(c + 1) * 1024],
                                     stage[:, c * 1024:(c + 1) * 1024].unsqueeze(1)).then_inc(r_stored[l][c], 16)

            store_rel(0)
            store_rel(1)
            sp.wait_ge(r_based[1], NT + 1)
            load(xw1, a["xw1"].rearrange("(k p) n -> p k n", p=P), ffn1_loaded)
            load(xw2, a["xw2"].rearrange("(m p) n -> p m n", p=P), ffn1_loaded)
            load(negmask, a["negmask"], ffn1_loaded)
            load(xb2, a["xb2"], ffn1_loaded)
            load(rwT, a["rwT"].rearrange("(k p) n -> p k n", p=P), ffn1_loaded)
            load(rb, a["rb"].partition_broadcast(P), ffn1_loaded)
            load(xb1, a["xb1T"], ffn1_loaded)
            with sp.Fori(0, NG) as g:
                sp.wait_ge(x_oread, g * 3 + 4)
                sp.dma_start(out_rows[:, bass.ds(g * G, G), :], outs).then_inc(x_stored, 16)
            sp.wait_ge(x_stored, 16 * (NG + 1))

        @block.gpsimd
        def _(pool):
            pool.iota(iota_n[:, :], pattern=[[1, NT * P]], base=0, channel_multiplier=0).then_inc(consts_done, 1)
            pool.iota(iota_x[:, :], pattern=[[1, X1]], base=0, channel_multiplier=0,
                      allow_small_or_imprecise_dtypes=True).then_inc(consts_done, 1)
            pool.iota(tile_no[:, :], pattern=[[P, U]], base=0, channel_multiplier=1,
                      allow_small_or_imprecise_dtypes=True).then_inc(consts_done, 1)
            pool.memset(zeros[:, :], 0.0).then_inc(consts_done, 1)
            pool.memset(pr[:, :, :], -1.0).then_inc(consts_done, 1)
            pool.wait_ge(bounds_ready, 1)
            pool.partition_all_reduce(xT5[:, 0, 0:2 * NT], xT5[:, 1, 0:2 * NT], P,
                                      bass.bass_isa.ReduceOp.max).then_inc(bounds_max, 1)

            def gather(l, j, table, width):
                pool.indirect_dma_start(
                    out=ring[:, j, 0:width], out_offset=None, in_=table,
                    in_offset=bass.IndirectOffsetOnAxis(ap=idx4[:, j:j + 1], axis=0)).then_inc(got[l][j], 16)

            pool.wait_ge(meta_loaded, 6 * 16)
            pool.wait_ge(t_stored, 16 * (NG + 1))
            with pool.Fori(0, GT) as i:
                for j in range(U):
                    hold(pool, used[2][j], i + 1)
                    gather(2, j, gat_table, T0W)
            pool.wait_ge(lmax_ready, 1)
            pool.partition_all_reduce(gmx[:, :], mx[:, :], P, bass.bass_isa.ReduceOp.max).then_inc(gmax_ready, 1)

            pool.wait_ge(small0_loaded, small_loads * 16)
            steps = Steps(pool, pool_step)
            for l in range(2):
                pool.wait_ge(basis_loaded, 16 * (l + 1))
                with pool.Fori(0, R) as r:
                    steps.enter(r, 2 * B - 1)
                    steps.step(pool.tensor_copy(att_cur[:, :], att_bc[:, l, bass.ds(r * B, B)]))
                    steps.step(pool.tensor_scalar(wacc[:, 0], basis[:, 0], att_cur[:, 0:1], None, ALU.mult))
                    for b in range(1, B):
                        steps.step(pool.tensor_scalar(wacc[:, 1], basis[:, b], att_cur[:, b:b + 1], None,
                                                      ALU.mult))
                        if b < B - 1:
                            steps.step(pool.tensor_tensor(wacc[:, 0], wacc[:, 0], wacc[:, 1], ALU.add))
                        else:
                            pool.tensor_tensor(wrel[l][:, :, bass.ds(r * D, D)], wacc[:, 0], wacc[:, 1],
                                               ALU.add).then_inc(wrel_done, 1)
                            hold(pool, wrel_done, r + (l * R + 1))
                steps.leave(R)

            for l in range(2):
                for c in range(4):
                    pool.wait_ge(r_stored[l][c], 16 * (NT + 1))
                pool.wait_ge(ranges_done, 1)
                with pool.Fori(0, NT) as t:
                    lo, cnt, q0 = walk(pool, t)
                    with pool.Fori(0, cnt, U) as r:
                        for j in range(U):
                            hold(pool, e_ready[l], q0 + r + (j + 1))
                            gather(l, j, rel_table[l], D)

        @block.scalar
        def _(act):
            for l in range(2):
                for j in range(U):
                    act.nop().then_inc(used[l][j], 1)
            for j in range(U):
                act.nop().then_inc(s0_used[j], 1)
            for l in range(2):
                act.nop().then_inc(r_evenout[l], 2)

            def std_group(k):
                hold(act, var_ready, k + 1)
                act.activation(std[:, :], veps[:, :], ACT.Sqrt).then_inc(std_ready, 1)

            def copy_turned(k):
                hold(act, turned, k + 2)
                act.activation(xT5[:, 0, 0:512], bank[0][:, :], ACT.Copy)
                act.activation(xT5[:, 1, 0:512], bank[2][:, :], ACT.Copy)
                act.activation(xT5[:, :, 512:GN], bank[1][:, 0:256].rearrange("p (k n) -> p k n", k=2),
                               ACT.Copy).then_inc(xT_ready, 1)

            with act.Fori(0, NG) as g:
                std_group(g)
                copy_turned(g)
            act.wait_ge(meta_loaded, 6 * 16)
            with act.Fori(0, GT) as i:
                d4 = dir_e[:, bass.ds(i * U, U), :]
                for j in range(U):
                    hold(act, got[2][j], (i + 1) * 16)
                    act.activation(rev[:, j, :], ring[:, j, C0:T0W], ACT.Copy,
                                   scale=d4[:, j, 1:2]).then_inc(g0_rev, 1)
            act.wait_ge(exp_in, 1)
            act.activation(msg[:, :, F + 1:MW], msg[:, :, F + 1:MW], ACT.Exp).then_inc(exp_out, 1)

            act.wait_ge(small0_loaded, small_loads * 16)
            with act.Fori(0, NG) as g:
                def h1_out(e):
                    for m in range(2):
                        for nb in range(2):
                            hold(act, f_h1, g * (X0 * 4) + (e * 4 + m * 2 + nb + 1))
                            act.activation(h1T[:, e % 2, m, nb * HB:(nb + 1) * HB], bank[nb][:, 0:HB],
                                           ACT.Relu, bias=eb1[:, e, m:m + 1]).then_inc(f_h1T, 1)

                def h2_out(e):
                    for m in range(2):
                        for nb in range(2):
                            hold(act, f_h2, g * (X0 * 4) + (e * 4 + m * 2 + nb + 1))
                            act.activation(h2T[:, e % 2, m, nb * HB:(nb + 1) * HB], bank[2 + nb][:, 0:HB],
                                           ACT.Relu, bias=eb2[:, e, m:m + 1]).then_inc(f_h2T, 1)

                std_group(g + NG)
                copy_turned(g + NG)
                for nb in range(2):
                    hold(act, f_rh, g * 2 + (nb + 1))
                    act.activation(rhT[:, nb * HB:(nb + 1) * HB], bank[6 + nb][:, 0:HB], ACT.Relu,
                                   bias=rb1[:, 0:1]).then_inc(f_rhT, 1)
                h1_out(0)
                hold(act, f_softin, g + 1)
                act.activation(lg[:, :, 0:X0], lg[:, :, 0:X0], ACT.Exp).then_inc(f_softout, 1)
                h1_out(1)
                hold(act, f_gap, g + 1)
                act.activation(gate[:, :, 1:2], gate[:, :, 0:1], ACT.Exp).then_inc(f_gapexp, 1)
                h2_out(0)
                hold(act, f_wturned, g + 1)
                act.activation(wT[:, 0:512], bank[6][0:X0, :], ACT.Copy)
                act.activation(wT[:, 512:GN], bank[7][0:X0, 0:P], ACT.Copy).then_inc(f_wT, 1)
                for e in range(2, X0):
                    h1_out(e)
                    h2_out(e - 1)
                h2_out(X0 - 1)

            def rel_groups(l):
                with act.Fori(0, NG) as g:
                    if l == 0:
                        std_group(g + 2 * NG)
                    copy_turned(g + (2 + l) * NG)
                    for j in range(G):
                        for c in range(4):
                            hold(act, r_even[l], g * (4 * G) + (j * 4 + c + 1))
                            hold(act, r_stored[l][c], g * (16 * G) + (j + 1) * 16)
                            act.activation(stage[:, c * 1024:c * 1024 + 512], bank[4 + 2 * (c % 2)][:, :],
                                           ACT.Copy).then_inc(r_evenout[l], 1)

            def seg_std(l):
                with act.Fori(0, NT) as t:
                    hold(act, e_var[l], t + 1)
                    act.activation(std[:, 0:1], veps[:, 0:1], ACT.Sqrt).then_inc(e_std[l], 1)

            for l in range(2):
                rel_groups(l)
                seg_std(l)
            act.wait_ge(ffn1_loaded, 7 * 16)
            with act.Fori(0, NG) as g:
                std_group(g + 3 * NG)
                copy_turned(g + 4 * NG)
                hold(act, x_ohturned, g + 1)
                act.activation(ohTb[:, 0:512], bank[3][0:X1, :], ACT.Copy)
                act.activation(ohTb[:, 512:GN], bank[1][0:X1, 256:384], ACT.Copy).then_inc(x_ohT, 1)
                act.activation(ohT[:, 0:512], bank[3][0:X1, :], ACT.Copy)
                act.activation(ohT[:, 512:GN], bank[1][0:X1, 256:384], ACT.Copy).then_inc(x_ohT, 1)
                for m in range(M1):
                    for nb in range(2):
                        u = m * 2 + nb
                        hold(act, x_h, g * (2 * M1) + (u + 1))
                        act.activation(hmT[:, m, nb * HB:(nb + 1) * HB], bank[4 + u % 3][:, 0:HB], ACT.Relu,
                                       bias=xb1[:, m:m + 1]).then_inc(x_hT, 1)

        @block.tensor
        def _(pe):
            def turn_group(k):
                hold(pe, xn_ready, k + 1)
                for j in range(G):
                    for h in range(2):
                        o = bank[2 * h][:, j * P:(j + 1) * P] if j < 4 else bank[1][:, h * P:(h + 1) * P]
                        last = pe.transpose(o, xn5[:, j, h * P:(h + 1) * P], ident[:, :])
                last.then_inc(turned, 1)
                hold(pe, xT_ready, k + 1)

            def zero_product(dst, width, start):
                return pe.matmul(dst[:, 0:width], zeros[:, 0:P], zeros[:, 0:width], start=start, stop=not start,
                                 skip_group_check=True)

            pe.wait_ge(gatw_loaded, 5 * 16)
            for d in range(2):
                for k in range(2):
                    last = pe.matmul(bank[5][:, (d * 2 + k) * HEADS:(d * 2 + k + 1) * HEADS],
                                     onehot[0:F, 2 * d + k, :], ring[0:F, 0, 0:HEADS], start=True, stop=True)
            last.then_inc(attw_done, 1)
            pe.wait_ge(ident_loaded, 16)
            pe.wait_ge(wcat_done, 1)
            with pe.Fori(0, NG) as g:
                turn_group(g)
                for half, tiles in ((0, (0, 1, 2)), (1, (3, 4))):
                    for i, j in enumerate(tiles):
                        for k in range(2):
                            last = pe.matmul(bank[3 + half][:, i * T0W:(i + 1) * T0W],
                                             xT5[:, k, j * P:(j + 1) * P], wcat[:, k, :],
                                             start=(k == 0), stop=(k == 1))
                    last.then_inc(t_product, 1)
            pe.wait_ge(consts_done, 5)
            pe.wait_ge(ranges_done, 1)
            with pe.Fori(0, NT) as t:
                lo, cnt, q0 = walk(pe, t)
                hold(pe, s0_read, t + 1)
                zero_product(bank[5], S0W, True)
                with pe.Fori(0, cnt, U) as r:
                    for j in range(U):
                        hold(pe, s0_ready, q0 + r + (j + 1))
                        pe.matmul(bank[5][:, 0:S0W], onehot[:, j, :], rhs0[:, j, 0:S0W], start=False, stop=False,
                                  skip_group_check=True).then_inc(s0_used[j], 1)
                zero_product(bank[5], S0W, False).then_inc(s0_summed, 1)

            pe.wait_ge(ffn0_loaded, X0 * 3 * 16)
            pe.wait_ge(small0_loaded, small_loads * 16)
            pe.wait_ge(rw1_loaded, 16)
            with pe.Fori(0, NG) as g:
                def h1_product(e):
                    for m in range(2):
                        for nb in range(2):
                            u = e * 4 + m * 2 + nb
                            if u >= 2:
                                hold(pe, f_h1T, g * (X0 * 4) + (u - 1))
                            for k in range(2):
                                last = pe.matmul(bank[nb][:, 0:HB], ew[e][0][:, k, m * P:(m + 1) * P],
                                                 xT5[:, k, nb * HB:(nb + 1) * HB], start=(k == 0), stop=(k == 1))
                            last.then_inc(f_h1, 1)

                def h2_product(e):
                    hold(pe, f_h1T, g * (X0 * 4) + (e * 4 + 4))
                    for m in range(2):
                        for nb in range(2):
                            u = e * 4 + m * 2 + nb
                            if u >= 2:
                                hold(pe, f_h2T, g * (X0 * 4) + (u - 1))
                            for k in range(2):
                                last = pe.matmul(bank[2 + nb][:, 0:HB], ew[e][1][:, k, m * P:(m + 1) * P],
                                                 h1T[:, e % 2, k, nb * HB:(nb + 1) * HB],
                                                 start=(k == 0), stop=(k == 1))
                            last.then_inc(f_h2, 1)

                def o_unit(e, pair, product):
                    u = (e + 1) * 3 + pair
                    hold(pe, f_oread, g * 21 + (max(u - 1, 0) + 1))
                    for i, j in enumerate(range(2 * pair, min(2 * pair + 2, G))):
                        last = product(bank[4 + u % 2][:, i * D:(i + 1) * D], j)
                    last.then_inc(f_o, 1)

                def o_product(e):
                    hold(pe, f_h2T, g * (X0 * 4) + (e * 4 + 4))

                    def product(o, j):
                        for k in range(2):
                            last = pe.matmul(o, h2T[:, e % 2, k, j * P:(j + 1) * P], ew[e][2][:, k, :],
                                             start=(k == 0), stop=(k == 1))
                        return last
                    for pair in range(3):
                        o_unit(e, pair, product)

                turn_group(g + NG)
                for nb in range(2):
                    for k in range(2):
                        last = pe.matmul(bank[6 + nb][:, 0:HB], rw1[:, k, :], xT5[:, k, nb * HB:(nb + 1) * HB],
                                         start=(k == 0), stop=(k == 1))
                    last.then_inc(f_rh, 1)
                hold(pe, f_rhT, g * 2 + 2)
                for j in range(G):
                    last = pe.matmul(bank[3][:, j * 8:j * 8 + X0], rhT[:, j * P:(j + 1) * P], rw2[:, :],
                                     start=True, stop=True)
                last.then_inc(f_logits, 1)
                h1_product(0)
                h1_product(1)
                hold(pe, f_softin, g + 1)
                h2_product(0)
                hold(pe, f_w, g + 1)
                for j in range(G):
                    o = bank[6][0:X0, j * P:(j + 1) * P] if j < 4 else bank[7][0:X0, 0:P]
                    last = pe.transpose(o, wsel[:, 0, j, :], ident[:, :])
                last.then_inc(f_wturned, 1)
                hold(pe, f_wT, g + 1)
                for pair in range(3):
                    o_unit(-1, pair, lambda o, j: pe.matmul(o, wT[:, j * P:(j + 1) * P], eb3[:, :],
                                                            start=True, stop=True))
                for e in range(2, X0):
                    h1_product(e)
                    h2_product(e - 1)
                    o_product(e - 2)
                h2_product(X0 - 1)
                o_product(X0 - 2)
                o_product(X0 - 1)

            def rel_groups(l):
                with pe.Fori(0, NG) as g:
                    turn_group(g + (2 + l) * NG)
                    for j in range(G):
                        n1 = g * G + (j + 1)
                        hold(pe, r_based[l], n1)
                        for k in range(2):
                            last = pe.matmul(bank[3][:, 0:D], xT5[:, k, j * P:(j + 1) * P], root[:, l, k, :],
                                             start=(k == 0), stop=(k == 1))
                        last.then_inc(r_rootx[l], 1)
                        for c in range(4):
                            for half, (out_of, done) in enumerate(((r_evenout[l], r_even[l]),
                                                                   (r_oddout[l], r_odd[l]))):
                                hold(pe, out_of, g * (4 * G) + (j * 4 + c + 1))
                                for k in range(2):
                                    col = c * 1024 + half * 512
                                    last = pe.matmul(bank[4 + 2 * (c % 2) + half][:, :],
                                                     xT5[:, k, j * P:(j + 1) * P], wrel[l][:, k, col:col + 512],
                                                     start=(k == 0), stop=(k == 1))
                                last.then_inc(done, 1)

            def edge_sums(l):
                with pe.Fori(0, NT) as t:
                    lo, cnt, q0 = walk(pe, t)
                    hold(pe, e_read[l], t + 1)
                    zero_product(bank[0], D, True)
                    with pe.Fori(0, cnt, U) as r:
                        for j in range(U):
                            hold(pe, e_ready[l], q0 + r + (j + 1))
                            hold(pe, got[l][j], ((q0 + r) // U) * 16 + 16)
                            pe.matmul(bank[0][:, 0:D], onehot[:, j, :], ring[:, j, :], start=False, stop=False,
                                      skip_group_check=True).then_inc(used[l][j], 1)
                    zero_product(bank[0], D, False).then_inc(e_summed[l], 1)

            for l in range(2):
                if l == 0:
                    pe.wait_ge(wrel_done, 2 * R)
                    pe.wait_ge(rows_loaded, 8 * 16)
                rel_groups(l)
                edge_sums(l)
            pe.wait_ge(ffn1_loaded, 7 * 16)
            with pe.Fori(0, NG) as g:
                turn_group(g + 4 * NG)
                hold(pe, x_oread, g * 3 + 1)
                for j in range(G):
                    for k in range(2):
                        last = pe.matmul(bank[7][:, j * X1:(j + 1) * X1], xT5[:, k, j * P:(j + 1) * P],
                                         rwT[:, k, :], start=(k == 0), stop=(k == 1))
                last.then_inc(x_logits, 1)
                hold(pe, x_oh, g + 1)
                for j in range(G):
                    o = bank[3][0:X1, j * P:(j + 1) * P] if j < 4 else bank[1][0:X1, 256:384]
                    last = pe.transpose(o, oh[:, j, :], ident[:, :])
                last.then_inc(x_ohturned, 1)
                hold(pe, x_ohT, g * 2 + 1)
                for m in range(M1):
                    for nb in range(2):
                        u = m * 2 + nb
                        if u >= 3:
                            hold(pe, x_hT, g * (2 * M1) + (u - 2))
                        o = bank[4 + u % 3][:, 0:HB]
                        for k in range(2):
                            pe.matmul(o, xw1[:, k, m * P:(m + 1) * P], xT5[:, k, nb * HB:(nb + 1) * HB],
                                      start=(k == 0), stop=False)
                        pe.matmul(o, negmask[:, m * P:(m + 1) * P], ohTb[:, nb * HB:(nb + 1) * HB],
                                  start=False, stop=True).then_inc(x_h, 1)
                hold(pe, x_ohT, g * 2 + 2)
                hold(pe, x_hT, g * (2 * M1) + 2 * M1)
                for pair in range(3):
                    if pair == 2:
                        hold(pe, x_oread, g * 3 + 2)
                    for i, j in enumerate(range(2 * pair, min(2 * pair + 2, G))):
                        o = bank[3 + 4 * (pair % 2)][:, i * D:(i + 1) * D]
                        pe.matmul(o, ohT[:, j * P:(j + 1) * P], xb2, start=True, stop=False)
                        for m in range(M1):
                            last = pe.matmul(o, hmT[:, m, j * P:(j + 1) * P], xw2[:, m, :],
                                             start=False, stop=(m == M1 - 1))
                    last.then_inc(x_o, 1)

        @block.vector
        def _(dve):
            steps = Steps(dve, dve_step)
            v = dve
            for one in (turned, s0_read, f_oread, r_based[0], r_based[1], e_read[0], e_read[1], x_oread):
                v.nop().then_inc(one, 1)
            for l in range(2):
                v.nop().then_inc(r_oddout[l], 2)

            def norm_group(g, k, ks):
                hold(v, turned, k + 1)
                for j in range(G):
                    last = v.bn_stats(stats[:, j, :], x_res[:, bass.ds(g * G + j, 1), :].rearrange("p o d -> p (o d)"))
                steps.step(last)
                for j in range(G):
                    last = v.bn_aggr(mv[:, j, :], stats[:, j, :])
                steps.step(last)
                v.tensor_scalar(veps[:, :], mv[:, :, 1], EPS, None, ALU.add).then_inc(var_ready, 1)
                hold(v, std_ready, ks + 1)
                steps.step(v.reciprocal(rstd[:, :], std[:, :]))
                for j in range(G):
                    last = v.tensor_scalar(xn5[:, j, :], x_res[:, bass.ds(g * G + j, 1), :].rearrange(
                        "p o d -> p (o d)"), mv[:, j, 0:1], rstd[:, j:j + 1], ALU.subtract, ALU.mult)
                last.then_inc(xn_ready, 1)

            v.wait_ge(meta_loaded, 6 * 16)
            v.wait_ge(consts_done, 5)
            tmp = xn5[:, :, :].rearrange("p t d -> p (t d)")
            emin, emax = tmp[:, 0:4], tmp[:, 4:8]
            c1 = tmp[:, 130:230].rearrange("p (n j) -> p n j", j=4)
            c2 = tmp[:, 230:330].rearrange("p (n j) -> p n j", j=4)
            c3 = tmp[:, 330:430].rearrange("p (n j) -> p n j", j=4)
            up = xT5[:, 1, 0:2 * NT]
            m2 = xT5[:, 0, 0:2 * NT]
            first = iota_n[:, :].rearrange("p (n q) -> p n q", q=P)[:, :, 0:1].broadcast_to([P, NT, 4])

            def row(x):
                return x.unsqueeze(1).broadcast_to([P, NT, 4])
            steps.step(v.tensor_reduce(emin, dstT, AX.X, ALU.min))
            steps.step(v.tensor_reduce(emax, dstT, AX.X, ALU.max))
            steps.step(v.tensor_scalar(emin, emin, float(P - 1), None, ALU.subtract))
            steps.step(v.tensor_tensor(c1, row(emin), first, ALU.is_le))
            steps.step(v.tensor_tensor(c2, row(emax), first, ALU.is_ge))
            steps.step(v.tensor_tensor(c1, c1, c2, ALU.mult))
            steps.step(v.tensor_scalar(tmp[:, 8:12], tile_no[:, :], -1.0, float(ET), ALU.mult, ALU.add))
            steps.step(v.tensor_scalar(tmp[:, 12:16], tile_no[:, :], 1.0, None, ALU.add))
            steps.step(v.tensor_tensor(c2, c1, row(tmp[:, 8:12]), ALU.mult))
            steps.step(v.tensor_tensor(c3, c1, row(tmp[:, 12:16]), ALU.mult))
            v.tensor_reduce(up[:, 0:NT], c2, AX.X, ALU.max)
            v.tensor_reduce(up[:, NT:2 * NT], c3, AX.X, ALU.max).then_inc(bounds_ready, 1)
            v.wait_ge(bounds_max, 1)
            lo_f, cnt_f = tmp[:, 20:45], tmp[:, 45:70]
            cnt_i = tmp[:, 70:95].bitcast(I32)
            steps.step(v.tensor_scalar(lo_f, m2[:, 0:NT], -1.0, float(ET), ALU.mult, ALU.add))
            steps.step(v.scalar_tensor_tensor(cnt_i, m2[:, NT:2 * NT], float(U - 1), lo_f, ALU.add, ALU.subtract))
            steps.step(v.tensor_scalar(cnt_i, cnt_i, 2, None, ALU.arith_shift_right))
            steps.step(v.tensor_scalar(cnt_f, cnt_i, float(U), float(U), ALU.mult, ALU.max))
            steps.step(v.tensor_scalar(tmp[:, 95:95 + NT], cnt_f, -1.0, float(ETP), ALU.mult, ALU.add))
            steps.step(v.tensor_tensor(ranges[:, 0, :], lo_f, tmp[:, 95:95 + NT], ALU.min))
            steps.step(v.tensor_copy(ranges[:, 1, :], cnt_f))
            sums = [tmp[:, 430:455], tmp[:, 455:480]]
            steps.step(v.memset(sums[0][:, 0:1], 0.0))
            steps.step(v.tensor_copy(sums[0][:, 1:NT], cnt_f[:, 0:NT - 1]))
            d, cur = 1, 0
            while d < NT:
                steps.step(v.tensor_copy(sums[1 - cur][:, 0:d], sums[cur][:, 0:d]))
                steps.step(v.tensor_tensor(sums[1 - cur][:, d:NT], sums[cur][:, d:NT], sums[cur][:, 0:NT - d],
                                           ALU.add))
                d, cur = 2 * d, 1 - cur
            v.tensor_copy(ranges[:, 2, :], sums[cur]).then_inc(ranges_done, 1)
            v.wait_ge(ranges_done, 1)
            v.memset(src_idx[:, ETP:ETP + U], 0)
            v.scalar_tensor_tensor(rel_idx[:, :], src_idx[:, 0:ETP], float(R), et_i, ALU.mult, ALU.add)
            v.tensor_copy(dst_f[:, :], dst_i).then_inc(relidx_done, 1)
            v.wait_ge(relidx_done, 1)

            v.wait_ge(attw_done, 1)
            for d in range(2):
                for k in range(2):
                    last = v.tensor_copy(wcat[:, k, d * C0 + F:(d + 1) * C0],
                                         bank[5][:, (d * 2 + k) * HEADS:(d * 2 + k + 1) * HEADS])
            last.then_inc(wcat_done, 1)
            v.wait_ge(x_loaded, 16)
            with v.Fori(0, NG) as g:
                steps.enter(g, 3)
                norm_group(g, g, g)
                hold(v, t_stored, (g + 1) * 16)
                hold(v, t_product, g * 2 + 1)
                v.tensor_copy(t0s[:, 0:3, :], bank[3][:, 0:3 * T0W].rearrange("p (j c) -> p j c", c=T0W))\
                    .then_inc(t_staged, 1)
                hold(v, t_product, g * 2 + 2)
                v.tensor_copy(t0s[:, 3:5, :], bank[4][:, 0:2 * T0W].rearrange("p (j c) -> p j c", c=T0W))\
                    .then_inc(t_staged, 1)
            steps.leave(NG)
            v.memset(msg[:, :, F:F + 1], 1.0)
            v.wait_ge(t_stored, (NG + 1) * 16)
            v.memset(rhs0[:, :, S0W - 1:S0W], 1.0)
            v.wait_ge(wcat_done, 1)
            for j in range(U):
                v.tensor_copy(idx4[:, j:j + 1], src_idx[:, j:j + 1]).then_inc(used[2][j], 1)
            with v.Fori(0, GT) as i:
                next4 = src_idx[:, bass.ds(i * U + U, U)]
                m4 = msg[:, bass.ds(i * U, U), :]
                d4 = dir_e[:, bass.ds(i * U, U), :]
                for j in range(U):
                    hold(v, g0_rev, i * U + (j + 1))
                    v.scalar_tensor_tensor(m4[:, j, 0:F], ring[:, j, 0:F], d4[:, j, 0:1], rev[:, j, 0:F],
                                           ALU.mult, ALU.add)
                    v.scalar_tensor_tensor(m4[:, j, F + 1:MW], ring[:, j, F:C0], d4[:, j, 0:1], rev[:, j, F:C0],
                                           ALU.mult, ALU.add)
                    v.tensor_copy(idx4[:, j:j + 1], next4[:, j:j + 1]).then_inc(used[2][j], 1)
            for j in range(U):
                v.wait_ge(used[2][j], GT + 1)
            scores = msg[:, :, F + 1:MW]
            v.tensor_reduce(mx[:, :], scores.rearrange("p t h -> p h t"), AX.X, ALU.max).then_inc(lmax_ready, 1)
            v.wait_ge(lmax_ready, 1)
            steps.step(v.scalar_tensor_tensor(scores, scores, 0.2, scores, ALU.mult, ALU.max))
            v.wait_ge(gmax_ready, 1)
            steps.step(v.scalar_tensor_tensor(glr[:, :], gmx[:, :], 0.2, gmx[:, :], ALU.mult, ALU.max))
            v.tensor_tensor(scores, scores, glr[:, :].unsqueeze(1).broadcast_to([P, GT * U, HEADS]),
                            ALU.subtract).then_inc(exp_in, 1)
            v.wait_ge(exp_out, 1)
            heads = bank[5][:, 0:S0W - 1].rearrange("p (h c) -> p h c", h=HEADS)
            with v.Fori(0, NT) as t:
                steps.enter(t, 2)
                lo, cnt, q0 = walk(v, t)
                nodes = iota_n[:, bass.ds(t * P, P)]
                with v.Fori(0, cnt, U) as r:
                    m4 = msg[:, bass.ds(tile_of(lo, r), U), :]
                    d4 = dst_f[:, bass.ds(tile_of(lo, r), U)]
                    for j in range(U):
                        hold(v, s0_used[j], (q0 + r) // U + 1)
                        v.tensor_scalar(onehot[:, j, :], nodes, d4[:, j:j + 1], None, ALU.is_equal)
                        v.tensor_tensor(rhs0[:, j, 0:S0W - 1].rearrange("p (h c) -> p h c", h=HEADS),
                                        m4[:, j, 0:F + 1].unsqueeze(1).broadcast_to([P, HEADS, F + 1]),
                                        m4[:, j, F + 1:MW].unsqueeze(2).broadcast_to([P, HEADS, F + 1]),
                                        ALU.mult).then_inc(s0_ready, 1)
                hold(v, s0_summed, t + 1)
                v.tensor_scalar(den[:, 0:HEADS], heads[:, :, F], 1e-10, None, ALU.add)
                steps.step(v.tensor_scalar(den[:, HEADS:HEADS + 1], bank[5][:, S0W - 1:S0W], 1.0, None, ALU.add))
                steps.step(v.reciprocal(rden[:, :], den[:, :]))
                v.tensor_copy(rcnt[:, bass.ds(t, 1)], rden[:, HEADS:HEADS + 1])
                xt = x_res[:, bass.ds(t, 1), :].rearrange("p o d -> p (o d)")
                for h in range(HEADS):
                    last = v.scalar_tensor_tensor(xt[:, h * F:(h + 1) * F], heads[:, h, 0:F], rden[:, h:h + 1],
                                                  xt[:, h * F:(h + 1) * F], ALU.mult, ALU.add)
                last.then_inc(s0_read, 1)
            steps.leave(NT)
            v.wait_ge(s0_read, NT + 1)

            v.wait_ge(small0_loaded, small_loads * 16)
            with v.Fori(0, NG) as g:
                steps.enter(g, 18)

                def o_read(e):
                    for pair in range(3):
                        u = (e + 1) * 3 + pair
                        hold(v, f_o, g * 21 + (u + 1))
                        if e >= 0:
                            hold(v, f_oread, g * 21 + (u - 1))
                        js = range(2 * pair, min(2 * pair + 2, G))
                        if e < 0:
                            xs = x_res[:, bass.ds(g * G + js[0], len(js)), :].rearrange("p t d -> p (t d)")
                            last = v.tensor_tensor(xs, bank[4 + u % 2][:, 0:len(js) * D], xs, ALU.add)
                        else:
                            xs = x_res[:, bass.ds(g * G + js[0], len(js)), :]
                            for i, j in enumerate(js):
                                last = v.scalar_tensor_tensor(
                                    xs[:, i, :], bank[4 + u % 2][:, i * D:(i + 1) * D],
                                    wsel[:, 0, j, e:e + 1], xs[:, i, :], ALU.mult, ALU.add)
                        last.then_inc(f_oread, 1)

                def each(x, n):
                    return x.broadcast_to([P, G, n])

                norm_group(g, g + NG, g + NG)
                hold(v, f_logits, g + 1)
                steps.step(v.tensor_tensor(
                    lg[:, :, 0:X0], bank[3][:, 0:G * 8].rearrange("p (j c) -> p j c", c=8)[:, :, 0:X0],
                    rb2[:, :].unsqueeze(1).broadcast_to([P, G, X0]), ALU.add))
                steps.step(v.tensor_reduce(gate[:, :, 2:3].rearrange("p t o -> p (t o)"), lg[:, :, 0:X0],
                                           AX.X, ALU.max))
                v.tensor_tensor(lg[:, :, 0:X0], lg[:, :, 0:X0], each(gate[:, :, 2:3], X0),
                                ALU.subtract).then_inc(f_softin, 1)
                hold(v, f_softout, g + 1)
                steps.step(v.tensor_reduce(gate[:, :, 3:4].rearrange("p t o -> p (t o)"), lg[:, :, 0:X0],
                                           AX.X, ALU.add))
                steps.step(v.reciprocal(gate[:, :, 2:3], gate[:, :, 3:4]))
                steps.step(v.tensor_tensor(pr[:, :, 0:X0], lg[:, :, 0:X0], each(gate[:, :, 2:3], X0), ALU.mult))
                for j in range(G):
                    last = v.max(top[:, j, :], pr[:, j, :])
                steps.step(last)
                v.tensor_tensor(gate[:, :, 0:1], top[:, :, 1:2], top[:, :, 0:1], ALU.subtract).then_inc(f_gap, 1)
                for j in range(G):
                    last = v.max_index(topi[:, j, :], top[:, j, :], pr[:, j, :])
                steps.step(last)
                steps.step(v.tensor_copy(idxf[:, :, :], topi[:, :, 0:2]))
                hold(v, f_gapexp, g + 1)
                steps.step(v.tensor_scalar(gate[:, :, 2:3], gate[:, :, 1:2], 1.0, None, ALU.add))
                steps.step(v.reciprocal(gate[:, :, 2:3], gate[:, :, 2:3]))
                steps.step(v.tensor_tensor(gate[:, :, 3:4], gate[:, :, 1:2], gate[:, :, 2:3], ALU.mult))
                for c in range(2):
                    steps.step(v.tensor_tensor(
                        wsel[:, c], iota_x[:, 0:X0].unsqueeze(1).broadcast_to([P, G, X0]),
                        each(idxf[:, :, c:c + 1], X0), ALU.is_equal))
                    steps.step(v.tensor_tensor(wsel[:, c], wsel[:, c], each(gate[:, :, 2 + c:3 + c], X0), ALU.mult))
                v.tensor_tensor(wsel[:, 0], wsel[:, 0], wsel[:, 1], ALU.add).then_inc(f_w, 1)
                hold(v, f_w, g + 1)
                for e in range(-1, X0):
                    o_read(e)
            steps.leave(NG)
            v.wait_ge(f_oread, NG * 21 + 1)

            lgb = onehot[:, 0:2, :].rearrange("p a b -> p (a b)")

            def rel_groups(l):
                with v.Fori(0, NG) as g:
                    steps.enter(g, (3 if l == 0 else 0) + 2 * G)
                    if l == 0:
                        norm_group(g, g + 2 * NG, g + 2 * NG)
                        hold(v, xn_ready, g + (2 * NG + 1))
                    else:
                        hold(v, turned, g + (3 * NG + 1))
                        v.tensor_copy(xn5[:, :, :], h_res[:, bass.ds(g * G, G), :]).then_inc(xn_ready, 1)
                        hold(v, xn_ready, g + (3 * NG + 1))
                    for j in range(G):
                        hold(v, r_rootx[l], g * G + (j + 1))
                        steps.step(v.tensor_tensor(lgb, bank[3][:, 0:D], xn5[:, j, :], ALU.add))
                        steps.step(v.tensor_tensor(lgb, lgb, rows_bc[:, l, 0, :], ALU.add))
                        for c in range(4):
                            hold(v, r_odd[l], g * (4 * G) + (j * 4 + c + 1))
                            hold(v, r_stored[l][c], g * (16 * G) + (j + 1) * 16)
                            b = bank[5 + 2 * (c % 2)]
                            if c == 3:
                                v.scalar_tensor_tensor(
                                    base[:, bass.ds(g * G + j, 1), :].rearrange("p o d -> p (o d)"), b[:, D:2 * D],
                                    rcnt[:, bass.ds(g * G + j, 1)], lgb, ALU.mult, ALU.add).then_inc(r_based[l], 1)
                            v.tensor_copy(stage[:, c * 1024 + 512:(c + 1) * 1024], b[:, :]).then_inc(r_oddout[l], 1)
                steps.leave(NG)
                v.wait_ge(r_based[l], NT + 1)


            def edge_sums(l):
                y, z = xn5[:, 0, :], xn5[:, 1, :]
                with v.Fori(0, NT) as t:
                    steps.enter(t, 6)
                    lo, cnt, q0 = walk(v, t)
                    nodes = iota_n[:, bass.ds(t * P, P)]
                    with v.Fori(0, cnt, U) as r:
                        d4 = dst_f[:, bass.ds(tile_of(lo, r), U)]
                        e4 = ea[:, bass.ds(tile_of(lo, r), U)]
                        i4 = rel_idx[:, bass.ds(tile_of(lo, r), U)]
                        for j in range(U):
                            hold(v, used[l][j], (q0 + r) // U + 1)
                            v.tensor_scalar(onehot[:, j, :], nodes, d4[:, j:j + 1], e4[:, j:j + 1],
                                            ALU.is_equal, ALU.mult)
                            v.tensor_copy(idx4[:, j:j + 1], i4[:, j:j + 1]).then_inc(e_ready[l], 1)
                    hold(v, e_summed[l], t + 1)
                    v.scalar_tensor_tensor(y, bank[0][:, 0:D], rcnt[:, bass.ds(t, 1)],
                                           base[:, bass.ds(t, 1), :].rearrange("p o d -> p (o d)"),
                                           ALU.mult, ALU.add).then_inc(e_read[l], 1)
                    hold(v, e_read[l], t + 2)
                    steps.step(v.bn_stats(stats[:, 0, :], y))
                    steps.step(v.bn_aggr(mv[:, 0, :], stats[:, 0, :]))
                    v.tensor_scalar(veps[:, 0:1], mv[:, 0, 1:2], EPS, None, ALU.add).then_inc(e_var[l], 1)
                    hold(v, e_std[l], t + 1)
                    steps.step(v.reciprocal(rstd[:, 0:1], std[:, 0:1]))
                    steps.step(v.tensor_scalar(z, y, mv[:, 0, 0:1], rstd[:, 0:1], ALU.subtract, ALU.mult))
                    steps.step(v.tensor_tensor(z, z, rows_bc[:, l, 1, :], ALU.mult))
                    steps.step(v.tensor_tensor(z, z, rows_bc[:, l, 2, :], ALU.add))
                    if l == 0:
                        v.tensor_scalar(h_res[:, bass.ds(t, 1), :].rearrange("p o d -> p (o d)"), z, 0.0, None,
                                        ALU.max).then_inc(e_posted[l], 1)
                    else:
                        xt = x_res[:, bass.ds(t, 1), :].rearrange("p o d -> p (o d)")
                        v.scalar_tensor_tensor(xt, z, 0.0, xt, ALU.max, ALU.add).then_inc(e_posted[l], 1)
                steps.leave(NT)
                v.wait_ge(e_posted[l], NT)

            for l in range(2):
                if l == 0:
                    v.wait_ge(rows_loaded, 8 * 16)
                rel_groups(l)
                edge_sums(l)
            v.wait_ge(ffn1_loaded, 7 * 16)
            with v.Fori(0, NG) as g:
                steps.enter(g, 7)
                norm_group(g, g + 4 * NG, g + 3 * NG)
                hold(v, x_logits, g + 1)
                steps.step(v.tensor_tensor(lg[:, :, :], bank[7][:, 0:G * X1].rearrange("p (j c) -> p j c", c=X1),
                                           rb.unsqueeze(1).broadcast_to([P, G, X1]), ALU.add))
                for j in range(G):
                    last = v.max(top[:, j, :], lg[:, j, :])
                steps.step(last)
                for j in range(G):
                    last = v.max_index(topi[:, j, :], top[:, j, :], lg[:, j, :])
                steps.step(last)
                steps.step(v.tensor_copy(idxf[:, :, 0:1], topi[:, :, 0:1]))
                v.tensor_tensor(oh[:, :, :], iota_x[:, :].unsqueeze(1).broadcast_to([P, G, X1]),
                                idxf[:, :, 0:1].broadcast_to([P, G, X1]), ALU.is_equal).then_inc(x_oh, 1)
                hold(v, x_stored, (g + 1) * 16)
                for pair in range(3):
                    hold(v, x_o, g * 3 + (pair + 1))
                    n = min(2, G - 2 * pair)
                    v.scalar_tensor_tensor(
                        outs[:, 2 * pair:2 * pair + n, :].rearrange("p t d -> p (t d)"),
                        bank[3 + 4 * (pair % 2)][:, 0:n * D], 0.0,
                        x_res[:, bass.ds(g * G + 2 * pair, n), :].rearrange("p t d -> p (t d)"),
                        ALU.max, ALU.add).then_inc(x_oread, 1)
            steps.leave(NG)


def kernel(**inputs):
    import ml_dtypes
    import numpy as np
    import concourse.bacc as bacc
    from concourse.bass_utils import run_bass_kernel_spmd as run

    v = {k: np.asarray(x) for k, x in inputs.items()}

    def tiles(x, mode, **kw):
        pad = [(0, ETP * P - E)] + [(0, 0)] * (x.ndim - 1)
        x = np.pad(x, pad, mode=mode, **kw).reshape((ETP, P) + x.shape[1:])
        return np.ascontiguousarray(np.moveaxis(x, 0, 1))

    def cols(x):
        x = x.reshape(x.shape[:-1] + (x.shape[-1] // P, P))
        return np.ascontiguousarray(np.moveaxis(x, -1, 0))

    far = np.full((X1, X1, H1), FAR, np.float32)
    far[np.arange(X1), np.arange(X1)] = 0
    dst_rows = np.pad(v["dst"], (0, 4 * P * P - E), constant_values=NOWHERE)
    arrays = {
        "x": np.pad(v["x"], ((0, NT * P - N), (0, 0))),
        "dst_rows": np.ascontiguousarray(dst_rows.reshape(4, P, P).transpose(1, 0, 2)),
        "dst_t": tiles(v["dst"], "constant", constant_values=NOWHERE),
        "src_t": tiles(v["src"], "edge"),
        "et_t": tiles(v["edge_type_16"], "edge"),
        "ea_t": tiles(v["edge_weight"], "constant"),
        "dir_t": tiles(v["edge_attr_2"], "edge"),
        "wf": v["L0_gnn_W_forward"], "wf_T": np.ascontiguousarray(v["L0_gnn_W_forward"].T),
        "wr": v["L0_gnn_W_reverse"], "wr_T": np.ascontiguousarray(v["L0_gnn_W_reverse"].T),
        "attn_T": np.ascontiguousarray(v["L0_gnn_attn_forward"][0].T),
        "ident": np.eye(P, dtype=np.float32),
        "rw1": v["L0_ffn_router_w1"], "rb1": v["L0_ffn_router_b1"],
        "rw2": v["L0_ffn_router_w2"], "rb2": v["L0_ffn_router_b2"],
        "ew1": v["L0_ffn_expert_w1"], "ew2": v["L0_ffn_expert_w2"], "ew3": v["L0_ffn_expert_w3"],
        "eb1T": cols(v["L0_ffn_expert_b1"]), "eb2T": cols(v["L0_ffn_expert_b2"]), "eb3": v["L0_ffn_expert_b3"],
        "xw1": np.ascontiguousarray(v["L1_ffn_W1"].transpose(1, 0, 2).reshape(D, X1 * H1)),
        "xb1T": cols(v["L1_ffn_b1"].reshape(X1 * H1)),
        "xw2": v["L1_ffn_W2"].reshape(X1 * H1, D), "xb2": v["L1_ffn_b2"],
        "rwT": np.ascontiguousarray(v["L1_ffn_router_w"].T), "rb": v["L1_ffn_router_b"],
        "negmask": far.reshape(X1, X1 * H1).astype(ml_dtypes.bfloat16),
    }
    for l in range(2):
        arrays[f"basis{l}"] = v[f"L1_gnn_basis{l + 1}"]
        arrays[f"att{l}"] = v[f"L1_gnn_att{l + 1}"].reshape(R * B)
        arrays[f"root{l}"] = v[f"L1_gnn_root{l + 1}"]
        arrays[f"bias{l}"] = v[f"L1_gnn_bias{l + 1}"]
        arrays[f"ln_g{l}"] = v[f"L1_gnn_ln{l + 1}_g"]
        arrays[f"ln_b{l}"] = v[f"L1_gnn_ln{l + 1}_b"]

    nc = bacc.Bacc("TRN2", target_bir_lowering=False, num_devices=1)
    arrays = {f"in_{k}": np.ascontiguousarray(x) for k, x in arrays.items()}
    aps = {k[3:]: nc.dram_tensor(k, x.shape, mybir.dt.from_np(x.dtype), kind="ExternalInput").ap()
           for k, x in arrays.items()}
    out = nc.dram_tensor("out", (NT * P, D), F32, kind="ExternalOutput").ap()
    build(nc, aps, out)
    r = run(nc, [arrays], core_ids=[0])
    return r.results[0]["out"][:N]
```

```python
from contextlib import ExitStack

import concourse.bass as bass
from concourse import mybir

ALU = mybir.AluOpType
ACT = mybir.ActivationFunctionType
AX = mybir.AxisListType
F32 = mybir.dt.float32
BF16 = mybir.dt.bfloat16
I32 = mybir.dt.int32
U32 = mybir.dt.uint32
I16 = mybir.dt.int16

P = 128
N = 3125
NT = 25
G = 5
NG = NT // G
GN = G * P
HB = GN // 2
D = 256
E = 50000
ET = (E + P - 1) // P
U = 6
UH = U // 2
U_MIN = 2
GT = (ET + U - 1) // U
ETP = GT * U
NOWHERE = 4096
HEADS = 4
F = 64
C0 = F + HEADS
T0W = 2 * C0
MW = F + 1 + HEADS
S0W = HEADS * (F + 1) + 1
R = 16
B = 8
X0 = 6
X1 = 32
H1 = 64
M1 = X1 * H1 // P
EPS = 1e-5
FAR = -1.7e38


class Steps:

    def __init__(self, eng, sem):
        self.eng, self.sem = eng, sem
        self.before, self.n, self.turn, self.per_turn = 0, 0, None, 0

    def enter(self, turn, per_turn):
        self.before += self.n
        self.turn, self.per_turn, self.n = turn, per_turn, 0

    def leave(self, turns):
        assert self.n == self.per_turn, f"steps a turn: {self.n}"
        self.before += turns * self.per_turn
        self.turn, self.n = None, 0

    def step(self, ins):
        ins.then_inc(self.sem, 1)
        self.n += 1
        if self.turn is None:
            self.eng.wait_ge(self.sem, self.before + self.n)
        else:
            self.eng.wait_ge(self.sem, self.turn * self.per_turn + (self.before + self.n))
            self.eng.nop(nofuse=True)


def hold(eng, sem, value):
    eng.wait_ge(sem, value)
    eng.nop(nofuse=True)


def build(nc, a, out):
    ctx = ExitStack()
    with ctx:
        def sb(name, shape, dt=F32):
            return ctx.enter_context(nc.sbuf_tensor(name, shape, dt))

        def sem(name):
            return ctx.enter_context(nc.semaphore(name))

        gat_table = nc.dram_tensor("gat_table", (NT * P, T0W), F32, kind="Internal").ap()
        rel_table = [nc.dram_tensor(f"rel_table{l}", (NT * P * R, D), F32, kind="Internal").ap()
                     for l in range(2)]

        x_res = sb("x_res", [P, NT, D])
        region_a = sb("region_a", [P, 9216])
        region_b = sb("region_b", [P, 4096])
        region_m = sb("region_m", [P, GT * U * MW])
        iota_n = sb("iota_n", [P, NT * P], I16)
        src_idx = sb("src_idx", [P, ETP + U], I32)
        dst_f = sb("dst_f", [P, ETP])
        idx = sb("idx", [P, U], I32)
        gat_ring = sb("gat_ring", [P, U, T0W])
        onehot = sb("onehot", [P, U, P])
        ident = sb("ident", [P, P])
        rb1 = sb("rb1", [P, 1])
        rw2 = sb("rw2", [P, X0])
        rb2 = sb("rb2", [P, X0])
        eb1 = sb("eb1", [P, X0, 2])
        eb2 = sb("eb2", [P, X0, 2])
        eb3 = sb("eb3", [X0, D])
        stats = sb("stats", [P, G, 6])
        mv = sb("mv", [P, G, 2])
        veps = sb("veps", [P, G])
        std = sb("std", [P, G])
        rstd = sb("rstd", [P, G])
        rcnt = sb("rcnt", [P, NT])
        mx = sb("mx", [P, HEADS])
        gmx = sb("gmx", [P, HEADS])
        glr = sb("glr", [P, HEADS])
        den = sb("den", [P, HEADS + 1])
        rden = sb("rden", [P, HEADS + 1])
        ranges = sb("ranges", [P, 3, NT], I32)
        zeros = sb("zeros", [P, S0W], BF16)
        att_bc = sb("att_bc", [P, 2, R * B])
        att_cur = sb("att_cur", [P, B])
        lg = sb("lg", [P, G, X1])
        pr = sb("pr", [P, G, 8])
        top = sb("top", [P, G, 8])
        topi = sb("topi", [P, G, 8], U32)
        idxf = sb("idxf", [P, G, 2])
        gate = sb("gate", [P, G, 4])
        wsel = sb("wsel", [P, 2, G, X0])
        oh = sb("oh", [P, G, X1])
        iota_x = sb("iota_x", [P, X1])
        tile_no = sb("tile_no", [P, 4])

        ew = [[region_a[:, (e * 3 + w) * 512:(e * 3 + w + 1) * 512].rearrange("p (k n) -> p k n", k=2)
               for w in range(3)] for e in range(X0)]
        h_res = region_a[:, 0:NT * D].rearrange("p (t d) -> p t d", d=D)
        rows_bc = region_a[:, 6656:6656 + 6 * D].rearrange("p (l c d) -> p l c d", l=2, c=3)
        root = region_a[:, 8192:8192 + 4 * D].rearrange("p (l k d) -> p l k d", l=2, k=2)
        negmask = region_a[0:X1, 0:1024].bitcast(BF16)
        ohT = region_a[0:X1, 1024:1024 + GN]
        ohTb = region_a[0:X1, 1664:1664 + GN // 2].bitcast(BF16)
        xb2 = region_a[0:X1, 2048:2048 + D]
        rwT = region_a[:, 2304:2304 + 2 * X1].rearrange("p (k n) -> p k n", k=2)
        rb = region_a[:, 2368:2368 + X1]
        xb1 = region_a[:, 2400:2400 + M1]
        outs = region_a[:, 2432:2432 + G * D].rearrange("p (t d) -> p t d", d=D)
        dir_e = region_b[:, 0:2 * ETP].rearrange("p (t c) -> p t c", c=2)
        rev = region_b[:, 800:800 + U * C0].rearrange("p (j c) -> p j c", c=C0)
        rhs0 = region_b[:, 1208:1208 + U * (S0W + 1)].rearrange("p (j c) -> p j c", c=S0W + 1)
        t0s = region_b[:, 1208:1208 + G * T0W].rearrange("p (j c) -> p j c", c=T0W)
        dstT = region_b[:, 1888:1888 + 512].bitcast(I32).rearrange("p (j c) -> p j c", c=P)
        et_i = region_b[:, 2784:2784 + ETP].bitcast(I32)
        dst_i = region_b[:, 3180:3180 + ETP].bitcast(I32)
        sums0 = region_b[:, 3576:3576 + S0W]
        wcat = region_b[:, 3576:3576 + 2 * T0W].rearrange("p (k c) -> p k c", k=2)
        basis = [x.rearrange("p (b k n) -> p b k n", b=B, k=2) for x in (region_b[:, :], region_a[:, 0:4096])]
        stage = region_b
        msg = region_m[:, :].rearrange("p (t c) -> p t c", c=MW)
        wrel = [region_m[:, l * 8192:(l + 1) * 8192].rearrange("p (k n) -> p k n", k=2) for l in range(2)]
        at = 16384
        base = region_m[:, at:at + NT * D].rearrange("p (t d) -> p t d", d=D)
        h1T = region_m[:, at:at + 2560].rearrange("p (s m n) -> p s m n", s=2, m=2)
        h2T = region_m[:, at + 2560:at + 5120].rearrange("p (s m n) -> p s m n", s=2, m=2)
        wacc = [x.rearrange("p (s k n) -> p s k n", s=2, k=2)
                for x in (region_m[:, at + 5120:at + 6144], region_a[:, 4096:5120])]
        at += NT * D
        xn5 = region_m[:, at:at + G * D].rearrange("p (t d) -> p t d", d=D)
        at += G * D
        mean = xn5[:, 0, :]
        xT5 = region_m[:, at:at + 2 * GN].rearrange("p (k n) -> p k n", k=2)
        at += 2 * GN
        rhT = region_m[:, at:at + GN]
        wT = region_m[0:X0, at + GN:at + 2 * GN]
        rw1 = region_m[:, at + 2 * GN:at + 2 * GN + 2 * P].rearrange("p (k n) -> p k n", k=2)
        rel_ring = region_m[:, at:at + U * D].rearrange("p (j d) -> p j d", j=U)
        at += U * D
        ea = region_m[:, at:at + ETP]
        assert at + ETP <= GT * U * MW
        xw1 = region_m[:, 0:4096].rearrange("p (k n) -> p k n", k=2)
        xw2 = region_m[:, 4096:8192].rearrange("p (m n) -> p m n", m=M1)
        hmT = region_m[:, 8192:8192 + M1 * GN].rearrange("p (m n) -> p m n", m=M1)

        bank = [ctx.enter_context(nc.psum_tensor(f"bank{i}", [P, 512], F32)) for i in range(8)]

        meta_loaded, x_loaded, gatw_loaded, ident_loaded = map(sem, (
            "meta_loaded", "x_loaded", "gatw_loaded", "ident_loaded"))
        ffn0_loaded, small0_loaded, basis_loaded, rows_loaded, ffn1_loaded = map(sem, (
            "ffn0_loaded", "small0_loaded", "basis_loaded", "rows_loaded", "ffn1_loaded"))
        consts_done, bounds_ready, bounds_max, ranges_done, dst_done = map(sem, (
            "consts_done", "bounds_ready", "bounds_max", "ranges_done", "dst_done"))
        attw_done, wcat_done = map(sem, ("attw_done", "wcat_done"))
        var_ready, std_ready, xn_ready, turned, xT_ready = map(sem, (
            "var_ready", "std_ready", "xn_ready", "turned", "xT_ready"))
        t_product, t_staged, t_stored = map(sem, ("t_product", "t_staged", "t_stored"))
        g0_rev, lmax_ready, gmax_ready, exp_in, exp_out = map(sem, (
            "g0_rev", "lmax_ready", "gmax_ready", "exp_in", "exp_out"))
        s0_ready, s0_weighted, s0_summed, s0_read, s0_posted = map(sem, (
            "s0_ready", "s0_weighted", "s0_summed", "s0_read", "s0_posted"))
        s0_used = [sem(f"s0_used{h}") for h in range(2)]
        f_rh, f_rhT, f_logits, f_softin, f_softout, f_gap, f_gapexp, f_w, f_wturned, f_wT = map(sem, (
            "f_rh", "f_rhT", "f_logits", "f_softin", "f_softout", "f_gap", "f_gapexp", "f_w", "f_wturned", "f_wT"))
        f_h1, f_h1T, f_h2, f_h2T, f_o, f_oread = map(sem, ("f_h1", "f_h1T", "f_h2", "f_h2T", "f_o", "f_oread"))
        wrel_done = sem("wrel_done")
        rw1_loaded = sem("rw1_loaded")
        r_rootx, r_based, r_even, r_odd, r_evenout, r_oddout = [
            [sem(f"{n}{l}") for l in range(2)] for n in (
                "r_rootx", "r_based", "r_even", "r_odd", "r_evenout", "r_oddout")]
        r_stored = [[sem(f"r_stored{l}_{c}") for c in range(4)] for l in range(2)]
        e_index, e_ready, e_summed, e_read, e_var, e_std, e_posted = [
            [sem(f"{n}{l}") for l in range(2)] for n in (
                "e_index", "e_ready", "e_summed", "e_read", "e_var", "e_std", "e_posted")]
        got = [[sem(f"got{l}_{j}") for j in range(U)] for l in range(3)]
        used = [[sem(f"used{l}_{j}") for j in range(U)] for l in range(3)]
        x_logits, x_oh, x_ohturned, x_ohT, x_h, x_hT, x_o, x_oread, x_stored = map(sem, (
            "x_logits", "x_oh", "x_ohturned", "x_ohT", "x_h", "x_hT", "x_o", "x_oread", "x_stored"))
        dve_step, pool_step = map(sem, ("dve_step", "pool_step"))

        x_d = a["x"].rearrange("(t p) d -> p t d", p=P)
        gat_rows = gat_table.rearrange("(t p) c -> p t c", p=P)
        rel_rows = [rel_table[l].rearrange("(t p r) d -> p t (r d)", p=P, r=R) for l in range(2)]
        out_rows = out.rearrange("(t p) d -> p t d", p=P)
        small_loads = 6 + 2 * X0

        def walk(eng, t):
            return (eng.value_load(ranges[0:1, 0, bass.ds(t, 1)], min_val=0, max_val=ETP - U_MIN * U),
                    eng.value_load(ranges[0:1, 1, bass.ds(t, 1)], min_val=U_MIN, max_val=GT),
                    eng.value_load(ranges[0:1, 2, bass.ds(t, 1)], min_val=0, max_val=NT * GT))

        def tile_of(lo, r):
            return nc.s_assert_within(lo + r * U, 0, ETP - U)

        def weigh(eng, lo, h):
            js = slice(h * UH, (h + 1) * UH)
            msgs = msg[:, bass.ds(lo, U), :]
            return eng.tensor_tensor(rhs0[:, js, 0:S0W - 1].rearrange("p j (h c) -> p j h c", h=HEADS),
                                     msgs[:, js, 0:F + 1].unsqueeze(2).broadcast_to([P, UH, HEADS, F + 1]),
                                     msgs[:, js, F + 1:MW].unsqueeze(3).broadcast_to([P, UH, HEADS, F + 1]),
                                     ALU.mult)

        block = ctx.enter_context(nc.Block())

        @block.sync
        def _(sp):
            def load(dst, src, done):
                sp.dma_start(dst, src).then_inc(done, 16)

            sp.nop().then_inc(t_stored, 16)
            for l in range(2):
                for c in range(4):
                    sp.nop().then_inc(r_stored[l][c], 16)
            sp.nop().then_inc(x_stored, 16)

            load(dstT, a["dst_rows"], meta_loaded)
            load(dst_i, a["dst_t"], meta_loaded)
            load(src_idx[:, 0:ETP], a["src_t"], meta_loaded)
            load(et_i, a["et_t"], meta_loaded)
            load(dir_e, a["dir_t"], meta_loaded)
            load(x_res[:, :, :], x_d, x_loaded)
            load(wcat[:, :, 0:F], a["wf_T"].rearrange("(k p) f -> p k f", p=P), gatw_loaded)
            load(wcat[:, :, C0:C0 + F], a["wr_T"].rearrange("(k p) f -> p k f", p=P), gatw_loaded)
            load(onehot[0:F, 0:2, :], a["wf"].rearrange("f (k n) -> f k n", k=2), gatw_loaded)
            load(onehot[0:F, 2:4, :], a["wr"].rearrange("f (k n) -> f k n", k=2), gatw_loaded)
            load(gat_ring[0:F, 0, 0:HEADS], a["attn_T"], gatw_loaded)
            load(ident[:, :], a["ident"], ident_loaded)
            for e in range(X0):
                for w, name in enumerate(("ew1", "ew2", "ew3")):
                    load(ew[e][w], a[name][e].rearrange("(k p) n -> p k n", p=P), ffn0_loaded)
            load(rb1[:, :], a["rb1"].rearrange("(p o) -> p o", o=1), small0_loaded)
            load(rw2[:, :], a["rw2"], small0_loaded)
            load(rb2[:, :], a["rb2"].partition_broadcast(P), small0_loaded)
            for e in range(X0):
                load(eb1[:, e, :], a["eb1T"][:, e, :], small0_loaded)
                load(eb2[:, e, :], a["eb2T"][:, e, :], small0_loaded)
            load(eb3[:, :], a["eb3"], small0_loaded)
            for l in range(2):
                load(att_bc[:, l, :], a[f"att{l}"].partition_broadcast(P), small0_loaded)

            with sp.Fori(0, NG) as g:
                sp.wait_ge(t_staged, g * 2 + 3)
                sp.dma_start(gat_rows[:, bass.ds(g * G, G), :], t0s).then_inc(t_stored, 16)
            sp.wait_ge(s0_posted, NT + 1)
            load(basis[0], a["basis0"].rearrange("b (k p) n -> p b k n", p=P), basis_loaded)
            load(rw1, a["rw1"].rearrange("(k p) n -> p k n", p=P), rw1_loaded)
            sp.wait_ge(f_oread, NG * 21 + 1)
            load(ea, a["ea_t"], rows_loaded)
            load(basis[1], a["basis1"].rearrange("b (k p) n -> p b k n", p=P), basis_loaded)
            for l in range(2):
                for c, name in enumerate(("bias", "ln_g", "ln_b")):
                    load(rows_bc[:, l, c, :], a[f"{name}{l}"].partition_broadcast(P), rows_loaded)
                load(root[:, l, :, :], a[f"root{l}"].rearrange("(k p) n -> p k n", p=P), rows_loaded)

            def store_rel(l):
                with sp.Fori(0, NT) as t:
                    for c in range(4):
                        sp.wait_ge(r_evenout[l], t * 4 + (c + 3))
                        sp.wait_ge(r_oddout[l], t * 4 + (c + 3))
                        sp.dma_start(rel_rows[l][:, bass.ds(t, 1), c * 1024:(c + 1) * 1024],
                                     stage[:, c * 1024:(c + 1) * 1024].unsqueeze(1)).then_inc(r_stored[l][c], 16)

            store_rel(0)
            store_rel(1)
            sp.wait_ge(r_based[1], NT + 1)
            load(xw1, a["xw1"].rearrange("(k p) n -> p k n", p=P), ffn1_loaded)
            load(xw2, a["xw2"].rearrange("(m p) n -> p m n", p=P), ffn1_loaded)
            load(negmask, a["negmask"], ffn1_loaded)
            load(xb2, a["xb2"], ffn1_loaded)
            load(rwT, a["rwT"].rearrange("(k p) n -> p k n", p=P), ffn1_loaded)
            load(rb, a["rb"].partition_broadcast(P), ffn1_loaded)
            load(xb1, a["xb1T"], ffn1_loaded)
            with sp.Fori(0, NG) as g:
                sp.wait_ge(x_oread, g * 3 + 4)
                sp.dma_start(out_rows[:, bass.ds(g * G, G), :], outs).then_inc(x_stored, 16)
            sp.wait_ge(x_stored, 16 * (NG + 1))

        @block.gpsimd
        def _(pool):
            pool.iota(iota_n[:, :], pattern=[[1, NT * P]], base=0, channel_multiplier=0).then_inc(consts_done, 1)
            pool.iota(iota_x[:, :], pattern=[[1, X1]], base=0, channel_multiplier=0,
                      allow_small_or_imprecise_dtypes=True).then_inc(consts_done, 1)
            pool.iota(tile_no[:, :], pattern=[[P, 4]], base=0, channel_multiplier=1,
                      allow_small_or_imprecise_dtypes=True).then_inc(consts_done, 1)
            pool.memset(zeros[:, :], 0.0).then_inc(consts_done, 1)
            pool.memset(pr[:, :, :], -1.0).then_inc(consts_done, 1)
            pool.wait_ge(bounds_ready, 1)
            pool.partition_all_reduce(xT5[:, 0, 0:2 * NT], xT5[:, 1, 0:2 * NT], P,
                                      bass.bass_isa.ReduceOp.max).then_inc(bounds_max, 1)

            def gather(l, j, table):
                pool.indirect_dma_start(
                    out=(gat_ring if l == 2 else rel_ring)[:, j, :], out_offset=None, in_=table,
                    in_offset=bass.IndirectOffsetOnAxis(ap=idx[:, j:j + 1], axis=0)).then_inc(got[l][j], 16)

            pool.wait_ge(meta_loaded, 5 * 16)
            pool.wait_ge(t_stored, 16 * (NG + 1))
            with pool.Fori(0, GT) as i:
                for j in range(U):
                    hold(pool, used[2][j], i + 1)
                    gather(2, j, gat_table)
            pool.wait_ge(lmax_ready, 1)
            pool.partition_all_reduce(gmx[:, :], mx[:, :], P, bass.bass_isa.ReduceOp.max).then_inc(gmax_ready, 1)

            pool.wait_ge(exp_out, 1)
            pool.wait_ge(ranges_done, 1)
            with pool.Fori(0, NT) as t:
                lo, cnt, q0 = walk(pool, t)
                with pool.Fori(0, cnt) as r:
                    hold(pool, s0_used[1], q0 + r + 1)
                    weigh(pool, tile_of(lo, r), 1).then_inc(s0_weighted, 1)

            pool.wait_ge(small0_loaded, small_loads * 16)
            steps = Steps(pool, pool_step)
            for l in range(2):
                pool.wait_ge(basis_loaded, 16 * (l + 1))
                with pool.Fori(0, R) as r:
                    steps.enter(r, 2 * B - 1)
                    steps.step(pool.tensor_copy(att_cur[:, :], att_bc[:, l, bass.ds(r * B, B)]))
                    def product(o, b):
                        return pool.tensor_tensor(o, basis[l][:, b], att_cur[:, b:b + 1].unsqueeze(1)
                                                  .broadcast_to([P, 2, D]), ALU.mult)
                    steps.step(product(wacc[l][:, 0], 0))
                    for b in range(1, B):
                        steps.step(product(wacc[l][:, 1], b))
                        if b < B - 1:
                            steps.step(pool.tensor_tensor(wacc[l][:, 0], wacc[l][:, 0], wacc[l][:, 1], ALU.add))
                        else:
                            pool.tensor_tensor(wrel[l][:, :, bass.ds(r * D, D)], wacc[l][:, 0], wacc[l][:, 1],
                                               ALU.add).then_inc(wrel_done, 1)
                            hold(pool, wrel_done, r + (l * R + 1))
                steps.leave(R)

            for l in range(2):
                for c in range(4):
                    pool.wait_ge(r_stored[l][c], 16 * (NT + 1))
                pool.wait_ge(ranges_done, 1)
                with pool.Fori(0, NT) as t:
                    lo, cnt, q0 = walk(pool, t)
                    with pool.Fori(0, cnt) as r:
                        for j in range(U):
                            hold(pool, e_index[l], (q0 + r) * U + (j + 1))
                            hold(pool, used[l][j], q0 + r + 1)
                            gather(l, j, rel_table[l])

        @block.scalar
        def _(act):
            for l in range(2):
                for j in range(U):
                    act.nop().then_inc(used[l][j], 1)
            for h in range(2):
                act.nop().then_inc(s0_used[h], 1)
            for l in range(2):
                act.nop().then_inc(r_evenout[l], 2)

            def std_group(k):
                hold(act, var_ready, k + 1)
                act.activation(std[:, :], veps[:, :], ACT.Sqrt).then_inc(std_ready, 1)

            def copy_turned(k):
                hold(act, turned, k + 2)
                act.activation(xT5[:, 0, 0:512], bank[0][:, :], ACT.Copy)
                act.activation(xT5[:, 1, 0:512], bank[2][:, :], ACT.Copy)
                act.activation(xT5[:, :, 512:GN], bank[1][:, 0:256].rearrange("p (k n) -> p k n", k=2),
                               ACT.Copy).then_inc(xT_ready, 1)

            with act.Fori(0, NG) as g:
                std_group(g)
                copy_turned(g)
            act.wait_ge(meta_loaded, 5 * 16)
            with act.Fori(0, GT) as i:
                dd = dir_e[:, bass.ds(i * U, U), :]
                for j in range(U):
                    hold(act, got[2][j], (i + 1) * 16)
                    act.activation(rev[:, j, :], gat_ring[:, j, C0:T0W], ACT.Copy,
                                   scale=dd[:, j, 1:2]).then_inc(g0_rev, 1)
            act.wait_ge(exp_in, 1)
            act.activation(msg[:, :, F + 1:MW], msg[:, :, F + 1:MW], ACT.Exp).then_inc(exp_out, 1)
            with act.Fori(0, NT) as t:
                hold(act, s0_summed, t + 1)
                hold(act, s0_posted, t + 1)
                act.activation(sums0, bank[5][:, 0:S0W], ACT.Copy).then_inc(s0_read, 1)

            act.wait_ge(small0_loaded, small_loads * 16)
            std_group(NG)
            copy_turned(NG)
            with act.Fori(0, NG) as g:
                def h1_out(e):
                    for m in range(2):
                        for nb in range(2):
                            hold(act, f_h1, g * (X0 * 4) + (e * 4 + m * 2 + nb + 1))
                            act.activation(h1T[:, e % 2, m, nb * HB:(nb + 1) * HB], bank[nb][:, 0:HB],
                                           ACT.Relu, bias=eb1[:, e, m:m + 1]).then_inc(f_h1T, 1)

                def h2_out(e):
                    for m in range(2):
                        for nb in range(2):
                            hold(act, f_h2, g * (X0 * 4) + (e * 4 + m * 2 + nb + 1))
                            act.activation(h2T[:, e % 2, m, nb * HB:(nb + 1) * HB], bank[2 + nb][:, 0:HB],
                                           ACT.Relu, bias=eb2[:, e, m:m + 1]).then_inc(f_h2T, 1)

                for nb in range(2):
                    hold(act, f_rh, g * 2 + (nb + 1))
                    act.activation(rhT[:, nb * HB:(nb + 1) * HB], bank[6 + nb][:, 0:HB], ACT.Relu,
                                   bias=rb1[:, 0:1]).then_inc(f_rhT, 1)
                h1_out(0)
                hold(act, f_softin, g + 1)
                act.activation(lg[:, :, 0:X0], lg[:, :, 0:X0], ACT.Exp).then_inc(f_softout, 1)
                h1_out(1)
                hold(act, f_gap, g + 1)
                act.activation(gate[:, :, 1:2], gate[:, :, 0:1], ACT.Exp).then_inc(f_gapexp, 1)
                h2_out(0)
                hold(act, f_wturned, g + 1)
                act.activation(wT[:, 0:512], bank[6][0:X0, :], ACT.Copy)
                act.activation(wT[:, 512:GN], bank[7][0:X0, 0:P], ACT.Copy).then_inc(f_wT, 1)
                for e in range(2, X0):
                    h1_out(e)
                    h2_out(e - 1)
                std_group(g + (NG + 1))
                h2_out(X0 - 1)
                copy_turned(g + (NG + 1))

            def rel_groups(l):
                with act.Fori(0, NG) as g:
                    if l == 1:
                        copy_turned(g + (3 * NG + 1))
                    for j in range(G):
                        for c in range(4):
                            hold(act, r_even[l], g * (4 * G) + (j * 4 + c + 1))
                            hold(act, r_stored[l][c], g * (16 * G) + (j + 1) * 16)
                            act.activation(stage[:, c * 1024:c * 1024 + 512], bank[4 + 2 * (c % 2)][:, :],
                                           ACT.Copy).then_inc(r_evenout[l], 1)
                    if l == 0:
                        std_group(g + (2 * NG + 1))
                        copy_turned(g + (2 * NG + 1))

            def edge_indices(l):
                def turn(lo, q=None):
                    idxs = src_idx[:, bass.ds(lo, U)]
                    for j in range(U):
                        if q is not None:
                            hold(act, got[l][j], q * 16)
                        act.activation(idx[:, j:j + 1], idxs[:, j:j + 1], ACT.Copy).then_inc(e_index[l], 1)

                def read_out(t):
                    hold(act, e_summed[l], t + 1)
                    hold(act, e_var[l], t + 1)
                    act.activation(mean, bank[0][:, 0:D], ACT.Copy,
                                   scale=rcnt[:, bass.ds(t, 1)]).then_inc(e_read[l], 1)

                def root_of_var(t):
                    hold(act, e_var[l], t + 2)
                    act.activation(std[:, 0:1], veps[:, 0:1], ACT.Sqrt).then_inc(e_std[l], 1)

                lo, cnt, _ = walk(act, 0)
                turn(lo)
                with act.Fori(1, cnt) as r:
                    turn(tile_of(lo, r), r)
                with act.Fori(1, NT) as t:
                    lo, cnt, q0 = walk(act, t)
                    turn(lo, nc.s_assert_within(q0, 1, NT * GT))
                    read_out(t - 1)
                    with act.Fori(1, cnt) as r:
                        turn(tile_of(lo, r), q0 + r)
                    root_of_var(t - 1)
                read_out(NT - 1)
                root_of_var(NT - 1)

            for l in range(2):
                rel_groups(l)
                edge_indices(l)
            act.wait_ge(ffn1_loaded, 7 * 16)
            with act.Fori(0, NG) as g:
                std_group(g + (3 * NG + 1))
                copy_turned(g + (4 * NG + 1))
                hold(act, x_ohturned, g + 1)
                act.activation(ohTb[:, 0:512], bank[3][0:X1, :], ACT.Copy)
                act.activation(ohTb[:, 512:GN], bank[1][0:X1, 256:384], ACT.Copy).then_inc(x_ohT, 1)
                act.activation(ohT[:, 0:512], bank[3][0:X1, :], ACT.Copy)
                act.activation(ohT[:, 512:GN], bank[1][0:X1, 256:384], ACT.Copy).then_inc(x_ohT, 1)
                for m in range(M1):
                    for nb in range(2):
                        u = m * 2 + nb
                        hold(act, x_h, g * (2 * M1) + (u + 1))
                        act.activation(hmT[:, m, nb * HB:(nb + 1) * HB], bank[4 + u % 3][:, 0:HB], ACT.Relu,
                                       bias=xb1[:, m:m + 1]).then_inc(x_hT, 1)

        @block.tensor
        def _(pe):
            def turn_group(k, wait=True):
                hold(pe, xn_ready, k + 1)
                for j in range(G):
                    for h in range(2):
                        o = bank[2 * h][:, j * P:(j + 1) * P] if j < 4 else bank[1][:, h * P:(h + 1) * P]
                        last = pe.transpose(o, xn5[:, j, h * P:(h + 1) * P], ident[:, :])
                last.then_inc(turned, 1)
                if wait:
                    hold(pe, xT_ready, k + 1)

            def zero_product(dst, width, start):
                return pe.matmul(dst[:, 0:width], zeros[:, 0:P], zeros[:, 0:width], start=start, stop=not start,
                                 skip_group_check=True)

            pe.wait_ge(gatw_loaded, 5 * 16)
            for d in range(2):
                for k in range(2):
                    last = pe.matmul(bank[5][:, (d * 2 + k) * HEADS:(d * 2 + k + 1) * HEADS],
                                     onehot[0:F, 2 * d + k, :], gat_ring[0:F, 0, 0:HEADS], start=True, stop=True)
            last.then_inc(attw_done, 1)
            pe.wait_ge(ident_loaded, 16)
            pe.wait_ge(wcat_done, 1)
            with pe.Fori(0, NG) as g:
                turn_group(g)
                hold(pe, t_staged, g * 2 + 1)
                for half, tiles in ((0, (0, 1, 2)), (1, (3, 4))):
                    for i, j in enumerate(tiles):
                        for k in range(2):
                            last = pe.matmul(bank[3 + half][:, i * T0W:(i + 1) * T0W],
                                             xT5[:, k, j * P:(j + 1) * P], wcat[:, k, :],
                                             start=(k == 0), stop=(k == 1))
                    last.then_inc(t_product, 1)
            pe.wait_ge(consts_done, 5)
            pe.wait_ge(ranges_done, 1)
            with pe.Fori(0, NT) as t:
                lo, cnt, q0 = walk(pe, t)
                hold(pe, s0_read, t + 1)
                zero_product(bank[5], S0W, True)
                with pe.Fori(0, cnt) as r:
                    for h in range(2):
                        hold(pe, s0_ready, (q0 + r) * 2 + (h + 1))
                        if h == 1:
                            hold(pe, s0_weighted, q0 + r + 1)
                        for j in range(h * UH, (h + 1) * UH):
                            last = pe.matmul(bank[5][:, 0:S0W], onehot[:, j, :], rhs0[:, j, 0:S0W],
                                             start=False, stop=False, skip_group_check=True)
                        last.then_inc(s0_used[h], 1)
                zero_product(bank[5], S0W, False).then_inc(s0_summed, 1)

            pe.wait_ge(ffn0_loaded, X0 * 3 * 16)
            pe.wait_ge(small0_loaded, small_loads * 16)
            pe.wait_ge(rw1_loaded, 16)
            turn_group(NG)
            with pe.Fori(0, NG) as g:
                def h1_product(e):
                    for m in range(2):
                        for nb in range(2):
                            u = e * 4 + m * 2 + nb
                            if u >= 2:
                                hold(pe, f_h1T, g * (X0 * 4) + (u - 1))
                            for k in range(2):
                                last = pe.matmul(bank[nb][:, 0:HB], ew[e][0][:, k, m * P:(m + 1) * P],
                                                 xT5[:, k, nb * HB:(nb + 1) * HB], start=(k == 0), stop=(k == 1))
                            last.then_inc(f_h1, 1)

                def h2_product(e):
                    hold(pe, f_h1T, g * (X0 * 4) + (e * 4 + 4))
                    for m in range(2):
                        for nb in range(2):
                            u = e * 4 + m * 2 + nb
                            if u >= 2:
                                hold(pe, f_h2T, g * (X0 * 4) + (u - 1))
                            for k in range(2):
                                last = pe.matmul(bank[2 + nb][:, 0:HB], ew[e][1][:, k, m * P:(m + 1) * P],
                                                 h1T[:, e % 2, k, nb * HB:(nb + 1) * HB],
                                                 start=(k == 0), stop=(k == 1))
                            last.then_inc(f_h2, 1)

                def o_unit(e, pair, product):
                    u = (e + 1) * 3 + pair
                    hold(pe, f_oread, g * 21 + (max(u - 1, 0) + 1))
                    for i, j in enumerate(range(2 * pair, min(2 * pair + 2, G))):
                        last = product(bank[4 + u % 2][:, i * D:(i + 1) * D], j)
                    last.then_inc(f_o, 1)

                def o_product(e):
                    hold(pe, f_h2T, g * (X0 * 4) + (e * 4 + 4))

                    def product(o, j):
                        for k in range(2):
                            last = pe.matmul(o, h2T[:, e % 2, k, j * P:(j + 1) * P], ew[e][2][:, k, :],
                                             start=(k == 0), stop=(k == 1))
                        return last
                    for pair in range(3):
                        o_unit(e, pair, product)

                hold(pe, xT_ready, g + (NG + 1))
                for nb in range(2):
                    for k in range(2):
                        last = pe.matmul(bank[6 + nb][:, 0:HB], rw1[:, k, :], xT5[:, k, nb * HB:(nb + 1) * HB],
                                         start=(k == 0), stop=(k == 1))
                    last.then_inc(f_rh, 1)
                hold(pe, f_rhT, g * 2 + 2)
                for j in range(G):
                    last = pe.matmul(bank[3][:, j * 8:j * 8 + X0], rhT[:, j * P:(j + 1) * P], rw2[:, :],
                                     start=True, stop=True)
                last.then_inc(f_logits, 1)
                h1_product(0)
                h1_product(1)
                hold(pe, f_softin, g + 1)
                h2_product(0)
                hold(pe, f_w, g + 1)
                for j in range(G):
                    o = bank[6][0:X0, j * P:(j + 1) * P] if j < 4 else bank[7][0:X0, 0:P]
                    last = pe.transpose(o, wsel[:, 0, j, :], ident[:, :])
                last.then_inc(f_wturned, 1)
                hold(pe, f_wT, g + 1)
                for pair in range(3):
                    o_unit(-1, pair, lambda o, j: pe.matmul(o, wT[:, j * P:(j + 1) * P], eb3[:, :],
                                                            start=True, stop=True))
                for e in range(2, X0):
                    h1_product(e)
                    h2_product(e - 1)
                    o_product(e - 2)
                h2_product(X0 - 1)
                hold(pe, f_h2T, g * (X0 * 4) + (X0 * 4 - 1))
                turn_group(g + (NG + 1), wait=False)
                o_product(X0 - 2)
                o_product(X0 - 1)

            def rel_groups(l):
                with pe.Fori(0, NG) as g:
                    if l == 0:
                        hold(pe, xT_ready, g + (2 * NG + 1))
                    else:
                        turn_group(g + (3 * NG + 1))
                    for j in range(G):
                        n1 = g * G + (j + 1)
                        hold(pe, r_based[l], n1)
                        for k in range(2):
                            last = pe.matmul(bank[3][:, 0:D], xT5[:, k, j * P:(j + 1) * P], root[:, l, k, :],
                                             start=(k == 0), stop=(k == 1))
                        last.then_inc(r_rootx[l], 1)
                        for c in range(4):
                            for half, (out_of, done) in enumerate(((r_evenout[l], r_even[l]),
                                                                   (r_oddout[l], r_odd[l]))):
                                hold(pe, out_of, g * (4 * G) + (j * 4 + c + 1))
                                for k in range(2):
                                    col = c * 1024 + half * 512
                                    last = pe.matmul(bank[4 + 2 * (c % 2) + half][:, :],
                                                     xT5[:, k, j * P:(j + 1) * P], wrel[l][:, k, col:col + 512],
                                                     start=(k == 0), stop=(k == 1))
                                last.then_inc(done, 1)
                    if l == 0:
                        turn_group(g + (2 * NG + 1), wait=False)
                if l == 0:
                    pe.wait_ge(xT_ready, 3 * NG + 1)

            def edge_sums(l):
                with pe.Fori(0, NT) as t:
                    lo, cnt, q0 = walk(pe, t)
                    hold(pe, e_read[l], t + 1)
                    zero_product(bank[0], D, True)
                    with pe.Fori(0, cnt) as r:
                        for j in range(U):
                            hold(pe, e_ready[l], (q0 + r) * U + (j + 1))
                            hold(pe, got[l][j], (q0 + r) * 16 + 16)
                            pe.matmul(bank[0][:, 0:D], onehot[:, j, :], rel_ring[:, j, :], start=False, stop=False,
                                      skip_group_check=True).then_inc(used[l][j], 1)
                    zero_product(bank[0], D, False).then_inc(e_summed[l], 1)

            for l in range(2):
                pe.wait_ge(wrel_done, (l + 1) * R)
                if l == 0:
                    pe.wait_ge(rows_loaded, 9 * 16)
                rel_groups(l)
                edge_sums(l)
            pe.wait_ge(ffn1_loaded, 7 * 16)
            with pe.Fori(0, NG) as g:
                turn_group(g + (4 * NG + 1))
                hold(pe, x_oread, g * 3 + 1)
                for j in range(G):
                    for k in range(2):
                        last = pe.matmul(bank[7][:, j * X1:(j + 1) * X1], xT5[:, k, j * P:(j + 1) * P],
                                         rwT[:, k, :], start=(k == 0), stop=(k == 1))
                last.then_inc(x_logits, 1)
                hold(pe, x_oh, g + 1)
                for j in range(G):
                    o = bank[3][0:X1, j * P:(j + 1) * P] if j < 4 else bank[1][0:X1, 256:384]
                    last = pe.transpose(o, oh[:, j, :], ident[:, :])
                last.then_inc(x_ohturned, 1)
                hold(pe, x_ohT, g * 2 + 1)
                for m in range(M1):
                    for nb in range(2):
                        u = m * 2 + nb
                        if u >= 3:
                            hold(pe, x_hT, g * (2 * M1) + (u - 2))
                        o = bank[4 + u % 3][:, 0:HB]
                        for k in range(2):
                            pe.matmul(o, xw1[:, k, m * P:(m + 1) * P], xT5[:, k, nb * HB:(nb + 1) * HB],
                                      start=(k == 0), stop=False)
                        pe.matmul(o, negmask[:, m * P:(m + 1) * P], ohTb[:, nb * HB:(nb + 1) * HB],
                                  start=False, stop=True).then_inc(x_h, 1)
                hold(pe, x_ohT, g * 2 + 2)
                hold(pe, x_hT, g * (2 * M1) + 2 * M1)
                for pair in range(3):
                    if pair == 2:
                        hold(pe, x_oread, g * 3 + 2)
                    for i, j in enumerate(range(2 * pair, min(2 * pair + 2, G))):
                        o = bank[3 + 4 * (pair % 2)][:, i * D:(i + 1) * D]
                        pe.matmul(o, ohT[:, j * P:(j + 1) * P], xb2, start=True, stop=False)
                        for m in range(M1):
                            last = pe.matmul(o, hmT[:, m, j * P:(j + 1) * P], xw2[:, m, :],
                                             start=False, stop=(m == M1 - 1))
                    last.then_inc(x_o, 1)

        @block.vector
        def _(dve):
            steps = Steps(dve, dve_step)
            v = dve
            for one in (t_staged, turned, s0_read, s0_posted, f_oread, r_based[0], r_based[1], e_read[0], e_read[1],
                        e_var[0], e_var[1], x_oread):
                v.nop().then_inc(one, 1)
            for l in range(2):
                v.nop().then_inc(r_oddout[l], 2)

            def norm_group(g, k, ks, read=None, count=None):
                hold(v, turned, k + 1)
                for j in range(G):
                    last = v.bn_stats(stats[:, j, :], x_res[:, bass.ds(g * G + j, 1), :].rearrange("p o d -> p (o d)"))
                steps.step(last)
                for j in range(G):
                    last = v.bn_aggr(mv[:, j, :], stats[:, j, :])
                steps.step(last)
                v.tensor_scalar(veps[:, :], mv[:, :, 1], EPS, None, ALU.add).then_inc(var_ready, 1)
                hold(v, std_ready, ks + 1)
                steps.step(v.reciprocal(rstd[:, :], std[:, :]))
                if read is not None:
                    hold(v, read, count)
                for j in range(G):
                    last = v.tensor_scalar(xn5[:, j, :], x_res[:, bass.ds(g * G + j, 1), :].rearrange(
                        "p o d -> p (o d)"), mv[:, j, 0:1], rstd[:, j:j + 1], ALU.subtract, ALU.mult)
                last.then_inc(xn_ready, 1)

            v.wait_ge(meta_loaded, 5 * 16)
            v.wait_ge(consts_done, 5)
            tmp = xn5[:, :, :].rearrange("p t d -> p (t d)")
            emin, emax = tmp[:, 0:4], tmp[:, 4:8]
            c1 = tmp[:, 130:230].rearrange("p (n j) -> p n j", j=4)
            c2 = tmp[:, 230:330].rearrange("p (n j) -> p n j", j=4)
            c3 = tmp[:, 330:430].rearrange("p (n j) -> p n j", j=4)
            up = xT5[:, 1, 0:2 * NT]
            m2 = xT5[:, 0, 0:2 * NT]
            first = iota_n[:, :].rearrange("p (n q) -> p n q", q=P)[:, :, 0:1].broadcast_to([P, NT, 4])

            def row(x):
                return x.unsqueeze(1).broadcast_to([P, NT, 4])
            steps.step(v.tensor_reduce(emin, dstT, AX.X, ALU.min))
            steps.step(v.tensor_reduce(emax, dstT, AX.X, ALU.max))
            steps.step(v.tensor_scalar(emin, emin, float(P - 1), None, ALU.subtract))
            steps.step(v.tensor_tensor(c1, row(emin), first, ALU.is_le))
            steps.step(v.tensor_tensor(c2, row(emax), first, ALU.is_ge))
            steps.step(v.tensor_tensor(c1, c1, c2, ALU.mult))
            steps.step(v.tensor_scalar(tmp[:, 8:12], tile_no[:, :], -1.0, float(ET), ALU.mult, ALU.add))
            steps.step(v.tensor_scalar(tmp[:, 12:16], tile_no[:, :], 1.0, None, ALU.add))
            steps.step(v.tensor_tensor(c2, c1, row(tmp[:, 8:12]), ALU.mult))
            steps.step(v.tensor_tensor(c3, c1, row(tmp[:, 12:16]), ALU.mult))
            v.tensor_reduce(up[:, 0:NT], c2, AX.X, ALU.max)
            v.tensor_reduce(up[:, NT:2 * NT], c3, AX.X, ALU.max).then_inc(bounds_ready, 1)
            v.wait_ge(bounds_max, 1)
            lo_f, cnt_f = tmp[:, 20:45], tmp[:, 45:70]
            cnt_i = tmp[:, 70:95].bitcast(I32)
            steps.step(v.tensor_scalar(lo_f, m2[:, 0:NT], -1.0, float(ET), ALU.mult, ALU.add))
            steps.step(v.scalar_tensor_tensor(cnt_i, m2[:, NT:2 * NT], float(U - 1), lo_f, ALU.add, ALU.subtract))
            steps.step(v.tensor_scalar(cnt_i, cnt_i, float(65536 // U + 1), None, ALU.mult))
            steps.step(v.tensor_scalar(cnt_i, cnt_i, 16, None, ALU.arith_shift_right))
            steps.step(v.tensor_scalar(cnt_f, cnt_i, float(U_MIN), None, ALU.max))
            steps.step(v.tensor_scalar(tmp[:, 95:95 + NT], cnt_f, -float(U), float(ETP), ALU.mult, ALU.add))
            steps.step(v.tensor_tensor(ranges[:, 0, :], lo_f, tmp[:, 95:95 + NT], ALU.min))
            steps.step(v.tensor_copy(ranges[:, 1, :], cnt_f))
            sums = [tmp[:, 430:455], tmp[:, 455:480]]
            steps.step(v.memset(sums[0][:, 0:1], 0.0))
            steps.step(v.tensor_copy(sums[0][:, 1:NT], cnt_f[:, 0:NT - 1]))
            d, cur = 1, 0
            while d < NT:
                steps.step(v.tensor_copy(sums[1 - cur][:, 0:d], sums[cur][:, 0:d]))
                steps.step(v.tensor_tensor(sums[1 - cur][:, d:NT], sums[cur][:, d:NT], sums[cur][:, 0:NT - d],
                                           ALU.add))
                d, cur = 2 * d, 1 - cur
            v.tensor_copy(ranges[:, 2, :], sums[cur]).then_inc(ranges_done, 1)
            v.wait_ge(ranges_done, 1)
            v.memset(src_idx[:, ETP:ETP + U], 0)
            v.tensor_copy(dst_f[:, :], dst_i).then_inc(dst_done, 1)
            v.wait_ge(dst_done, 1)

            v.wait_ge(attw_done, 1)
            for d in range(2):
                for k in range(2):
                    last = v.tensor_copy(wcat[:, k, d * C0 + F:(d + 1) * C0],
                                         bank[5][:, (d * 2 + k) * HEADS:(d * 2 + k + 1) * HEADS])
            last.then_inc(wcat_done, 1)
            v.wait_ge(x_loaded, 16)
            def stage_table(g):
                hold(v, t_stored, (g + 1) * 16)
                hold(v, t_product, g * 2 + 1)
                v.tensor_copy(t0s[:, 0:3, :], bank[3][:, 0:3 * T0W].rearrange("p (j c) -> p j c", c=T0W))\
                    .then_inc(t_staged, 1)
                hold(v, t_product, g * 2 + 2)
                v.tensor_copy(t0s[:, 3:5, :], bank[4][:, 0:2 * T0W].rearrange("p (j c) -> p j c", c=T0W))\
                    .then_inc(t_staged, 1)

            norm_group(0, 0, 0)
            with v.Fori(0, NG - 1) as g:
                steps.enter(g, 3)
                norm_group(g + 1, g + 1, g + 1)
                stage_table(g)
            steps.leave(NG - 1)
            stage_table(NG - 1)
            v.memset(msg[:, :, F:F + 1], 1.0)
            v.wait_ge(t_stored, (NG + 1) * 16)
            v.memset(rhs0[:, :, S0W - 1:S0W], 1.0)
            v.wait_ge(wcat_done, 1)
            for j in range(U):
                v.tensor_copy(idx[:, j:j + 1], src_idx[:, j:j + 1]).then_inc(used[2][j], 1)
            with v.Fori(0, GT) as i:
                next_idx = src_idx[:, bass.ds(i * U + U, U)]
                msgs = msg[:, bass.ds(i * U, U), :]
                dd = dir_e[:, bass.ds(i * U, U), :]
                for j in range(U):
                    hold(v, g0_rev, i * U + (j + 1))
                    v.scalar_tensor_tensor(msgs[:, j, 0:F], gat_ring[:, j, 0:F], dd[:, j, 0:1], rev[:, j, 0:F],
                                           ALU.mult, ALU.add)
                    v.scalar_tensor_tensor(msgs[:, j, F + 1:MW], gat_ring[:, j, F:C0], dd[:, j, 0:1], rev[:, j, F:C0],
                                           ALU.mult, ALU.add)
                    v.tensor_copy(idx[:, j:j + 1], next_idx[:, j:j + 1]).then_inc(used[2][j], 1)
            for j in range(U):
                v.wait_ge(used[2][j], GT + 1)
            steps.step(v.scalar_tensor_tensor(src_idx[:, 0:ETP], src_idx[:, 0:ETP], float(R), et_i,
                                              ALU.mult, ALU.add))
            scores = msg[:, :, F + 1:MW]
            v.tensor_reduce(mx[:, :], scores.rearrange("p t h -> p h t"), AX.X, ALU.max).then_inc(lmax_ready, 1)
            v.wait_ge(lmax_ready, 1)
            steps.step(v.scalar_tensor_tensor(scores, scores, 0.2, scores, ALU.mult, ALU.max))
            v.wait_ge(gmax_ready, 1)
            steps.step(v.scalar_tensor_tensor(glr[:, :], gmx[:, :], 0.2, gmx[:, :], ALU.mult, ALU.max))
            v.tensor_tensor(scores, scores, glr[:, :].unsqueeze(1).broadcast_to([P, GT * U, HEADS]),
                            ALU.subtract).then_inc(exp_in, 1)
            v.wait_ge(exp_out, 1)
            heads = sums0[:, 0:S0W - 1].rearrange("p (h c) -> p h c", h=HEADS)

            def gat_turn(nodes, lo, q):
                dd = dst_f[:, bass.ds(lo, U)]
                q = v.snap(q)
                for h in range(2):
                    hold(v, s0_used[h], q + 1)
                    for j in range(h * UH, (h + 1) * UH):
                        last = v.tensor_scalar(onehot[:, j, :], nodes, dd[:, j:j + 1], None, ALU.is_equal)
                    if h == 0:
                        last = weigh(v, lo, 0)
                    last.then_inc(s0_ready, 1)

            def gat_out(t):
                hold(v, s0_read, t + 2)
                v.tensor_scalar(den[:, 0:HEADS], heads[:, :, F], 1e-10, None, ALU.add)
                steps.step(v.tensor_scalar(den[:, HEADS:HEADS + 1], sums0[:, S0W - 1:S0W], 1.0, None, ALU.add))
                steps.step(v.reciprocal(rden[:, :], den[:, :]))
                v.tensor_copy(rcnt[:, bass.ds(t, 1)], rden[:, HEADS:HEADS + 1])
                xt = x_res[:, bass.ds(t, 1), :].rearrange("p o d -> p (o d)")
                for h in range(HEADS):
                    last = v.scalar_tensor_tensor(xt[:, h * F:(h + 1) * F], heads[:, h, 0:F], rden[:, h:h + 1],
                                                  xt[:, h * F:(h + 1) * F], ALU.mult, ALU.add)
                last.then_inc(s0_posted, 1)

            lo, cnt, q0 = walk(v, 0)
            with v.Fori(0, cnt) as r:
                gat_turn(iota_n[:, 0:P], tile_of(lo, r), q0 + r)
            with v.Fori(1, NT) as t:
                steps.enter(t - 1, 2)
                lo, cnt, q0 = walk(v, t)
                nodes = iota_n[:, bass.ds(t * P, P)]
                gat_turn(nodes, lo, q0)
                gat_out(t - 1)
                with v.Fori(1, cnt) as r:
                    gat_turn(nodes, tile_of(lo, r), q0 + r)
            steps.leave(NT - 1)
            gat_out(NT - 1)
            v.wait_ge(s0_posted, NT + 1)

            v.wait_ge(small0_loaded, small_loads * 16)
            norm_group(0, NG, NG)
            with v.Fori(0, NG) as g:
                steps.enter(g, 18)

                def o_read(e):
                    for pair in range(3):
                        u = (e + 1) * 3 + pair
                        hold(v, f_o, g * 21 + (u + 1))
                        if e >= 0:
                            hold(v, f_oread, g * 21 + (u - 1))
                        js = range(2 * pair, min(2 * pair + 2, G))
                        if e < 0:
                            xs = x_res[:, bass.ds(g * G + js[0], len(js)), :].rearrange("p t d -> p (t d)")
                            last = v.tensor_tensor(xs, bank[4 + u % 2][:, 0:len(js) * D], xs, ALU.add)
                        else:
                            xs = x_res[:, bass.ds(g * G + js[0], len(js)), :]
                            for i, j in enumerate(js):
                                last = v.scalar_tensor_tensor(
                                    xs[:, i, :], bank[4 + u % 2][:, i * D:(i + 1) * D],
                                    wsel[:, 0, j, e:e + 1], xs[:, i, :], ALU.mult, ALU.add)
                        last.then_inc(f_oread, 1)

                def each(x, n):
                    return x.broadcast_to([P, G, n])

                hold(v, f_logits, g + 1)
                steps.step(v.tensor_tensor(
                    lg[:, :, 0:X0], bank[3][:, 0:G * 8].rearrange("p (j c) -> p j c", c=8)[:, :, 0:X0],
                    rb2[:, :].unsqueeze(1).broadcast_to([P, G, X0]), ALU.add))
                steps.step(v.tensor_reduce(gate[:, :, 2:3].rearrange("p t o -> p (t o)"), lg[:, :, 0:X0],
                                           AX.X, ALU.max))
                v.tensor_tensor(lg[:, :, 0:X0], lg[:, :, 0:X0], each(gate[:, :, 2:3], X0),
                                ALU.subtract).then_inc(f_softin, 1)
                hold(v, f_softout, g + 1)
                steps.step(v.tensor_reduce(gate[:, :, 3:4].rearrange("p t o -> p (t o)"), lg[:, :, 0:X0],
                                           AX.X, ALU.add))
                steps.step(v.reciprocal(gate[:, :, 2:3], gate[:, :, 3:4]))
                steps.step(v.tensor_tensor(pr[:, :, 0:X0], lg[:, :, 0:X0], each(gate[:, :, 2:3], X0), ALU.mult))
                for j in range(G):
                    last = v.max(top[:, j, :], pr[:, j, :])
                steps.step(last)
                v.tensor_tensor(gate[:, :, 0:1], top[:, :, 1:2], top[:, :, 0:1], ALU.subtract).then_inc(f_gap, 1)
                for j in range(G):
                    last = v.max_index(topi[:, j, :], top[:, j, :], pr[:, j, :])
                steps.step(last)
                steps.step(v.tensor_copy(idxf[:, :, :], topi[:, :, 0:2]))
                hold(v, f_gapexp, g + 1)
                steps.step(v.tensor_scalar(gate[:, :, 2:3], gate[:, :, 1:2], 1.0, None, ALU.add))
                steps.step(v.reciprocal(gate[:, :, 2:3], gate[:, :, 2:3]))
                steps.step(v.tensor_tensor(gate[:, :, 3:4], gate[:, :, 1:2], gate[:, :, 2:3], ALU.mult))
                for c in range(2):
                    steps.step(v.tensor_tensor(
                        wsel[:, c], iota_x[:, 0:X0].unsqueeze(1).broadcast_to([P, G, X0]),
                        each(idxf[:, :, c:c + 1], X0), ALU.is_equal))
                    steps.step(v.tensor_tensor(wsel[:, c], wsel[:, c], each(gate[:, :, 2 + c:3 + c], X0), ALU.mult))
                v.tensor_tensor(wsel[:, 0], wsel[:, 0], wsel[:, 1], ALU.add).then_inc(f_w, 1)
                hold(v, f_w, g + 1)
                for e in range(-1, X0):
                    if e == X0 - 2:
                        norm_group((g + 1) % NG, g + (NG + 1), g + (NG + 1))
                    o_read(e)
            steps.leave(NG)
            v.wait_ge(f_oread, NG * 21 + 1)

            lgb = onehot[:, 0:2, :].rearrange("p a b -> p (a b)")

            def rel_groups(l):
                with v.Fori(0, NG) as g:
                    steps.enter(g, (3 if l == 0 else 0) + 2 * G)
                    if l == 0:
                        hold(v, xn_ready, g + (2 * NG + 1))
                    else:
                        hold(v, turned, g + (3 * NG + 2))
                        v.tensor_copy(xn5[:, :, :], h_res[:, bass.ds(g * G, G), :]).then_inc(xn_ready, 1)
                        hold(v, xn_ready, g + (3 * NG + 2))
                    for j in range(G):
                        hold(v, r_rootx[l], g * G + (j + 1))
                        steps.step(v.tensor_tensor(lgb, bank[3][:, 0:D], xn5[:, j, :], ALU.add))
                        steps.step(v.tensor_tensor(lgb, lgb, rows_bc[:, l, 0, :], ALU.add))
                        for c in range(4):
                            hold(v, r_odd[l], g * (4 * G) + (j * 4 + c + 1))
                            hold(v, r_stored[l][c], g * (16 * G) + (j + 1) * 16)
                            b = bank[5 + 2 * (c % 2)]
                            if c == 3:
                                v.scalar_tensor_tensor(
                                    base[:, bass.ds(g * G + j, 1), :].rearrange("p o d -> p (o d)"), b[:, D:2 * D],
                                    rcnt[:, bass.ds(g * G + j, 1)], lgb, ALU.mult, ALU.add).then_inc(r_based[l], 1)
                            v.tensor_copy(stage[:, c * 1024 + 512:(c + 1) * 1024], b[:, :]).then_inc(r_oddout[l], 1)
                    if l == 0:
                        norm_group((g + 1) % NG, g + (2 * NG + 1), g + (2 * NG + 1), r_based[0], g * G + (G + 1))
                steps.leave(NG)
                v.wait_ge(r_based[l], NT + 1)


            def edge_sums(l):
                y, z = xn5[:, 1, :], xn5[:, 2, :]

                def turn(nodes, lo, q):
                    dd = dst_f[:, bass.ds(lo, U)]
                    weights = ea[:, bass.ds(lo, U)]
                    for j in range(U):
                        hold(v, used[l][j], q + 1)
                        v.tensor_scalar(onehot[:, j, :], nodes, dd[:, j:j + 1], weights[:, j:j + 1],
                                        ALU.is_equal, ALU.mult).then_inc(e_ready[l], 1)

                def variance(t):
                    hold(v, e_read[l], t + 2)
                    steps.step(v.tensor_tensor(y, mean, base[:, bass.ds(t, 1), :].rearrange("p o d -> p (o d)"),
                                               ALU.add))
                    steps.step(v.bn_stats(stats[:, 0, :], y))
                    steps.step(v.bn_aggr(mv[:, 0, :], stats[:, 0, :]))
                    v.tensor_scalar(veps[:, 0:1], mv[:, 0, 1:2], EPS, None, ALU.add).then_inc(e_var[l], 1)

                def norm(t):
                    hold(v, e_std[l], t + 1)
                    steps.step(v.reciprocal(rstd[:, 0:1], std[:, 0:1]))
                    steps.step(v.tensor_scalar(z, y, mv[:, 0, 0:1], rstd[:, 0:1], ALU.subtract, ALU.mult))
                    steps.step(v.tensor_tensor(z, z, rows_bc[:, l, 1, :], ALU.mult))
                    steps.step(v.tensor_tensor(z, z, rows_bc[:, l, 2, :], ALU.add))
                    if l == 0:
                        v.tensor_scalar(h_res[:, bass.ds(t, 1), :].rearrange("p o d -> p (o d)"), z, 0.0, None,
                                        ALU.max).then_inc(e_posted[l], 1)
                    else:
                        xt = x_res[:, bass.ds(t, 1), :].rearrange("p o d -> p (o d)")
                        v.scalar_tensor_tensor(xt, z, 0.0, xt, ALU.max, ALU.add).then_inc(e_posted[l], 1)

                lo, cnt, q0 = walk(v, 0)
                with v.Fori(0, cnt) as r:
                    turn(iota_n[:, 0:P], tile_of(lo, r), q0 + r)
                with v.Fori(1, NT) as t:
                    steps.enter(t - 1, 7)
                    lo, cnt, q0 = walk(v, t)
                    nodes = iota_n[:, bass.ds(t * P, P)]
                    turn(nodes, lo, q0)
                    variance(t - 1)
                    with v.Fori(1, cnt) as r:
                        turn(nodes, tile_of(lo, r), q0 + r)
                    norm(t - 1)
                steps.leave(NT - 1)
                variance(NT - 1)
                norm(NT - 1)
                v.wait_ge(e_posted[l], NT)

            for l in range(2):
                if l == 0:
                    v.wait_ge(rows_loaded, 9 * 16)
                rel_groups(l)
                if l == 0:
                    v.wait_ge(wrel_done, 2 * R)
                edge_sums(l)
            v.wait_ge(ffn1_loaded, 7 * 16)
            with v.Fori(0, NG) as g:
                steps.enter(g, 7)
                norm_group(g, g + (4 * NG + 1), g + (3 * NG + 1))
                hold(v, x_logits, g + 1)
                steps.step(v.tensor_tensor(lg[:, :, :], bank[7][:, 0:G * X1].rearrange("p (j c) -> p j c", c=X1),
                                           rb.unsqueeze(1).broadcast_to([P, G, X1]), ALU.add))
                for j in range(G):
                    last = v.max(top[:, j, :], lg[:, j, :])
                steps.step(last)
                for j in range(G):
                    last = v.max_index(topi[:, j, :], top[:, j, :], lg[:, j, :])
                steps.step(last)
                steps.step(v.tensor_copy(idxf[:, :, 0:1], topi[:, :, 0:1]))
                v.tensor_tensor(oh[:, :, :], iota_x[:, :].unsqueeze(1).broadcast_to([P, G, X1]),
                                idxf[:, :, 0:1].broadcast_to([P, G, X1]), ALU.is_equal).then_inc(x_oh, 1)
                hold(v, x_stored, (g + 1) * 16)
                for pair in range(3):
                    hold(v, x_o, g * 3 + (pair + 1))
                    n = min(2, G - 2 * pair)
                    v.scalar_tensor_tensor(
                        outs[:, 2 * pair:2 * pair + n, :].rearrange("p t d -> p (t d)"),
                        bank[3 + 4 * (pair % 2)][:, 0:n * D], 0.0,
                        x_res[:, bass.ds(g * G + 2 * pair, n), :].rearrange("p t d -> p (t d)"),
                        ALU.max, ALU.add).then_inc(x_oread, 1)
            steps.leave(NG)


def kernel(**inputs):
    import ml_dtypes
    import numpy as np
    import concourse.bacc as bacc
    from concourse.bass_utils import run_bass_kernel_spmd as run

    v = {k: np.asarray(x) for k, x in inputs.items()}

    def tiles(x, mode, **kw):
        pad = [(0, ETP * P - E)] + [(0, 0)] * (x.ndim - 1)
        x = np.pad(x, pad, mode=mode, **kw).reshape((ETP, P) + x.shape[1:])
        return np.ascontiguousarray(np.moveaxis(x, 0, 1))

    def cols(x):
        x = x.reshape(x.shape[:-1] + (x.shape[-1] // P, P))
        return np.ascontiguousarray(np.moveaxis(x, -1, 0))

    far = np.full((X1, X1, H1), FAR, np.float32)
    far[np.arange(X1), np.arange(X1)] = 0
    dst_rows = np.pad(v["dst"], (0, 4 * P * P - E), constant_values=NOWHERE)
    arrays = {
        "x": np.pad(v["x"], ((0, NT * P - N), (0, 0))),
        "dst_rows": np.ascontiguousarray(dst_rows.reshape(4, P, P).transpose(1, 0, 2)),
        "dst_t": tiles(v["dst"], "constant", constant_values=NOWHERE),
        "src_t": tiles(v["src"], "edge"),
        "et_t": tiles(v["edge_type_16"], "edge"),
        "ea_t": tiles(v["edge_weight"], "constant"),
        "dir_t": tiles(v["edge_attr_2"], "edge"),
        "wf": v["L0_gnn_W_forward"], "wf_T": np.ascontiguousarray(v["L0_gnn_W_forward"].T),
        "wr": v["L0_gnn_W_reverse"], "wr_T": np.ascontiguousarray(v["L0_gnn_W_reverse"].T),
        "attn_T": np.ascontiguousarray(v["L0_gnn_attn_forward"][0].T),
        "ident": np.eye(P, dtype=np.float32),
        "rw1": v["L0_ffn_router_w1"], "rb1": v["L0_ffn_router_b1"],
        "rw2": v["L0_ffn_router_w2"], "rb2": v["L0_ffn_router_b2"],
        "ew1": v["L0_ffn_expert_w1"], "ew2": v["L0_ffn_expert_w2"], "ew3": v["L0_ffn_expert_w3"],
        "eb1T": cols(v["L0_ffn_expert_b1"]), "eb2T": cols(v["L0_ffn_expert_b2"]), "eb3": v["L0_ffn_expert_b3"],
        "xw1": np.ascontiguousarray(v["L1_ffn_W1"].transpose(1, 0, 2).reshape(D, X1 * H1)),
        "xb1T": cols(v["L1_ffn_b1"].reshape(X1 * H1)),
        "xw2": v["L1_ffn_W2"].reshape(X1 * H1, D), "xb2": v["L1_ffn_b2"],
        "rwT": np.ascontiguousarray(v["L1_ffn_router_w"].T), "rb": v["L1_ffn_router_b"],
        "negmask": far.reshape(X1, X1 * H1).astype(ml_dtypes.bfloat16),
    }
    for l in range(2):
        arrays[f"basis{l}"] = v[f"L1_gnn_basis{l + 1}"]
        arrays[f"att{l}"] = v[f"L1_gnn_att{l + 1}"].reshape(R * B)
        arrays[f"root{l}"] = v[f"L1_gnn_root{l + 1}"]
        arrays[f"bias{l}"] = v[f"L1_gnn_bias{l + 1}"]
        arrays[f"ln_g{l}"] = v[f"L1_gnn_ln{l + 1}_g"]
        arrays[f"ln_b{l}"] = v[f"L1_gnn_ln{l + 1}_b"]

    nc = bacc.Bacc("TRN2", target_bir_lowering=False, num_devices=1)
    arrays = {f"in_{k}": np.ascontiguousarray(x) for k, x in arrays.items()}
    aps = {k[3:]: nc.dram_tensor(k, x.shape, mybir.dt.from_np(x.dtype), kind="ExternalInput").ap()
           for k, x in arrays.items()}
    out = nc.dram_tensor("out", (NT * P, D), F32, kind="ExternalOutput").ap()
    build(nc, aps, out)
    r = run(nc, [arrays], core_ids=[0])
    return r.results[0]["out"][:N]
```

```python
from contextlib import ExitStack

import concourse.bass as bass
from concourse import mybir

ALU = mybir.AluOpType
ACT = mybir.ActivationFunctionType
AX = mybir.AxisListType
F32 = mybir.dt.float32
BF16 = mybir.dt.bfloat16
I32 = mybir.dt.int32
U32 = mybir.dt.uint32
I16 = mybir.dt.int16

P = 128
N = 3125
NT = 25
G = 5
NG = NT // G
GN = G * P
HB = GN // 2
D = 256
E = 50000
ET = (E + P - 1) // P
U = 6
PARTS = ((0, 2), (2, 6))
U_MIN = 3
GT = (ET + U - 1) // U
ETP = GT * U
TURNS, BEFORE = 1 << 9, 1 << 16
NOWHERE = 4096
HEADS = 4
F = 64
C0 = F + HEADS
T0W = 2 * C0
MW = F + 1 + HEADS
S0W = HEADS * (F + 1) + 1
R = 16
B = 8
X0 = 6
X1 = 32
H1 = 64
M1 = X1 * H1 // P
EPS = 1e-5
FAR = -1.7e38


class Steps:

    def __init__(self, eng, sem):
        self.eng, self.sem = eng, sem
        self.before, self.n, self.turn, self.per_turn = 0, 0, None, 0

    def enter(self, turn, per_turn):
        self.before += self.n
        self.turn, self.per_turn, self.n = turn, per_turn, 0

    def leave(self, turns):
        assert self.n == self.per_turn, f"steps a turn: {self.n}"
        self.before += turns * self.per_turn
        self.turn, self.n = None, 0

    def step(self, ins):
        ins.then_inc(self.sem, 1)
        self.n += 1
        if self.turn is None:
            self.eng.wait_ge(self.sem, self.before + self.n)
        else:
            self.eng.wait_ge(self.sem, self.turn * self.per_turn + (self.before + self.n))
            self.eng.nop(nofuse=True)


def hold(eng, sem, value):
    eng.wait_ge(sem, value)
    eng.nop(nofuse=True)


def build(nc, a, out):
    ctx = ExitStack()
    with ctx:
        def sb(name, shape, dt=F32):
            return ctx.enter_context(nc.sbuf_tensor(name, shape, dt))

        def sem(name):
            return ctx.enter_context(nc.semaphore(name))

        gat_table = nc.dram_tensor("gat_table", (NT * P, T0W), F32, kind="Internal").ap()
        rel_table = [nc.dram_tensor(f"rel_table{l}", (NT * P * R, D), F32, kind="Internal").ap()
                     for l in range(2)]

        x_res = sb("x_res", [P, NT, D])
        region_a = sb("region_a", [P, 9216])
        region_b = sb("region_b", [P, 4096])
        region_m = sb("region_m", [P, GT * U * MW])
        iota_n = sb("iota_n", [P, NT * P], I16)
        src_idx = sb("src_idx", [P, ETP + U], I32)
        dst_f = sb("dst_f", [P, ETP])
        idx = sb("idx", [P, U], I32)
        gat_ring = sb("gat_ring", [P, U, T0W])
        onehot = sb("onehot", [P, U, P])
        ident = sb("ident", [P, P])
        rb1 = sb("rb1", [P, 1])
        rw2 = sb("rw2", [P, X0])
        rb2 = sb("rb2", [P, X0])
        eb1 = sb("eb1", [P, X0, 2])
        eb2 = sb("eb2", [P, X0, 2])
        eb3 = sb("eb3", [X0, D])
        stats = sb("stats", [P, G, 6])
        mv = sb("mv", [P, G, 2])
        veps = sb("veps", [P, G])
        std = sb("std", [P, G])
        rstd = sb("rstd", [P, G])
        rcnt = sb("rcnt", [P, NT])
        mx = sb("mx", [P, HEADS])
        gmx = sb("gmx", [P, HEADS])
        glr = sb("glr", [P, HEADS])
        den = sb("den", [P, HEADS + 1])
        rden = sb("rden", [P, HEADS + 1])
        ranges = sb("ranges", [P, 3, NT], I32)
        zeros = sb("zeros", [P, S0W], BF16)
        att_bc = sb("att_bc", [P, 2, R * B])
        att_cur = sb("att_cur", [P, B])
        lg = sb("lg", [P, G, X1])
        pr = sb("pr", [P, G, 8])
        top = sb("top", [P, G, 8])
        topi = sb("topi", [P, G, 8], U32)
        idxf = sb("idxf", [P, G, 2])
        gate = sb("gate", [P, G, 4])
        wsel = sb("wsel", [P, 2, G, X0])
        oh = sb("oh", [P, G, X1])
        iota_x = sb("iota_x", [P, X1])
        tile_no = sb("tile_no", [P, 4])

        ew = [[region_a[:, (e * 3 + w) * 512:(e * 3 + w + 1) * 512].rearrange("p (k n) -> p k n", k=2)
               for w in range(3)] for e in range(X0)]
        rows_bc = region_a[:, 6656:6656 + 6 * D].rearrange("p (l c d) -> p l c d", l=2, c=3)
        root = region_a[:, 8192:8192 + 4 * D].rearrange("p (l k d) -> p l k d", l=2, k=2)
        negmask = region_a[0:X1, 0:1024].bitcast(BF16)
        ohT = region_a[0:X1, 1024:1024 + GN]
        ohTb = region_a[0:X1, 1664:1664 + GN // 2].bitcast(BF16)
        xb2 = region_a[0:X1, 2048:2048 + D]
        rwT = region_a[:, 2304:2304 + 2 * X1].rearrange("p (k n) -> p k n", k=2)
        rb = region_a[:, 2368:2368 + X1]
        xb1 = region_a[:, 2400:2400 + M1]
        outs = region_a[:, 2432:2432 + G * D].rearrange("p (t d) -> p t d", d=D)
        dir_e = region_b[:, 0:2 * ETP].rearrange("p (t c) -> p t c", c=2)
        rev = region_b[:, 800:800 + U * C0].rearrange("p (j c) -> p j c", c=C0)
        rhs0 = region_b[:, 0:(2 + 2 * 4) * (S0W + 1)].rearrange("p (j c) -> p j c", c=S0W + 1)
        t0s = region_b[:, 1208:1208 + G * T0W].rearrange("p (j c) -> p j c", c=T0W)
        dstT = region_b[:, 1888:1888 + 512].bitcast(I32).rearrange("p (j c) -> p j c", c=P)
        et_i = region_b[:, 2784:2784 + ETP].bitcast(I32)
        dst_i = region_b[:, 3180:3180 + ETP].bitcast(I32)
        sums0 = region_b[:, 3576:3576 + S0W]
        wcat = region_b[:, 3576:3576 + 2 * T0W].rearrange("p (k c) -> p k c", k=2)
        basis = [x.rearrange("p (b k n) -> p b k n", b=B, k=2) for x in (region_b[:, :], region_a[:, 0:4096])]
        stage = region_b
        msg = region_m[:, :].rearrange("p (t c) -> p t c", c=MW)
        wrel = [region_m[:, l * 8192:(l + 1) * 8192].rearrange("p (k n) -> p k n", k=2) for l in range(2)]
        at = 16384
        base = region_m[:, at:at + NT * D].rearrange("p (t d) -> p t d", d=D)
        h1T = region_m[:, at:at + 2560].rearrange("p (s m n) -> p s m n", s=2, m=2)
        h2T = region_m[:, at + 2560:at + 5120].rearrange("p (s m n) -> p s m n", s=2, m=2)
        wacc = [x.rearrange("p (s k n) -> p s k n", s=2, k=2)
                for x in (region_m[:, at + 5120:at + 6144], region_a[:, 4096:5120])]
        at += NT * D
        xn5 = region_m[:, at:at + G * D].rearrange("p (t d) -> p t d", d=D)
        at += G * D
        xn_x = region_a[:, 3712:3712 + G * D].rearrange("p (t d) -> p t d", d=D)
        e_stats, e_mv = region_a[:, 5632:5638], region_a[:, 5638:5640]
        e_veps, e_root, e_rstd = region_a[:, 5640:5641], region_a[:, 5641:5642], region_a[:, 5642:5643]
        mean, h_row, based = xn5[:, 0, :], xn5[:, 3, :], xn5[:, 4, :]
        xT5 = region_m[:, at:at + 2 * GN].rearrange("p (k n) -> p k n", k=2)
        at += 2 * GN
        rhT = region_m[:, at:at + GN]
        wT = region_m[0:X0, at + GN:at + 2 * GN]
        rw1 = region_m[:, at + 2 * GN:at + 2 * GN + 2 * P].rearrange("p (k n) -> p k n", k=2)
        rel_ring = region_m[:, at:at + U * D].rearrange("p (j d) -> p j d", j=U)
        at += U * D
        ea = region_m[:, at:at + ETP]
        assert at + ETP <= GT * U * MW
        xw1 = region_m[:, 0:4096].rearrange("p (k n) -> p k n", k=2)
        xw2 = region_m[:, 4096:8192].rearrange("p (m n) -> p m n", m=M1)
        hmT = [x[:, i * GN:(i + 1) * GN] for x, n in ((region_m[:, 8192:16384], 12), (region_b, M1 - 12))
               for i in range(n)]

        bank = [ctx.enter_context(nc.psum_tensor(f"bank{i}", [P, 512], F32)) for i in range(8)]

        meta_loaded, x_first, x_loaded, gatw_loaded, ident_loaded = map(sem, (
            "meta_loaded", "x_first", "x_loaded", "gatw_loaded", "ident_loaded"))
        ffn0_loaded, small0_loaded, basis_loaded, rows_loaded, ffn1_loaded = map(sem, (
            "ffn0_loaded", "small0_loaded", "basis_loaded", "rows_loaded", "ffn1_loaded"))
        consts_done, bounds_ready, bounds_max, ranges_done, dst_done = map(sem, (
            "consts_done", "bounds_ready", "bounds_max", "ranges_done", "dst_done"))
        attw_done, wcat_done = map(sem, ("attw_done", "wcat_done"))
        var_ready, std_ready, xn_ready, turned, xT_ready = map(sem, (
            "var_ready", "std_ready", "xn_ready", "turned", "xT_ready"))
        t_product, t_staged, t_stored = map(sem, ("t_product", "t_staged", "t_stored"))
        g0_rev, lmax_ready, gmax_ready, exp_in, exp_out = map(sem, (
            "g0_rev", "lmax_ready", "gmax_ready", "exp_in", "exp_out"))
        s0_ready, s0_weighted, s0_summed, s0_read, s0_posted = map(sem, (
            "s0_ready", "s0_weighted", "s0_summed", "s0_read", "s0_posted"))
        s0_used = [sem(f"s0_used{h}") for h in range(2)]
        f_rh, f_rhT, f_logits, f_softin, f_softout, f_gap, f_gapexp, f_w, f_wturned, f_wT = map(sem, (
            "f_rh", "f_rhT", "f_logits", "f_softin", "f_softout", "f_gap", "f_gapexp", "f_w", "f_wturned", "f_wT"))
        f_h1, f_h1T, f_h2, f_h2T, f_o, f_oread = map(sem, ("f_h1", "f_h1T", "f_h2", "f_h2T", "f_o", "f_oread"))
        wrel_done = sem("wrel_done")
        rw1_loaded = sem("rw1_loaded")
        h_turned, hT_ready = map(sem, ("h_turned", "hT_ready"))
        r_kept, r_lastT = map(sem, ("r_kept", "r_lastT"))
        r_rootread = [sem(f"r_rootread{l}") for l in range(2)]
        r_rootx, r_based, r_even, r_odd, r_evenout, r_oddout = [
            [sem(f"{n}{l}") for l in range(2)] for n in (
                "r_rootx", "r_based", "r_even", "r_odd", "r_evenout", "r_oddout")]
        r_stored = [[sem(f"r_stored{l}_{c}") for c in range(4)] for l in range(2)]
        e_index, e_ready, e_summed, e_read, e_var, e_std, e_posted = [
            [sem(f"{n}{l}") for l in range(2)] for n in (
                "e_index", "e_ready", "e_summed", "e_read", "e_var", "e_std", "e_posted")]
        got = [[sem(f"got{l}_{j}") for j in range(U)] for l in range(3)]
        used = [[sem(f"used{l}_{j}") for j in range(U)] for l in range(3)]
        x_logits, x_oh, x_ohturned, x_ohT, x_h, x_hT, x_o, x_oread, x_stored = map(sem, (
            "x_logits", "x_oh", "x_ohturned", "x_ohT", "x_h", "x_hT", "x_o", "x_oread", "x_stored"))
        dve_step, pool_step = map(sem, ("dve_step", "pool_step"))

        x_d = a["x"].rearrange("(t p) d -> p t d", p=P)
        gat_rows = gat_table.rearrange("(t p) c -> p t c", p=P)
        rel_rows = [rel_table[l].rearrange("(t p r) d -> p t (r d)", p=P, r=R) for l in range(2)]
        out_rows = out.rearrange("(t p) d -> p t d", p=P)
        small_loads = 6 + 2 * X0

        def walk(eng, t):
            w = eng.value_load(ranges[0:1, 0, bass.ds(t, 1)], min_val=0, max_val=(NT * GT + 1) * BEFORE - 1)
            return (nc.s_assert_within(eng.snap(w % TURNS), 0, ETP - U_MIN * U),
                    nc.s_assert_within(eng.snap(w // TURNS % (BEFORE // TURNS)), U_MIN, GT),
                    nc.s_assert_within(eng.snap(w // BEFORE), 0, NT * GT))

        def tile_of(lo, r):
            return nc.s_assert_within(lo + r * U, 0, ETP - U)

        def second_place(q):
            first, n = PARTS[1][0], PARTS[1][1] - PARTS[1][0]
            return nc.s_assert_within(q % 2 * n + first, first, first + n)

        def weigh(eng, lo, h, at):
            js = slice(*PARTS[h])
            n = PARTS[h][1] - PARTS[h][0]
            msgs = msg[:, bass.ds(lo, U), :]
            return eng.tensor_tensor(rhs0[:, bass.ds(at, n), 0:S0W - 1].rearrange("p j (h c) -> p j h c", h=HEADS),
                                     msgs[:, js, 0:F + 1].unsqueeze(2).broadcast_to([P, n, HEADS, F + 1]),
                                     msgs[:, js, F + 1:MW].unsqueeze(3).broadcast_to([P, n, HEADS, F + 1]),
                                     ALU.mult)

        block = ctx.enter_context(nc.Block())

        @block.sync
        def _(sp):
            def load(dst, src, done):
                sp.dma_start(dst, src).then_inc(done, 16)

            sp.nop().then_inc(t_stored, 16)
            for l in range(2):
                for c in range(4):
                    sp.nop().then_inc(r_stored[l][c], 16)
            sp.nop().then_inc(x_stored, 16)

            load(dstT, a["dst_rows"], meta_loaded)
            load(dst_i, a["dst_t"], meta_loaded)
            load(src_idx[:, 0:ETP], a["src_t"], meta_loaded)
            load(et_i, a["et_t"], meta_loaded)
            load(dir_e, a["dir_t"], meta_loaded)
            load(x_res[:, 0:G, :], x_d[:, 0:G, :], x_first)
            load(x_res[:, G:NT, :], x_d[:, G:NT, :], x_loaded)
            load(wcat[:, :, 0:F], a["wf_T"].rearrange("(k p) f -> p k f", p=P), gatw_loaded)
            load(wcat[:, :, C0:C0 + F], a["wr_T"].rearrange("(k p) f -> p k f", p=P), gatw_loaded)
            load(onehot[0:F, 0:2, :], a["wf"].rearrange("f (k n) -> f k n", k=2), gatw_loaded)
            load(onehot[0:F, 2:4, :], a["wr"].rearrange("f (k n) -> f k n", k=2), gatw_loaded)
            load(gat_ring[0:F, 0, 0:HEADS], a["attn_T"], gatw_loaded)
            load(ident[:, :], a["ident"], ident_loaded)
            for e in range(X0):
                for w, name in enumerate(("ew1", "ew2", "ew3")):
                    load(ew[e][w], a[name][e].rearrange("(k p) n -> p k n", p=P), ffn0_loaded)
            load(rb1[:, :], a["rb1"].rearrange("(p o) -> p o", o=1), small0_loaded)
            load(rw2[:, :], a["rw2"], small0_loaded)
            load(rb2[:, :], a["rb2"].partition_broadcast(P), small0_loaded)
            for e in range(X0):
                load(eb1[:, e, :], a["eb1T"][:, e, :], small0_loaded)
                load(eb2[:, e, :], a["eb2T"][:, e, :], small0_loaded)
            load(eb3[:, :], a["eb3"], small0_loaded)
            for l in range(2):
                load(att_bc[:, l, :], a[f"att{l}"].partition_broadcast(P), small0_loaded)

            with sp.Fori(0, NG) as g:
                sp.wait_ge(t_staged, g * 2 + 3)
                sp.dma_start(gat_rows[:, bass.ds(g * G, G), :], t0s).then_inc(t_stored, 16)
            sp.wait_ge(s0_posted, NT + 1)
            load(basis[0], a["basis0"].rearrange("b (k p) n -> p b k n", p=P), basis_loaded)
            load(rw1, a["rw1"].rearrange("(k p) n -> p k n", p=P), rw1_loaded)
            sp.wait_ge(f_oread, NG * 21 + 1)
            load(ea, a["ea_t"], rows_loaded)
            for l in range(2):
                for c, name in enumerate(("bias", "ln_g", "ln_b")):
                    load(rows_bc[:, l, c, :], a[f"{name}{l}"].partition_broadcast(P), rows_loaded)
                load(root[:, l, :, :], a[f"root{l}"].rearrange("(k p) n -> p k n", p=P), rows_loaded)
            load(basis[1], a["basis1"].rearrange("b (k p) n -> p b k n", p=P), basis_loaded)

            def store_rel(l):
                with sp.Fori(0, NT) as t:
                    for c in range(4):
                        sp.wait_ge(r_evenout[l], t * 4 + (c + 3))
                        sp.wait_ge(r_oddout[l], t * 4 + (c + 3))
                        sp.dma_start(rel_rows[l][:, bass.ds(t, 1), c * 1024:(c + 1) * 1024],
                                     stage[:, c * 1024:(c + 1) * 1024].unsqueeze(1)).then_inc(r_stored[l][c], 16)

            store_rel(0)
            store_rel(1)
            sp.wait_ge(r_based[1], NT + 1)
            load(xw1, a["xw1"].rearrange("(k p) n -> p k n", p=P), ffn1_loaded)
            load(xw2, a["xw2"].rearrange("(m p) n -> p m n", p=P), ffn1_loaded)
            load(negmask, a["negmask"], ffn1_loaded)
            load(xb2, a["xb2"], ffn1_loaded)
            load(rwT, a["rwT"].rearrange("(k p) n -> p k n", p=P), ffn1_loaded)
            load(rb, a["rb"].partition_broadcast(P), ffn1_loaded)
            load(xb1, a["xb1T"], ffn1_loaded)
            with sp.Fori(0, NG) as g:
                sp.wait_ge(x_oread, g * 3 + 4)
                sp.dma_start(out_rows[:, bass.ds(g * G, G), :], outs).then_inc(x_stored, 16)
            sp.wait_ge(x_stored, 16 * (NG + 1))

        @block.gpsimd
        def _(pool):
            pool.iota(iota_n[:, :], pattern=[[1, NT * P]], base=0, channel_multiplier=0).then_inc(consts_done, 1)
            pool.iota(iota_x[:, :], pattern=[[1, X1]], base=0, channel_multiplier=0,
                      allow_small_or_imprecise_dtypes=True).then_inc(consts_done, 1)
            pool.iota(tile_no[:, :], pattern=[[P, 4]], base=0, channel_multiplier=1,
                      allow_small_or_imprecise_dtypes=True).then_inc(consts_done, 1)
            pool.memset(zeros[:, :], 0.0).then_inc(consts_done, 1)
            pool.memset(pr[:, :, :], -1.0).then_inc(consts_done, 1)
            pool.wait_ge(bounds_ready, 1)
            pool.partition_all_reduce(xT5[:, 0, 0:2 * NT], xT5[:, 1, 0:2 * NT], P,
                                      bass.bass_isa.ReduceOp.max).then_inc(bounds_max, 1)

            def gather(l, j, table):
                pool.indirect_dma_start(
                    out=(gat_ring if l == 2 else rel_ring)[:, j, :], out_offset=None, in_=table,
                    in_offset=bass.IndirectOffsetOnAxis(ap=idx[:, j:j + 1], axis=0)).then_inc(got[l][j], 16)

            pool.wait_ge(meta_loaded, 5 * 16)
            pool.wait_ge(t_stored, 16 * (NG + 1))
            with pool.Fori(0, GT) as i:
                for j in range(U):
                    hold(pool, used[2][j], i + 1)
                    gather(2, j, gat_table)
            pool.wait_ge(lmax_ready, 1)
            pool.partition_all_reduce(gmx[:, :], mx[:, :], P, bass.bass_isa.ReduceOp.max).then_inc(gmax_ready, 1)

            pool.wait_ge(exp_out, 1)
            pool.wait_ge(ranges_done, 1)
            with pool.Fori(0, NT) as t:
                lo, cnt, q0 = walk(pool, t)
                with pool.Fori(0, cnt) as r:
                    hold(pool, s0_used[1], q0 + r + 1)
                    weigh(pool, tile_of(lo, r), 1, second_place(q0 + r)).then_inc(s0_weighted, 1)

            pool.wait_ge(small0_loaded, small_loads * 16)
            steps = Steps(pool, pool_step)
            for l in range(2):
                pool.wait_ge(basis_loaded, 16 * (l + 1))
                with pool.Fori(0, R) as r:
                    steps.enter(r, 2 * B - 1)
                    steps.step(pool.tensor_copy(att_cur[:, :], att_bc[:, l, bass.ds(r * B, B)]))
                    def product(o, b):
                        return pool.tensor_tensor(o, basis[l][:, b], att_cur[:, b:b + 1].unsqueeze(1)
                                                  .broadcast_to([P, 2, D]), ALU.mult)
                    steps.step(product(wacc[l][:, 0], 0))
                    for b in range(1, B):
                        steps.step(product(wacc[l][:, 1], b))
                        if b < B - 1:
                            steps.step(pool.tensor_tensor(wacc[l][:, 0], wacc[l][:, 0], wacc[l][:, 1], ALU.add))
                        else:
                            pool.tensor_tensor(wrel[l][:, :, bass.ds(r * D, D)], wacc[l][:, 0], wacc[l][:, 1],
                                               ALU.add).then_inc(wrel_done, 1)
                            hold(pool, wrel_done, r + (l * R + 1))
                steps.leave(R)

            for l in range(2):
                for c in range(4):
                    pool.wait_ge(r_stored[l][c], 16 * (NT + 1))
                pool.wait_ge(ranges_done, 1)
                with pool.Fori(0, NT) as t:
                    _, cnt, q0 = walk(pool, t)
                    with pool.Fori(0, cnt) as r:
                        for j in range(U):
                            hold(pool, e_index[l], (q0 + r) * U + (j + 1))
                            hold(pool, used[l][j], q0 + r + 1)
                            gather(l, j, rel_table[l])

        @block.scalar
        def _(act):
            for l in range(2):
                for j in range(U):
                    act.nop().then_inc(used[l][j], 1)
            for h in range(2):
                act.nop().then_inc(s0_used[h], 1 + h)
            for l in range(2):
                act.nop().then_inc(r_evenout[l], 2)
            act.nop().then_inc(r_lastT, 1)

            def std_group(k):
                hold(act, var_ready, k + 1)
                act.activation(std[:, :], veps[:, :], ACT.Sqrt).then_inc(std_ready, 1)

            def copy_turned(k, halves=(0, 2)):
                hold(act, turned, k + 2)
                for h in range(2):
                    act.activation(xT5[:, h, 0:512], bank[halves[h]][:, :], ACT.Copy)
                act.activation(xT5[:, :, 512:GN], bank[1][:, 0:256].rearrange("p (k n) -> p k n", k=2),
                               ACT.Copy).then_inc(xT_ready, 1)

            with act.Fori(0, NG) as g:
                std_group(g)
                copy_turned(g)
            act.wait_ge(meta_loaded, 5 * 16)
            with act.Fori(0, GT) as i:
                dirs = dir_e[:, bass.ds(i * U, U), :]
                for j in range(U):
                    hold(act, got[2][j], (i + 1) * 16)
                    act.activation(rev[:, j, :], gat_ring[:, j, C0:T0W], ACT.Copy,
                                   scale=dirs[:, j, 1:2]).then_inc(g0_rev, 1)
            act.wait_ge(exp_in, 1)
            act.activation(msg[:, :, F + 1:MW], msg[:, :, F + 1:MW], ACT.Exp).then_inc(exp_out, 1)
            with act.Fori(0, NT) as t:
                hold(act, s0_summed, t + 1)
                hold(act, s0_posted, t + 1)
                act.activation(sums0, bank[5][:, 0:S0W], ACT.Copy).then_inc(s0_read, 1)

            act.wait_ge(small0_loaded, small_loads * 16)
            std_group(NG)
            copy_turned(NG)
            with act.Fori(0, NG) as g:
                def h1_out(e):
                    for m in range(2):
                        for nb in range(2):
                            hold(act, f_h1, g * (X0 * 4) + (e * 4 + m * 2 + nb + 1))
                            act.activation(h1T[:, e % 2, m, nb * HB:(nb + 1) * HB], bank[nb][:, 0:HB],
                                           ACT.Relu, bias=eb1[:, e, m:m + 1]).then_inc(f_h1T, 1)

                def h2_out(e):
                    for m in range(2):
                        for nb in range(2):
                            hold(act, f_h2, g * (X0 * 4) + (e * 4 + m * 2 + nb + 1))
                            act.activation(h2T[:, e % 2, m, nb * HB:(nb + 1) * HB], bank[2 + nb][:, 0:HB],
                                           ACT.Relu, bias=eb2[:, e, m:m + 1]).then_inc(f_h2T, 1)

                for nb in range(2):
                    hold(act, f_rh, g * 2 + (nb + 1))
                    act.activation(rhT[:, nb * HB:(nb + 1) * HB], bank[6 + nb][:, 0:HB], ACT.Relu,
                                   bias=rb1[:, 0:1]).then_inc(f_rhT, 1)
                h1_out(0)
                hold(act, f_softin, g + 1)
                act.activation(lg[:, :, 0:X0], lg[:, :, 0:X0], ACT.Exp).then_inc(f_softout, 1)
                h1_out(1)
                hold(act, f_gap, g + 1)
                act.activation(gate[:, :, 1:2], gate[:, :, 0:1], ACT.Exp).then_inc(f_gapexp, 1)
                h2_out(0)
                hold(act, f_wturned, g + 1)
                act.activation(wT[:, 0:512], bank[6][0:X0, :], ACT.Copy)
                act.activation(wT[:, 512:GN], bank[7][0:X0, 0:P], ACT.Copy).then_inc(f_wT, 1)
                for e in range(2, X0):
                    h1_out(e)
                    h2_out(e - 1)
                std_group(g + (NG + 1))
                h2_out(X0 - 1)
                copy_turned(g + (NG + 1))

            def rel_groups():
                with act.Fori(0, NG) as g:
                    for j in range(G):
                        for c in range(4):
                            hold(act, r_even[0], g * (4 * G) + (j * 4 + c + 1))
                            hold(act, r_stored[0][c], g * (16 * G) + (j + 1) * 16)
                            act.activation(stage[:, c * 1024:c * 1024 + 512], bank[4 + 2 * (c % 2)][:, :],
                                           ACT.Copy).then_inc(r_evenout[0], 1)
                        if j == 1:
                            std_group(g + (2 * NG + 1))
                        if j == 3:
                            hold(act, turned, g + (2 * NG + 3))
                            act.activation(xT5[:, 0, 0:512], bank[0][:, :], ACT.Copy)
                            act.activation(xT5[:, 1, 0:512], bank[2][:, :], ACT.Copy).then_inc(xT_ready, 1)
                    hold(act, r_odd[0], g * (4 * G) + 4 * G)
                    act.activation(xT5[:, :, 512:GN], bank[1][:, 0:256].rearrange("p (k n) -> p k n", k=2),
                                   ACT.Copy).then_inc(r_lastT, 1)

            def edge_indices(l):
                def turn(lo, q=None):
                    idxs = src_idx[:, bass.ds(lo, U)]
                    for j in range(U):
                        if q is not None:
                            hold(act, got[l][j], q * 16)
                        act.activation(idx[:, j:j + 1], idxs[:, j:j + 1], ACT.Copy).then_inc(e_index[l], 1)

                def read_out(t):
                    hold(act, e_summed[l], t + 1)
                    hold(act, e_var[l], t + 1)
                    act.activation(mean, bank[0][:, 0:D], ACT.Copy,
                                   scale=rcnt[:, bass.ds(t, 1)]).then_inc(e_read[l], 1)

                def root_of_var(t):
                    hold(act, e_var[l], t + 2)
                    act.activation(e_root, e_veps, ACT.Sqrt).then_inc(e_std[l], 1)

                def turned_h(n):
                    hold(act, h_turned, n + 1)
                    act.activation(xT5[:, :, 0:P], bank[1][:, 0:D].rearrange("p (k n) -> p k n", k=2),
                                   ACT.Copy).then_inc(hT_ready, 1)

                def node_tile(t, then=None, end=None):
                    lo, cnt, q0 = walk(act, t)
                    turn(lo, nc.s_assert_within(q0, 1, NT * GT))
                    read_out(t - 1)
                    if then is not None:
                        then()
                    with act.Fori(1, cnt) as r:
                        turn(tile_of(lo, r), q0 + r)
                    root_of_var(t - 1)
                    if end is not None:
                        end()

                lo, cnt, _ = walk(act, 0)
                turn(lo)
                with act.Fori(1, cnt) as r:
                    turn(tile_of(lo, r), r)
                if l == 0:
                    node_tile(1)
                    with act.Fori(2, NT) as t:
                        node_tile(t, lambda: turned_h(t - 2))
                    read_out(NT - 1)
                    turned_h(NT - 2)
                    root_of_var(NT - 1)
                    turned_h(NT - 1)
                    return

                def x_root(g):
                    std_group(g + (3 * NG + 1))

                def x_turned(g):
                    copy_turned(g + (3 * NG + 1), (2, 3))

                def x_choice(g):
                    hold(act, x_ohturned, g + 1)
                    for o in (ohTb, ohT):
                        act.activation(o[:, 0:512], bank[3][0:X1, :], ACT.Copy)
                        act.activation(o[:, 512:GN], bank[1][0:X1, 256:384], ACT.Copy).then_inc(x_ohT, 1)

                def group(g):
                    node_tile(g * G + 1, end=lambda: x_root(g - 1))
                    node_tile(g * G + 2, then=lambda: x_turned(g - 1))
                    node_tile(g * G + 3, then=lambda: x_choice(g - 1))
                    node_tile(g * G + 4)

                with act.Fori(1, G + 1) as t:
                    node_tile(t)
                group(1)
                with act.Fori(2, NG) as g:
                    node_tile(g * G)
                    group(g)
                read_out(NT - 1)
                root_of_var(NT - 1)
                x_root(NG - 1)
                x_turned(NG - 1)
                x_choice(NG - 1)

            rel_groups()
            for l in range(2):
                edge_indices(l)

        @block.tensor
        def _(pe):
            def turn_group(k, wait=True, rows=xn5, halves=(0, 2)):
                hold(pe, xn_ready, k + 1)
                for j in range(G):
                    for h in range(2):
                        o = bank[halves[h]][:, j * P:(j + 1) * P] if j < 4 else bank[1][:, h * P:(h + 1) * P]
                        last = pe.transpose(o, rows[:, j, h * P:(h + 1) * P], ident[:, :])
                last.then_inc(turned, 1)
                if wait:
                    hold(pe, xT_ready, k + 1)

            def zero_product(dst, width, start):
                return pe.matmul(dst[:, 0:width], zeros[:, 0:P], zeros[:, 0:width], start=start, stop=not start,
                                 skip_group_check=True)

            pe.wait_ge(gatw_loaded, 5 * 16)
            for d in range(2):
                for k in range(2):
                    last = pe.matmul(bank[5][:, (d * 2 + k) * HEADS:(d * 2 + k + 1) * HEADS],
                                     onehot[0:F, 2 * d + k, :], gat_ring[0:F, 0, 0:HEADS], start=True, stop=True)
            last.then_inc(attw_done, 1)
            pe.wait_ge(ident_loaded, 16)
            pe.wait_ge(wcat_done, 1)
            with pe.Fori(0, NG) as g:
                turn_group(g)
                hold(pe, t_staged, g * 2 + 1)
                for half, tiles in ((0, (0, 1, 2)), (1, (3, 4))):
                    for i, j in enumerate(tiles):
                        for k in range(2):
                            last = pe.matmul(bank[3 + half][:, i * T0W:(i + 1) * T0W],
                                             xT5[:, k, j * P:(j + 1) * P], wcat[:, k, :],
                                             start=(k == 0), stop=(k == 1))
                    last.then_inc(t_product, 1)
            pe.wait_ge(consts_done, 5)
            pe.wait_ge(ranges_done, 1)
            with pe.Fori(0, NT) as t:
                _, cnt, q0 = walk(pe, t)
                hold(pe, s0_read, t + 1)
                zero_product(bank[5], S0W, True)
                with pe.Fori(0, cnt) as r:
                    for h in range(2):
                        hold(pe, s0_ready, (q0 + r) * 2 + (h + 1))
                        if h == 1:
                            hold(pe, s0_weighted, q0 + r + 1)
                        rows = rhs0[:, bass.ds(0 if h == 0 else second_place(q0 + r), PARTS[h][1] - PARTS[h][0]), :]
                        for j in range(*PARTS[h]):
                            last = pe.matmul(bank[5][:, 0:S0W], onehot[:, j, :], rows[:, j - PARTS[h][0], 0:S0W],
                                             start=False, stop=False, skip_group_check=True)
                        last.then_inc(s0_used[h], 1)
                zero_product(bank[5], S0W, False).then_inc(s0_summed, 1)

            pe.wait_ge(ffn0_loaded, X0 * 3 * 16)
            pe.wait_ge(small0_loaded, small_loads * 16)
            pe.wait_ge(rw1_loaded, 16)
            turn_group(NG)
            with pe.Fori(0, NG) as g:
                def h1_product(e):
                    for m in range(2):
                        for nb in range(2):
                            u = e * 4 + m * 2 + nb
                            if u >= 2:
                                hold(pe, f_h1T, g * (X0 * 4) + (u - 1))
                            for k in range(2):
                                last = pe.matmul(bank[nb][:, 0:HB], ew[e][0][:, k, m * P:(m + 1) * P],
                                                 xT5[:, k, nb * HB:(nb + 1) * HB], start=(k == 0), stop=(k == 1))
                            last.then_inc(f_h1, 1)

                def h2_product(e):
                    hold(pe, f_h1T, g * (X0 * 4) + (e * 4 + 4))
                    for m in range(2):
                        for nb in range(2):
                            u = e * 4 + m * 2 + nb
                            if u >= 2:
                                hold(pe, f_h2T, g * (X0 * 4) + (u - 1))
                            for k in range(2):
                                last = pe.matmul(bank[2 + nb][:, 0:HB], ew[e][1][:, k, m * P:(m + 1) * P],
                                                 h1T[:, e % 2, k, nb * HB:(nb + 1) * HB],
                                                 start=(k == 0), stop=(k == 1))
                            last.then_inc(f_h2, 1)

                def o_unit(e, pair, product):
                    u = (e + 1) * 3 + pair
                    hold(pe, f_oread, g * 21 + (max(u - 1, 0) + 1))
                    for i, j in enumerate(range(2 * pair, min(2 * pair + 2, G))):
                        last = product(bank[4 + u % 2][:, i * D:(i + 1) * D], j)
                    last.then_inc(f_o, 1)

                def o_product(e):
                    hold(pe, f_h2T, g * (X0 * 4) + (e * 4 + 4))

                    def product(o, j):
                        for k in range(2):
                            last = pe.matmul(o, h2T[:, e % 2, k, j * P:(j + 1) * P], ew[e][2][:, k, :],
                                             start=(k == 0), stop=(k == 1))
                        return last
                    for pair in range(3):
                        o_unit(e, pair, product)

                hold(pe, xT_ready, g + (NG + 1))
                for nb in range(2):
                    for k in range(2):
                        last = pe.matmul(bank[6 + nb][:, 0:HB], rw1[:, k, :], xT5[:, k, nb * HB:(nb + 1) * HB],
                                         start=(k == 0), stop=(k == 1))
                    last.then_inc(f_rh, 1)
                hold(pe, f_rhT, g * 2 + 2)
                for j in range(G):
                    last = pe.matmul(bank[3][:, j * 8:j * 8 + X0], rhT[:, j * P:(j + 1) * P], rw2[:, :],
                                     start=True, stop=True)
                last.then_inc(f_logits, 1)
                h1_product(0)
                h1_product(1)
                hold(pe, f_softin, g + 1)
                h2_product(0)
                hold(pe, f_w, g + 1)
                for j in range(G):
                    o = bank[6][0:X0, j * P:(j + 1) * P] if j < 4 else bank[7][0:X0, 0:P]
                    last = pe.transpose(o, wsel[:, 0, j, :], ident[:, :])
                last.then_inc(f_wturned, 1)
                hold(pe, f_wT, g + 1)
                for pair in range(3):
                    o_unit(-1, pair, lambda o, j: pe.matmul(o, wT[:, j * P:(j + 1) * P], eb3[:, :],
                                                            start=True, stop=True))
                for e in range(2, X0):
                    h1_product(e)
                    h2_product(e - 1)
                    o_product(e - 2)
                h2_product(X0 - 1)
                hold(pe, f_h2T, g * (X0 * 4) + (X0 * 4 - 1))
                turn_group(g + (NG + 1), wait=False)
                o_product(X0 - 2)
                o_product(X0 - 1)

            def rel_root(l, n, j):
                hold(pe, r_rootread[l], n + 1)
                for k in range(2):
                    last = pe.matmul(bank[3][:, 0:D], xT5[:, k, j * P:(j + 1) * P], root[:, l, k, :],
                                     start=(k == 0), stop=(k == 1))
                last.then_inc(r_rootx[l], 1)

            def rel_unit(l, n, j, u):
                out_of, done = ((r_evenout[l], r_even[l]), (r_oddout[l], r_odd[l]))[u % 2]
                hold(pe, out_of, n * 4 + (u // 2 + 1))
                for k in range(2):
                    last = pe.matmul(bank[4 + u % 4][:, :], xT5[:, k, j * P:(j + 1) * P],
                                     wrel[l][:, k, u * 512:(u + 1) * 512], start=(k == 0), stop=(k == 1))
                last.then_inc(done, 1)

            def rel_groups():
                with pe.Fori(0, NG) as g:
                    hold(pe, xT_ready, g + (2 * NG + 1))
                    for j in range(G):
                        if j == G - 1:
                            hold(pe, r_lastT, g + 1)
                        rel_root(0, g * G + j, j)
                        for u in range(8):
                            rel_unit(0, g * G + j, j, u)
                        if j == G - 2:
                            turn_group(g + (2 * NG + 1), wait=False)
                pe.wait_ge(xT_ready, 3 * NG + 1)
                pe.wait_ge(r_lastT, NG + 1)

            def turn_h(n):
                hold(pe, e_posted[0], n + 1)
                for k in range(2):
                    last = pe.transpose(bank[1][:, k * P:(k + 1) * P], h_row[:, k * P:(k + 1) * P], ident[:, :])
                last.then_inc(h_turned, 1)

            def edge_sums(l):
                def edge_tile(q, j):
                    hold(pe, e_ready[l], q * U + (j + 1))
                    hold(pe, got[l][j], q * 16 + 16)
                    pe.matmul(bank[0][:, 0:D], onehot[:, j, :], rel_ring[:, j, :], start=False, stop=False,
                              skip_group_check=True).then_inc(used[l][j], 1)

                def opened(t):
                    hold(pe, e_read[l], t + 1)
                    zero_product(bank[0], D, True)

                def turns(first, cnt, q0):
                    with pe.Fori(first, cnt) as r:
                        for j in range(U):
                            edge_tile(q0 + r, j)

                def node_tile(t, start=None, at=None):
                    if start is not None:
                        start()
                    _, cnt, q0 = walk(pe, t)
                    opened(t)
                    if at is None:
                        turns(0, cnt, q0)
                    else:
                        for i in range(2 * U):
                            edge_tile(q0 + i // U, i % U)
                            at(i)
                        turns(2, cnt, q0)
                    zero_product(bank[0], D, False).then_inc(e_summed[l], 1)

                node_tile(0)
                if l == 0:
                    def rel_part(n, i):
                        if i == 0:
                            hold(pe, hT_ready, n + 1)
                            rel_root(1, n, 0)
                        elif i % 2 == 1:
                            rel_unit(1, n, 0, i // 2)

                    def rel_end(n):
                        rel_unit(1, n, 0, 6)
                        rel_unit(1, n, 0, 7)

                    def rel_start(n):
                        rel_end(n - 1)
                        turn_h(n)

                    node_tile(1)
                    node_tile(2, lambda: turn_h(0), lambda i: rel_part(0, i))
                    with pe.Fori(3, NT) as t:
                        node_tile(t, lambda: rel_start(t - 2), lambda i: rel_part(t - 2, i))
                    rel_end(NT - 3)
                    for n in (NT - 2, NT - 1):
                        turn_h(n)
                        for i in range(2 * U):
                            rel_part(n, i)
                        rel_end(n)
                    return

                def x_turn(g):
                    hold(pe, x_oread, g * 3 + 1)
                    turn_group(g + (3 * NG + 1), wait=False, rows=xn_x, halves=(2, 3))

                def x_router(g):
                    hold(pe, xT_ready, g + (3 * NG + 2))
                    for j in range(G):
                        for k in range(2):
                            last = pe.matmul(bank[7][:, j * X1:(j + 1) * X1], xT5[:, k, j * P:(j + 1) * P],
                                             rwT[:, k, :], start=(k == 0), stop=(k == 1))
                    last.then_inc(x_logits, 1)

                def x_choice(g):
                    hold(pe, x_oh, g + 1)
                    for j in range(G):
                        o = bank[3][0:X1, j * P:(j + 1) * P] if j < 4 else bank[1][0:X1, 256:384]
                        last = pe.transpose(o, oh[:, j, :], ident[:, :])
                    last.then_inc(x_ohturned, 1)

                def x_hidden(g, first, units):
                    if first == 0:
                        hold(pe, x_ohT, g * 2 + 1)
                    for u in range(first, first + units):
                        m, nb = u // 2, u % 2
                        if u >= 3:
                            hold(pe, x_hT, g * (2 * M1) + (u - 2))
                        o = bank[4 + u % 3][:, 0:HB]
                        for k in range(2):
                            pe.matmul(o, xw1[:, k, m * P:(m + 1) * P], xT5[:, k, nb * HB:(nb + 1) * HB],
                                      start=(k == 0), stop=False)
                        pe.matmul(o, negmask[:, m * P:(m + 1) * P], ohTb[:, nb * HB:(nb + 1) * HB],
                                  start=False, stop=True).then_inc(x_h, 1)

                def x_out(g, first, count):
                    for i in range(first, min(first + count, G * (M1 + 1))):
                        j, m = i // (M1 + 1), i % (M1 + 1) - 1
                        if i == 0:
                            hold(pe, x_ohT, g * 2 + 2)
                            hold(pe, x_hT, g * (2 * M1) + 2 * M1)
                        if j == 4 and m < 0:
                            hold(pe, x_oread, g * 3 + 2)
                        o = bank[3 + 4 * (j // 2 % 2)][:, (j % 2) * D:(j % 2 + 1) * D]
                        if m < 0:
                            last = pe.matmul(o, ohT[:, j * P:(j + 1) * P], xb2, start=True, stop=False)
                        else:
                            last = pe.matmul(o, hmT[m][:, j * P:(j + 1) * P], xw2[:, m, :],
                                             start=False, stop=(m == M1 - 1))
                        if m == M1 - 1 and j in (1, 3, 4):
                            last.then_inc(x_o, 1)

                def group(g, outs):
                    node_tile(g * G + 1, start=(lambda: x_out(g - 2, 48, 8)) if outs else None,
                              at=(lambda i: x_out(g - 2, 56 + i * 3, 3)) if outs else None)
                    node_tile(g * G + 2, start=lambda: x_turn(g - 1), at=lambda i: x_router(g - 1) if i == U else None)
                    node_tile(g * G + 3, start=lambda: x_choice(g - 1),
                              at=lambda i: x_hidden(g - 1, i - 1 + max(i - 9, 0), 1 + (i >= 9)) if i >= 1 else None)
                    node_tile(g * G + 4, start=lambda: x_hidden(g - 1, 14, 3), at=lambda i: x_hidden(g - 1, 17 + i, 1))

                with pe.Fori(1, G + 1) as t:
                    node_tile(t)
                pe.wait_ge(ffn1_loaded, 7 * 16)
                group(1, False)
                with pe.Fori(2, NG) as g:
                    node_tile(g * G, start=lambda: x_hidden(g - 2, 29, 3), at=lambda i: x_out(g - 2, i * 4, 4))
                    group(g, True)
                x_hidden(NG - 2, 29, 3)
                x_out(NG - 2, 0, G * (M1 + 1))
                x_turn(NG - 1)
                x_router(NG - 1)
                x_choice(NG - 1)
                x_hidden(NG - 1, 0, 2 * M1)
                x_out(NG - 1, 0, G * (M1 + 1))

            pe.wait_ge(wrel_done, R)
            pe.wait_ge(rows_loaded, 9 * 16)
            rel_groups()
            pe.wait_ge(wrel_done, 2 * R)
            for l in range(2):
                edge_sums(l)

        @block.vector
        def _(dve):
            steps = Steps(dve, dve_step)
            v = dve
            for one in (t_staged, turned, s0_read, s0_posted, f_oread, r_based[0], r_based[1], e_read[0], e_read[1],
                        e_var[0], e_var[1], x_oread, r_rootread[0], r_rootread[1]):
                v.nop().then_inc(one, 1)
            for l in range(2):
                v.nop().then_inc(r_oddout[l], 2)

            def norm_stats(g):
                for j in range(G):
                    last = v.bn_stats(stats[:, j, :], x_res[:, bass.ds(g * G + j, 1), :].rearrange("p o d -> p (o d)"))
                steps.step(last)
                for j in range(G):
                    last = v.bn_aggr(mv[:, j, :], stats[:, j, :])
                steps.step(last)
                v.tensor_scalar(veps[:, :], mv[:, :, 1], EPS, None, ALU.add).then_inc(var_ready, 1)

            def norm_rows(g, k, rows=xn5):
                hold(v, turned, k + 1)
                hold(v, std_ready, k + 1)
                steps.step(v.reciprocal(rstd[:, :], std[:, :]))
                for j in range(G):
                    last = v.tensor_scalar(rows[:, j, :], x_res[:, bass.ds(g * G + j, 1), :].rearrange(
                        "p o d -> p (o d)"), mv[:, j, 0:1], rstd[:, j:j + 1], ALU.subtract, ALU.mult)
                last.then_inc(xn_ready, 1)

            def norm_group(g, k):
                norm_stats(g)
                norm_rows(g, k)

            v.wait_ge(meta_loaded, 5 * 16)
            v.wait_ge(consts_done, 5)
            tmp = xn5[:, :, :].rearrange("p t d -> p (t d)")
            emin, emax = tmp[:, 0:4], tmp[:, 4:8]
            c1 = tmp[:, 130:230].rearrange("p (n j) -> p n j", j=4)
            c2 = tmp[:, 230:330].rearrange("p (n j) -> p n j", j=4)
            c3 = tmp[:, 330:430].rearrange("p (n j) -> p n j", j=4)
            up = xT5[:, 1, 0:2 * NT]
            m2 = xT5[:, 0, 0:2 * NT]
            first = iota_n[:, :].rearrange("p (n q) -> p n q", q=P)[:, :, 0:1].broadcast_to([P, NT, 4])

            def row(x):
                return x.unsqueeze(1).broadcast_to([P, NT, 4])
            steps.step(v.tensor_reduce(emin, dstT, AX.X, ALU.min))
            steps.step(v.tensor_reduce(emax, dstT, AX.X, ALU.max))
            steps.step(v.tensor_scalar(emin, emin, float(P - 1), None, ALU.subtract))
            steps.step(v.tensor_tensor(c1, row(emin), first, ALU.is_le))
            steps.step(v.tensor_tensor(c2, row(emax), first, ALU.is_ge))
            steps.step(v.tensor_tensor(c1, c1, c2, ALU.mult))
            steps.step(v.tensor_scalar(tmp[:, 8:12], tile_no[:, :], -1.0, float(ET), ALU.mult, ALU.add))
            steps.step(v.tensor_scalar(tmp[:, 12:16], tile_no[:, :], 1.0, None, ALU.add))
            steps.step(v.tensor_tensor(c2, c1, row(tmp[:, 8:12]), ALU.mult))
            steps.step(v.tensor_tensor(c3, c1, row(tmp[:, 12:16]), ALU.mult))
            v.tensor_reduce(up[:, 0:NT], c2, AX.X, ALU.max)
            v.tensor_reduce(up[:, NT:2 * NT], c3, AX.X, ALU.max).then_inc(bounds_ready, 1)
            v.wait_ge(bounds_max, 1)
            lo_f, cnt_f = tmp[:, 20:45], tmp[:, 45:70]
            cnt_i = tmp[:, 70:95].bitcast(I32)
            steps.step(v.tensor_scalar(lo_f, m2[:, 0:NT], -1.0, float(ET), ALU.mult, ALU.add))
            steps.step(v.scalar_tensor_tensor(cnt_i, m2[:, NT:2 * NT], float(U - 1), lo_f, ALU.add, ALU.subtract))
            steps.step(v.tensor_scalar(cnt_i, cnt_i, float(65536 // U + 1), None, ALU.mult))
            steps.step(v.tensor_scalar(cnt_i, cnt_i, 16, None, ALU.arith_shift_right))
            steps.step(v.tensor_scalar(cnt_f, cnt_i, float(U_MIN), None, ALU.max))
            steps.step(v.tensor_scalar(tmp[:, 95:95 + NT], cnt_f, -float(U), float(ETP), ALU.mult, ALU.add))
            steps.step(v.tensor_tensor(ranges[:, 0, :], lo_f, tmp[:, 95:95 + NT], ALU.min))
            steps.step(v.tensor_copy(ranges[:, 1, :], cnt_f))
            sums = [tmp[:, 430:455], tmp[:, 455:480]]
            steps.step(v.memset(sums[0][:, 0:1], 0.0))
            steps.step(v.tensor_copy(sums[0][:, 1:NT], cnt_f[:, 0:NT - 1]))
            d, cur = 1, 0
            while d < NT:
                steps.step(v.tensor_copy(sums[1 - cur][:, 0:d], sums[cur][:, 0:d]))
                steps.step(v.tensor_tensor(sums[1 - cur][:, d:NT], sums[cur][:, d:NT], sums[cur][:, 0:NT - d],
                                           ALU.add))
                d, cur = 2 * d, 1 - cur
            steps.step(v.tensor_copy(ranges[:, 2, :], sums[cur]))
            for row, at in ((1, TURNS), (2, BEFORE)):
                steps.step(v.tensor_scalar(ranges[:, row, :], ranges[:, row, :], at.bit_length() - 1, None,
                                           ALU.logical_shift_left))
            steps.step(v.tensor_tensor(ranges[:, 0, :], ranges[:, 0, :], ranges[:, 1, :], ALU.bitwise_or))
            v.tensor_tensor(ranges[:, 0, :], ranges[:, 0, :], ranges[:, 2, :], ALU.bitwise_or).then_inc(ranges_done, 1)
            v.wait_ge(ranges_done, 1)
            v.memset(src_idx[:, ETP:ETP + U], 0)
            v.tensor_copy(dst_f[:, :], dst_i).then_inc(dst_done, 1)
            v.wait_ge(dst_done, 1)

            v.wait_ge(attw_done, 1)
            for d in range(2):
                for k in range(2):
                    last = v.tensor_copy(wcat[:, k, d * C0 + F:(d + 1) * C0],
                                         bank[5][:, (d * 2 + k) * HEADS:(d * 2 + k + 1) * HEADS])
            last.then_inc(wcat_done, 1)
            v.wait_ge(x_first, 16)
            def stage_table(g):
                hold(v, t_stored, (g + 1) * 16)
                hold(v, t_product, g * 2 + 1)
                v.tensor_copy(t0s[:, 0:3, :], bank[3][:, 0:3 * T0W].rearrange("p (j c) -> p j c", c=T0W))\
                    .then_inc(t_staged, 1)
                hold(v, t_product, g * 2 + 2)
                v.tensor_copy(t0s[:, 3:5, :], bank[4][:, 0:2 * T0W].rearrange("p (j c) -> p j c", c=T0W))\
                    .then_inc(t_staged, 1)

            norm_group(0, 0)
            v.wait_ge(x_loaded, 16)
            with v.Fori(0, NG - 1) as g:
                steps.enter(g, 3)
                norm_group(g + 1, g + 1)
                stage_table(g)
            steps.leave(NG - 1)
            stage_table(NG - 1)
            v.memset(msg[:, :, F:F + 1], 1.0)
            v.wait_ge(t_stored, (NG + 1) * 16)
            v.wait_ge(wcat_done, 1)
            for j in range(U):
                v.tensor_copy(idx[:, j:j + 1], src_idx[:, j:j + 1]).then_inc(used[2][j], 1)
            with v.Fori(0, GT) as i:
                next_idx = src_idx[:, bass.ds(i * U + U, U)]
                msgs = msg[:, bass.ds(i * U, U), :]
                dirs = dir_e[:, bass.ds(i * U, U), :]
                for j in range(U):
                    hold(v, g0_rev, i * U + (j + 1))
                    v.scalar_tensor_tensor(msgs[:, j, 0:F], gat_ring[:, j, 0:F], dirs[:, j, 0:1], rev[:, j, 0:F],
                                           ALU.mult, ALU.add)
                    v.scalar_tensor_tensor(msgs[:, j, F + 1:MW], gat_ring[:, j, F:C0], dirs[:, j, 0:1], rev[:, j, F:C0],
                                           ALU.mult, ALU.add)
                    v.tensor_copy(idx[:, j:j + 1], next_idx[:, j:j + 1]).then_inc(used[2][j], 1)
            for j in range(U):
                v.wait_ge(used[2][j], GT + 1)
            steps.step(v.scalar_tensor_tensor(src_idx[:, 0:ETP], src_idx[:, 0:ETP], float(R), et_i,
                                              ALU.mult, ALU.add))
            v.memset(rhs0[:, :, S0W - 1:S0W], 1.0)
            scores = msg[:, :, F + 1:MW]
            v.tensor_reduce(mx[:, :], scores.rearrange("p t h -> p h t"), AX.X, ALU.max).then_inc(lmax_ready, 1)
            v.wait_ge(lmax_ready, 1)
            steps.step(v.scalar_tensor_tensor(scores, scores, 0.2, scores, ALU.mult, ALU.max))
            v.wait_ge(gmax_ready, 1)
            steps.step(v.scalar_tensor_tensor(glr[:, :], gmx[:, :], 0.2, gmx[:, :], ALU.mult, ALU.max))
            v.tensor_tensor(scores, scores, glr[:, :].unsqueeze(1).broadcast_to([P, GT * U, HEADS]),
                            ALU.subtract).then_inc(exp_in, 1)
            v.wait_ge(exp_out, 1)
            heads = sums0[:, 0:S0W - 1].rearrange("p (h c) -> p h c", h=HEADS)

            def gat_turn(nodes, lo, q):
                targets = dst_f[:, bass.ds(lo, U)]
                q = v.snap(q)
                for h in range(2):
                    hold(v, s0_used[h], q + 1 + h)
                    for j in range(*PARTS[h]):
                        last = v.tensor_scalar(onehot[:, j, :], nodes, targets[:, j:j + 1], None, ALU.is_equal)
                    if h == 0:
                        last = weigh(v, lo, 0, 0)
                    last.then_inc(s0_ready, 1)

            def gat_out(t):
                hold(v, s0_read, t + 2)
                v.tensor_scalar(den[:, 0:HEADS], heads[:, :, F], 1e-10, None, ALU.add)
                steps.step(v.tensor_scalar(den[:, HEADS:HEADS + 1], sums0[:, S0W - 1:S0W], 1.0, None, ALU.add))
                steps.step(v.reciprocal(rden[:, :], den[:, :]))
                v.tensor_copy(rcnt[:, bass.ds(t, 1)], rden[:, HEADS:HEADS + 1])
                xt = x_res[:, bass.ds(t, 1), :].rearrange("p o d -> p (o d)")
                for h in range(HEADS):
                    last = v.scalar_tensor_tensor(xt[:, h * F:(h + 1) * F], heads[:, h, 0:F], rden[:, h:h + 1],
                                                  xt[:, h * F:(h + 1) * F], ALU.mult, ALU.add)
                last.then_inc(s0_posted, 1)

            lo, cnt, q0 = walk(v, 0)
            with v.Fori(0, cnt) as r:
                gat_turn(iota_n[:, 0:P], tile_of(lo, r), q0 + r)
            with v.Fori(1, NT) as t:
                steps.enter(t - 1, 2)
                lo, cnt, q0 = walk(v, t)
                nodes = iota_n[:, bass.ds(t * P, P)]
                gat_turn(nodes, lo, q0)
                gat_out(t - 1)
                with v.Fori(1, cnt) as r:
                    gat_turn(nodes, tile_of(lo, r), q0 + r)
            steps.leave(NT - 1)
            gat_out(NT - 1)
            v.wait_ge(s0_posted, NT + 1)

            v.wait_ge(small0_loaded, small_loads * 16)
            norm_group(0, NG)
            with v.Fori(0, NG) as g:
                steps.enter(g, 18)

                def o_read(e):
                    for pair in range(3):
                        u = (e + 1) * 3 + pair
                        hold(v, f_o, g * 21 + (u + 1))
                        if e >= 0:
                            hold(v, f_oread, g * 21 + (u - 1))
                        js = range(2 * pair, min(2 * pair + 2, G))
                        if e < 0:
                            xs = x_res[:, bass.ds(g * G + js[0], len(js)), :].rearrange("p t d -> p (t d)")
                            last = v.tensor_tensor(xs, bank[4 + u % 2][:, 0:len(js) * D], xs, ALU.add)
                        else:
                            xs = x_res[:, bass.ds(g * G + js[0], len(js)), :]
                            for i, j in enumerate(js):
                                last = v.scalar_tensor_tensor(
                                    xs[:, i, :], bank[4 + u % 2][:, i * D:(i + 1) * D],
                                    wsel[:, 0, j, e:e + 1], xs[:, i, :], ALU.mult, ALU.add)
                        last.then_inc(f_oread, 1)

                def each(x, n):
                    return x.broadcast_to([P, G, n])

                hold(v, f_logits, g + 1)
                steps.step(v.tensor_tensor(
                    lg[:, :, 0:X0], bank[3][:, 0:G * 8].rearrange("p (j c) -> p j c", c=8)[:, :, 0:X0],
                    rb2[:, :].unsqueeze(1).broadcast_to([P, G, X0]), ALU.add))
                steps.step(v.tensor_reduce(gate[:, :, 2:3].rearrange("p t o -> p (t o)"), lg[:, :, 0:X0],
                                           AX.X, ALU.max))
                v.tensor_tensor(lg[:, :, 0:X0], lg[:, :, 0:X0], each(gate[:, :, 2:3], X0),
                                ALU.subtract).then_inc(f_softin, 1)
                hold(v, f_softout, g + 1)
                steps.step(v.tensor_reduce(gate[:, :, 3:4].rearrange("p t o -> p (t o)"), lg[:, :, 0:X0],
                                           AX.X, ALU.add))
                steps.step(v.reciprocal(gate[:, :, 2:3], gate[:, :, 3:4]))
                steps.step(v.tensor_tensor(pr[:, :, 0:X0], lg[:, :, 0:X0], each(gate[:, :, 2:3], X0), ALU.mult))
                for j in range(G):
                    last = v.max(top[:, j, :], pr[:, j, :])
                steps.step(last)
                v.tensor_tensor(gate[:, :, 0:1], top[:, :, 1:2], top[:, :, 0:1], ALU.subtract).then_inc(f_gap, 1)
                for j in range(G):
                    last = v.max_index(topi[:, j, :], top[:, j, :], pr[:, j, :])
                steps.step(last)
                steps.step(v.tensor_copy(idxf[:, :, :], topi[:, :, 0:2]))
                hold(v, f_gapexp, g + 1)
                steps.step(v.tensor_scalar(gate[:, :, 2:3], gate[:, :, 1:2], 1.0, None, ALU.add))
                steps.step(v.reciprocal(gate[:, :, 2:3], gate[:, :, 2:3]))
                steps.step(v.tensor_tensor(gate[:, :, 3:4], gate[:, :, 1:2], gate[:, :, 2:3], ALU.mult))
                for c in range(2):
                    steps.step(v.tensor_tensor(
                        wsel[:, c], iota_x[:, 0:X0].unsqueeze(1).broadcast_to([P, G, X0]),
                        each(idxf[:, :, c:c + 1], X0), ALU.is_equal))
                    steps.step(v.tensor_tensor(wsel[:, c], wsel[:, c], each(gate[:, :, 2 + c:3 + c], X0), ALU.mult))
                v.tensor_tensor(wsel[:, 0], wsel[:, 0], wsel[:, 1], ALU.add).then_inc(f_w, 1)
                hold(v, f_w, g + 1)
                for e in range(-1, X0):
                    if e == X0 - 2:
                        norm_group((g + 1) % NG, g + (NG + 1))
                    o_read(e)
            steps.leave(NG)
            v.wait_ge(f_oread, NG * 21 + 1)

            lgb = onehot[:, 0:2, :].rearrange("p a b -> p (a b)")

            def rel_root(l, n, row, out):
                hold(v, r_rootx[l], n + 1)
                hold(v, r_based[l], n + 1)
                steps.step(v.tensor_tensor(out, bank[3][:, 0:D], row, ALU.add))
                v.tensor_tensor(out, out, rows_bc[:, l, 0, :], ALU.add).then_inc(r_rootread[l], 1)
                hold(v, r_rootread[l], n + 2)

            def rel_columns(l, n, u, rooted):
                c, half = u // 2, u % 2
                hold(v, (r_even, r_odd)[half][l], n * 4 + (c + 1))
                hold(v, r_stored[l][c], n * 16 + 16)
                b = bank[4 + u % 4]
                if u == 7:
                    v.scalar_tensor_tensor(
                        base[:, bass.ds(n, 1), :].rearrange("p o d -> p (o d)"), b[:, D:2 * D],
                        rcnt[:, bass.ds(n, 1)], rooted, ALU.mult, ALU.add).then_inc(r_based[l], 1)
                v.tensor_copy(stage[:, c * 1024 + half * 512:c * 1024 + (half + 1) * 512], b[:, :])\
                    .then_inc((r_evenout, r_oddout)[half][l], 1)

            def rel_groups():
                with v.Fori(0, NG) as g:
                    steps.enter(g, 3 + G)
                    hold(v, xn_ready, g + (2 * NG + 1))
                    v.tensor_copy(base[:, bass.ds(g * G, G), :], xn5[:, :, :]).then_inc(r_kept, 1)
                    hold(v, r_kept, g + 1)
                    for j in range(G):
                        rel_root(0, g * G + j, base[:, bass.ds(g * G + j, 1), :].rearrange("p o d -> p (o d)"), lgb)
                        for u in (1, 3, 5, 7):
                            rel_columns(0, g * G + j, u, lgb)
                        if j == 1:
                            norm_stats((g + 1) % NG)
                        if j == 2:
                            norm_rows((g + 1) % NG, g + (2 * NG + 1))
                steps.leave(NG)
                v.wait_ge(r_based[0], NT + 1)

            def edge_sums(l):
                y, z = xn5[:, 1, :], xn5[:, 2, :]

                def turn(nodes, lo, q, between=None):
                    targets = dst_f[:, bass.ds(lo, U)]
                    weights = ea[:, bass.ds(lo, U)]
                    for j in range(U):
                        hold(v, used[l][j], q + 1)
                        v.tensor_scalar(onehot[:, j, :], nodes, targets[:, j:j + 1], weights[:, j:j + 1],
                                        ALU.is_equal, ALU.mult).then_inc(e_ready[l], 1)
                        if between is not None:
                            between(j)

                def variance(t):
                    hold(v, e_read[l], t + 2)
                    steps.step(v.tensor_tensor(y, mean, base[:, bass.ds(t, 1), :].rearrange("p o d -> p (o d)"),
                                               ALU.add))
                    steps.step(v.bn_stats(e_stats, y))
                    steps.step(v.bn_aggr(e_mv, e_stats))
                    v.tensor_scalar(e_veps, e_mv[:, 1:2], EPS, None, ALU.add).then_inc(e_var[l], 1)

                def norm(t):
                    hold(v, e_std[l], t + 1)
                    steps.step(v.reciprocal(e_rstd, e_root))
                    steps.step(v.tensor_scalar(z, y, e_mv[:, 0:1], e_rstd, ALU.subtract, ALU.mult))
                    steps.step(v.tensor_tensor(z, z, rows_bc[:, l, 1, :], ALU.mult))
                    steps.step(v.tensor_tensor(z, z, rows_bc[:, l, 2, :], ALU.add))
                    if l == 0:
                        if not isinstance(t, int) or t > 0:
                            hold(v, h_turned, t)
                        v.tensor_scalar(h_row, z, 0.0, None, ALU.max).then_inc(e_posted[l], 1)
                    else:
                        xt = x_res[:, bass.ds(t, 1), :].rearrange("p o d -> p (o d)")
                        v.scalar_tensor_tensor(xt, z, 0.0, xt, ALU.max, ALU.add).then_inc(e_posted[l], 1)

                lo, cnt, q0 = walk(v, 0)
                with v.Fori(0, cnt) as r:
                    turn(iota_n[:, 0:P], tile_of(lo, r), q0 + r)
                def rel_unit(n, u):
                    if u < 0:
                        rel_root(1, n, h_row, based)
                    else:
                        rel_columns(1, n, u, based)

                def node_tile(t, early=None, between=None, after=None, late=None, end=None):
                    lo, cnt, q0 = walk(v, t)
                    nodes = iota_n[:, bass.ds(t * P, P)]
                    turn(nodes, lo, q0)
                    if early is not None:
                        early()
                    variance(t - 1)
                    turn(nodes, tile_of(lo, 1), q0 + 1, between)
                    if after is not None:
                        after()
                    with v.Fori(2, cnt) as r:
                        turn(nodes, tile_of(lo, r), q0 + r)
                    if late is not None:
                        late()
                    norm(t - 1)
                    if end is not None:
                        end()

                if l == 0:
                    def rel_units(n, first, last):
                        for u in range(first, last):
                            rel_unit(n, u)

                    def rel_tile(t, early):
                        n = t - 2
                        node_tile(t, early, lambda j: rel_unit(n, {0: -1, 2: 0, 3: 1, 5: 2}[j]) if j in (0, 2, 3, 5)
                                  else None, lambda: rel_unit(n, 3), lambda: rel_units(n, 4, 6))

                    node_tile(1)
                    rel_tile(2, None)
                    with v.Fori(3, NT) as t:
                        steps.enter(t - 3, 8)
                        rel_tile(t, lambda: rel_units(t - 3, 6, 8))
                    steps.leave(NT - 3)
                    rel_units(NT - 3, 6, 8)
                    variance(NT - 1)
                    rel_units(NT - 2, -1, 8)
                    norm(NT - 1)
                    rel_units(NT - 1, -1, 8)
                    v.wait_ge(r_based[1], NT + 1)
                    v.wait_ge(e_posted[0], NT)
                    return

                def x_stats(g):
                    hold(v, e_posted[1], (g + 1) * G)
                    norm_stats(g)

                def x_rows(g):
                    norm_rows(g, g + (3 * NG + 1), xn_x)

                def x_choose(g):
                    hold(v, x_logits, g + 1)
                    steps.step(v.tensor_tensor(lg[:, :, :], bank[7][:, 0:G * X1].rearrange("p (j c) -> p j c", c=X1),
                                               rb.unsqueeze(1).broadcast_to([P, G, X1]), ALU.add))
                    for j in range(G):
                        last = v.max(top[:, j, :], lg[:, j, :])
                    steps.step(last)
                    for j in range(G):
                        last = v.max_index(topi[:, j, :], top[:, j, :], lg[:, j, :])
                    steps.step(last)
                    steps.step(v.tensor_copy(idxf[:, :, 0:1], topi[:, :, 0:1]))
                    v.tensor_tensor(oh[:, :, :], iota_x[:, :].unsqueeze(1).broadcast_to([P, G, X1]),
                                    idxf[:, :, 0:1].broadcast_to([P, G, X1]), ALU.is_equal).then_inc(x_oh, 1)

                def x_hidden(g, first, units):
                    for u in range(first, first + units):
                        m, nb = u // 2, u % 2
                        hold(v, x_h, g * (2 * M1) + (u + 1))
                        v.tensor_scalar(hmT[m][:, nb * HB:(nb + 1) * HB], bank[4 + u % 3][:, 0:HB], xb1[:, m:m + 1],
                                        0.0, ALU.add, ALU.max).then_inc(x_hT, 1)

                def x_out(g, pair):
                    if pair == 0:
                        hold(v, x_stored, (g + 1) * 16)
                    hold(v, x_o, g * 3 + (pair + 1))
                    n = min(2, G - 2 * pair)
                    v.scalar_tensor_tensor(
                        outs[:, 2 * pair:2 * pair + n, :].rearrange("p t d -> p (t d)"),
                        bank[3 + 4 * (pair % 2)][:, 0:n * D], 0.0,
                        x_res[:, bass.ds(g * G + 2 * pair, n), :].rearrange("p t d -> p (t d)"),
                        ALU.max, ALU.add).then_inc(x_oread, 1)

                def x_outs_end(g):
                    x_out(g, 1)
                    x_out(g, 2)

                def group(g, outs):
                    def first_end():
                        x_stats(g - 1)
                        x_rows(g - 1)

                    node_tile(g * G + 1, late=(lambda: x_outs_end(g - 2)) if outs else None, end=first_end)
                    node_tile(g * G + 2, after=lambda: x_choose(g - 1))
                    node_tile(g * G + 3, between=lambda j: x_hidden(g - 1, j - 1, 1) if j >= 1 else None,
                              after=lambda: x_hidden(g - 1, 5, 7), late=lambda: x_hidden(g - 1, 12, 2))
                    node_tile(g * G + 4, lambda: x_hidden(g - 1, 14, 3), lambda j: x_hidden(g - 1, 17 + j, 1),
                              lambda: x_hidden(g - 1, 23, 4), lambda: x_hidden(g - 1, 27, 2))

                with v.Fori(1, G + 1) as t:
                    steps.enter(t - 1, 7)
                    node_tile(t)
                steps.leave(G)
                v.wait_ge(ffn1_loaded, 7 * 16)
                group(1, False)
                with v.Fori(2, NG) as g:
                    steps.enter(g - 2, 7 * G + 7)
                    node_tile(g * G, lambda: x_hidden(g - 2, 29, 3), late=lambda: x_out(g - 2, 0))
                    group(g, True)
                steps.leave(NG - 2)
                x_hidden(NG - 2, 29, 3)
                variance(NT - 1)
                norm(NT - 1)
                x_stats(NG - 1)
                x_rows(NG - 1)
                x_out(NG - 2, 0)
                x_outs_end(NG - 2)
                x_choose(NG - 1)
                x_hidden(NG - 1, 0, 2 * M1)
                x_out(NG - 1, 0)
                x_outs_end(NG - 1)

            v.wait_ge(rows_loaded, 9 * 16)
            rel_groups()
            for l in range(2):
                edge_sums(l)


def kernel(**inputs):
    import ml_dtypes
    import numpy as np
    import concourse.bacc as bacc
    from concourse.bass_utils import run_bass_kernel_spmd as run

    v = {k: np.asarray(x) for k, x in inputs.items()}

    def tiles(x, mode, **kw):
        pad = [(0, ETP * P - E)] + [(0, 0)] * (x.ndim - 1)
        x = np.pad(x, pad, mode=mode, **kw).reshape((ETP, P) + x.shape[1:])
        return np.ascontiguousarray(np.moveaxis(x, 0, 1))

    def cols(x):
        x = x.reshape(x.shape[:-1] + (x.shape[-1] // P, P))
        return np.ascontiguousarray(np.moveaxis(x, -1, 0))

    far = np.full((X1, X1, H1), FAR, np.float32)
    far[np.arange(X1), np.arange(X1)] = 0
    dst_rows = np.pad(v["dst"], (0, 4 * P * P - E), constant_values=NOWHERE)
    arrays = {
        "x": np.pad(v["x"], ((0, NT * P - N), (0, 0))),
        "dst_rows": np.ascontiguousarray(dst_rows.reshape(4, P, P).transpose(1, 0, 2)),
        "dst_t": tiles(v["dst"], "constant", constant_values=NOWHERE),
        "src_t": tiles(v["src"], "edge"),
        "et_t": tiles(v["edge_type_16"], "edge"),
        "ea_t": tiles(v["edge_weight"], "constant"),
        "dir_t": tiles(v["edge_attr_2"], "edge"),
        "wf": v["L0_gnn_W_forward"], "wf_T": np.ascontiguousarray(v["L0_gnn_W_forward"].T),
        "wr": v["L0_gnn_W_reverse"], "wr_T": np.ascontiguousarray(v["L0_gnn_W_reverse"].T),
        "attn_T": np.ascontiguousarray(v["L0_gnn_attn_forward"][0].T),
        "ident": np.eye(P, dtype=np.float32),
        "rw1": v["L0_ffn_router_w1"], "rb1": v["L0_ffn_router_b1"],
        "rw2": v["L0_ffn_router_w2"], "rb2": v["L0_ffn_router_b2"],
        "ew1": v["L0_ffn_expert_w1"], "ew2": v["L0_ffn_expert_w2"], "ew3": v["L0_ffn_expert_w3"],
        "eb1T": cols(v["L0_ffn_expert_b1"]), "eb2T": cols(v["L0_ffn_expert_b2"]), "eb3": v["L0_ffn_expert_b3"],
        "xw1": np.ascontiguousarray(v["L1_ffn_W1"].transpose(1, 0, 2).reshape(D, X1 * H1)),
        "xb1T": cols(v["L1_ffn_b1"].reshape(X1 * H1)),
        "xw2": v["L1_ffn_W2"].reshape(X1 * H1, D), "xb2": v["L1_ffn_b2"],
        "rwT": np.ascontiguousarray(v["L1_ffn_router_w"].T), "rb": v["L1_ffn_router_b"],
        "negmask": far.reshape(X1, X1 * H1).astype(ml_dtypes.bfloat16),
    }
    for l in range(2):
        arrays[f"basis{l}"] = v[f"L1_gnn_basis{l + 1}"]
        arrays[f"att{l}"] = v[f"L1_gnn_att{l + 1}"].reshape(R * B)
        arrays[f"root{l}"] = v[f"L1_gnn_root{l + 1}"]
        arrays[f"bias{l}"] = v[f"L1_gnn_bias{l + 1}"]
        arrays[f"ln_g{l}"] = v[f"L1_gnn_ln{l + 1}_g"]
        arrays[f"ln_b{l}"] = v[f"L1_gnn_ln{l + 1}_b"]

    nc = bacc.Bacc("TRN2", target_bir_lowering=False, num_devices=1)
    arrays = {f"in_{k}": np.ascontiguousarray(x) for k, x in arrays.items()}
    aps = {k[3:]: nc.dram_tensor(k, x.shape, mybir.dt.from_np(x.dtype), kind="ExternalInput").ap()
           for k, x in arrays.items()}
    out = nc.dram_tensor("out", (NT * P, D), F32, kind="ExternalOutput").ap()
    build(nc, aps, out)
    r = run(nc, [arrays], core_ids=[0])
    return r.results[0]["out"][:N]
```
